# Optimizing a Trainium2 kernel written in Bass

```python
import numpy as np
import jax
import jax.numpy as jnp

def _softmax(x, axis=-1):
    return jax.nn.softmax(x, axis=axis)

def _gelu(x):
    return jax.nn.gelu(x, approximate=True)

def _silu(x):
    return jax.nn.silu(x)

def _sigmoid(x):
    return jax.nn.sigmoid(x)

def _layernorm(x, axis=-1, eps=1e-05):
    m = jnp.mean(x, axis=axis, keepdims=True)
    v = jnp.var(x, axis=axis, keepdims=True)
    return (x - m) / jnp.sqrt(v + eps)

def _scatter_add(tgt, idx, src, axis=0):
    return tgt.at[idx].add(src)

def _segment_sum(src, seg, n):
    return jax.ops.segment_sum(src, seg, n)
kernel_name = 'mk_flamingo_gated_d4_seqx_r8_965127'

def setup_inputs(seed: int=0):
    np.random.seed(seed)
    _w = jnp.asarray

    def _rec_inputs():
        import jax
        import jax.numpy as jnp
        _rk = jax.random.key(seed)
        x = -0.0002928 + 1 * jax.random.normal(jax.random.fold_in(_rk, 1), (128, 64, 128), jnp.float32)
        _lenS = 64 - jax.random.randint(jax.random.fold_in(_rk, 7), (128,), 0, max(1, 64 // 4) + 1, jnp.int32)
        _lenS2 = 64 - jax.random.randint(jax.random.fold_in(_rk, 8), (128,), 0, max(1, 64 // 4) + 1, jnp.int32)
        _ctx_1024P = jax.random.normal(jax.random.fold_in(_rk, 11), (128, 16, 128), jnp.float32)
        _ctx_1024c = jax.random.dirichlet(jax.random.fold_in(_rk, 511), 0.3 * jnp.ones((16,), jnp.float32), (128, 64))
        _ctx_1024t = jnp.einsum('bsk,bkd->bsd', _ctx_1024c, _ctx_1024P)
        _ctx_1024t = _ctx_1024t * jax.lax.rsqrt(jnp.mean(jnp.square(_ctx_1024t)) + 1e-12) * 0.953939
        ctx_1024 = -1.39393e-06 + 0.999914 * (_ctx_1024t + 0.3 * jax.random.normal(jax.random.fold_in(_rk, 611), (128, 64, 128), jnp.float32))
        _validS = jnp.arange(64)[None, :] < _lenS[:, None]
        _validS2 = jnp.arange(64)[None, :] < _lenS2[:, None]
        _causal = jnp.tril(jnp.ones((64, 64), dtype=bool))
        mask_BxS2_ff1 = jnp.where(jnp.ones((128, 64), dtype=bool), 1.0, 0.0).astype(jnp.float32)
        mask_BxS2_bk0 = jnp.logical_not(jnp.broadcast_to(_validS2[:, :], (128, 64)))
        _g = jax.random.normal(jax.random.fold_in(_rk, 9001), (2, 4), jnp.float32)
        _g = jnp.sign(_g) * jnp.maximum(jnp.abs(_g), 1.0) + (_g == 0) * 1.0
        g_xattn = _g[0]
        g_ffn = _g[1]
        return (x, ctx_1024, mask_BxS2_ff1, mask_BxS2_bk0, g_xattn, g_ffn)
    x, ctx_1024, mask_BxS2_ff1, mask_BxS2_bk0, g_xattn, g_ffn = _rec_inputs()

    def _L0_xattn_setup():
        import jax, jax.numpy as jnp
        import numpy as np
        D_MODEL = 128
        N_HEADS = 16
        N_KV_HEADS = 4
        HEAD_DIM = 64
        key = jax.random.key(seed)
        ks = jax.random.split(key, 6)
        B, Tq, Tkv = (2, 256, 256)
        query = jax.random.normal(ks[0], (B, Tq, D_MODEL), dtype=jnp.float32)
        context = jax.random.normal(ks[1], (B, Tkv, D_MODEL), dtype=jnp.float32)
        s = 1.0 / np.sqrt(D_MODEL)
        Wq = jax.random.normal(ks[2], (N_HEADS * HEAD_DIM, D_MODEL), dtype=jnp.float32) * s
        Wk = jax.random.normal(ks[3], (N_KV_HEADS * HEAD_DIM, D_MODEL), dtype=jnp.float32) * s
        Wv = jax.random.normal(ks[4], (N_KV_HEADS * HEAD_DIM, D_MODEL), dtype=jnp.float32) * s
        Wo = jax.random.normal(ks[5], (D_MODEL, N_HEADS * HEAD_DIM), dtype=jnp.float32) * s
        return {'query': query, 'context': context, 'Wq': Wq, 'Wk': Wk, 'Wv': Wv, 'Wo': Wo}
    _L0_xattn_all = _L0_xattn_setup()
    _L0_xattn_in = {k: v for k, v in _L0_xattn_all.items() if k in ('Wq', 'Wk', 'Wv', 'Wo')}
    del _L0_xattn_all

    def _L0_ffn_setup():
        import jax, jax.numpy as jnp
        import numpy as np
        NUM_HEADS = 16
        TOP_K = 2
        key = jax.random.key(seed)
        ks = jax.random.split(key, 5)
        B, S, D, E = (4, 256, 128, 8)
        scale = 0.02
        return {'x': jax.random.normal(ks[0], (B, S, D), dtype=jnp.float32), 'W_qkv': jax.random.normal(ks[1], (D, 3 * D), dtype=jnp.float32) * scale, 'b_qkv': jnp.zeros((3 * D,), dtype=jnp.float32), 'W_gate': jax.random.normal(ks[2], (D, E), dtype=jnp.float32) * scale, 'b_gate': jnp.zeros((E,), dtype=jnp.float32), 'W_experts': jax.random.normal(ks[3], (E, D, D), dtype=jnp.float32) * scale, 'b_experts': jnp.zeros((E, D), dtype=jnp.float32)}
    _L0_ffn_all = _L0_ffn_setup()
    _L0_ffn_in = {k: v for k, v in _L0_ffn_all.items() if k in ('W_qkv', 'b_qkv', 'W_gate', 'b_gate', 'W_experts', 'b_experts')}
    del _L0_ffn_all

    def _L1_xattn_setup():
        import jax, jax.numpy as jnp
        import numpy as np
        EMBED_DIM = 128
        NUM_HEADS = 16
        HEAD_DIM = EMBED_DIM // NUM_HEADS
        BSZ, TGT, SRC = (4, 256, 256)

        def _split_heads(x, bsz, seqlen):
            return x.reshape(bsz, seqlen, NUM_HEADS, HEAD_DIM).transpose(0, 2, 1, 3)
        key = jax.random.key(seed)
        ks = jax.random.split(key, 8)
        s = EMBED_DIM ** (-0.5)
        return {'query': jax.random.normal(ks[0], (BSZ, TGT, EMBED_DIM), jnp.float32), 'key': jax.random.normal(ks[1], (BSZ, SRC, EMBED_DIM), jnp.float32), 'key_padding_mask': jnp.ones((BSZ, SRC), jnp.float32), 'Wq': jax.random.normal(ks[2], (EMBED_DIM, EMBED_DIM), jnp.float32) * s, 'bq': jnp.zeros((EMBED_DIM,), jnp.float32), 'Wk': jax.random.normal(ks[3], (EMBED_DIM, EMBED_DIM), jnp.float32) * s, 'bk': jnp.zeros((EMBED_DIM,), jnp.float32), 'Wv': jax.random.normal(ks[4], (EMBED_DIM, EMBED_DIM), jnp.float32) * s, 'bv': jnp.zeros((EMBED_DIM,), jnp.float32), 'Wo': jax.random.normal(ks[5], (EMBED_DIM, EMBED_DIM), jnp.float32) * s, 'bo': jnp.zeros((EMBED_DIM,), jnp.float32)}
    _L1_xattn_all = _L1_xattn_setup()
    _L1_xattn_in = {k: v for k, v in _L1_xattn_all.items() if k in ('Wq', 'bq', 'Wk', 'bk', 'Wv', 'bv', 'Wo', 'bo')}
    del _L1_xattn_all

    def _L1_ffn_setup():
        import jax, jax.numpy as jnp
        import numpy as np
        H, I, E_ROUTED, TOP_K = (128, 352, 7, 2)
        B, S = (4, 256)

        def _expert(h, g, u, d):
            return jnp.einsum('...i,hi->...h', jax.nn.silu(h @ g.T) * (h @ u.T), d)
        key = jax.random.key(seed)
        ks = jax.random.split(key, 10)
        sc = 0.02
        return {'x': jax.random.normal(ks[0], (B, S, H), dtype=jnp.float32), 'sg': jax.random.normal(ks[1], (I, H), dtype=jnp.float32) * sc, 'su': jax.random.normal(ks[2], (I, H), dtype=jnp.float32) * sc, 'sd': jax.random.normal(ks[3], (H, I), dtype=jnp.float32) * sc, 'rg': jax.random.normal(ks[4], (E_ROUTED, I, H), dtype=jnp.float32) * sc, 'ru': jax.random.normal(ks[5], (E_ROUTED, I, H), dtype=jnp.float32) * sc, 'rd': jax.random.normal(ks[6], (E_ROUTED, H, I), dtype=jnp.float32) * sc, 'wr': jax.random.normal(ks[7], (E_ROUTED, H), dtype=jnp.float32) * sc, 'rb': jnp.zeros((E_ROUTED,), dtype=jnp.float32)}
    _L1_ffn_all = _L1_ffn_setup()
    _L1_ffn_in = {k: v for k, v in _L1_ffn_all.items() if k in ('sg', 'su', 'sd', 'rg', 'ru', 'rd', 'wr', 'rb')}
    del _L1_ffn_all

    def _L2_xattn_setup():
        import jax, jax.numpy as jnp
        import numpy as np
        NUM_HEADS, NUM_KV, HEAD_DIM, WIDTH = (4, 1, 32, 128)
        MASK_FILL = -2.3819763e+38

        def _apply_rope(x, positions, max_wavelength=10000.0):
            d = x.shape[-1]
            freq_exp = 2.0 / d * jnp.arange(d // 2, dtype=jnp.float32)
            timescale = max_wavelength ** freq_exp
            radians = positions[..., None].astype(jnp.float32) / timescale
            radians = radians[..., None, :]
            sin, cos = (jnp.sin(radians), jnp.cos(radians))
            x1, x2 = jnp.split(x, 2, axis=-1)
            out = jnp.concatenate([x1 * cos - x2 * sin, x2 * cos + x1 * sin], axis=-1)
            return out.astype(x.dtype)

        def _rmsnorm(x, scale):
            var = jnp.mean(jnp.square(x.astype(jnp.float32)), axis=-1, keepdims=True)
            normed = x * jax.lax.rsqrt(var + 1e-06)
            return (normed * (1 + scale)).astype(x.dtype)
        key = jax.random.key(seed)
        ks = jax.random.split(key, 7)
        B, T, S = (8, 64, 256)
        return {'x': jax.random.normal(ks[0], (B, T, WIDTH), jnp.float32), 'mem_seq': jax.random.normal(ks[1], (B, S, WIDTH), jnp.float32), 'mem_mask': jax.random.randint(ks[2], (B, S), 0, 2).astype(bool), 'rms_scale': jax.random.normal(ks[3], (WIDTH,), jnp.float32) * 0.02, 'q_w': jax.random.normal(ks[4], (NUM_HEADS, WIDTH, HEAD_DIM), jnp.float32) / np.sqrt(WIDTH), 'kv_w': jax.random.normal(ks[5], (2, NUM_KV, WIDTH, HEAD_DIM), jnp.float32) / np.sqrt(WIDTH), 'out_w': jax.random.normal(ks[6], (NUM_HEADS, HEAD_DIM, WIDTH), jnp.float32) / np.sqrt(NUM_HEADS * HEAD_DIM)}
    _L2_xattn_all = _L2_xattn_setup()
    _L2_xattn_in = {k: v for k, v in _L2_xattn_all.items() if k in ('rms_scale', 'q_w', 'kv_w', 'out_w')}
    del _L2_xattn_all

    def _L2_ffn_setup():
        import jax, jax.numpy as jnp
        import numpy as np
        B, S, H, FFN, E = (2, 256, 128, 512, 8)
        key = jax.random.key(seed)
        k0, k1, k2, k3 = jax.random.split(key, 4)
        return {'hidden_states': jax.random.normal(k0, (B, S, H), dtype=jnp.float32), 'Wr': jax.random.normal(k1, (H, E), dtype=jnp.float32) * 0.02, 'br': jnp.zeros((E,), dtype=jnp.float32), 'W1': jax.random.normal(k2, (E, H, FFN), dtype=jnp.float32) * 0.02, 'W2': jax.random.normal(k3, (E, FFN, H), dtype=jnp.float32) * 0.02}
    _L2_ffn_all = _L2_ffn_setup()
    _L2_ffn_in = {k: v for k, v in _L2_ffn_all.items() if k in ('Wr', 'br', 'W1', 'W2')}
    del _L2_ffn_all

    def _L3_xattn_setup():
        import jax, jax.numpy as jnp
        import numpy as np
        B, S, D = (1, 512, 128)
        NUM_HEADS, HEAD_DIM = (16, 64)
        WINDOW = 128
        EMBED = NUM_HEADS * HEAD_DIM
        key = jax.random.key(seed)
        ks = jax.random.split(key, 7)
        scale_in = 1.0 / np.sqrt(D)
        scale_e = 1.0 / np.sqrt(EMBED)
        return {'query': jax.random.normal(ks[0], (B, S, D), dtype=jnp.float32), 'key': jax.random.normal(ks[1], (B, S, D), dtype=jnp.float32), 'value': jax.random.normal(ks[2], (B, S, D), dtype=jnp.float32), 'Wq': jax.random.normal(ks[3], (D, EMBED), dtype=jnp.float32) * scale_in, 'Wk': jax.random.normal(ks[4], (D, EMBED), dtype=jnp.float32) * scale_in, 'Wv': jax.random.normal(ks[5], (D, EMBED), dtype=jnp.float32) * scale_in, 'Wo': jax.random.normal(ks[6], (EMBED, D), dtype=jnp.float32) * scale_e}
    _L3_xattn_all = _L3_xattn_setup()
    _L3_xattn_in = {k: v for k, v in _L3_xattn_all.items() if k in ('Wq', 'Wk', 'Wv', 'Wo')}
    del _L3_xattn_all

    def _L3_ffn_setup():
        import jax, jax.numpy as jnp
        import numpy as np
        DIM = 128

        def _reference_tuple_inner(x, W_r, W_k, W_v, mu_r, mu_k):
            B, T, C = x.shape
            x_prev = jnp.concatenate([jnp.zeros((B, 1, C), x.dtype), x[:, :-1, :]], axis=1)
            xr = mu_r * x + (1.0 - mu_r) * x_prev
            xk = mu_k * x + (1.0 - mu_k) * x_prev
            r = jax.nn.sigmoid(jnp.einsum('btc,dc->btd', xr, W_r))
            k = jnp.einsum('btc,dc->btd', xk, W_k)
            k_act = jnp.square(jax.nn.relu(k))
            out = r * jnp.einsum('btc,dc->btd', k_act, W_v)
            new_state = x[:, -1, :]
            return (out, new_state)
        key = jax.random.key(seed)
        ks = jax.random.split(key, 6)
        B, T, C = (8, 256, DIM)
        x = jax.random.normal(ks[0], (B, T, C), dtype=jnp.float32)
        s = 1.0 / np.sqrt(C)
        W_r = jax.random.uniform(ks[1], (C, C), jnp.float32, -s, s)
        W_k = jax.random.uniform(ks[2], (C, C), jnp.float32, -s, s)
        W_v = jax.random.uniform(ks[3], (C, C), jnp.float32, -s, s)
        mu_r = jax.random.uniform(ks[4], (C,), jnp.float32)
        mu_k = jax.random.uniform(ks[5], (C,), jnp.float32)
        return {'x': x, 'W_r': W_r, 'W_k': W_k, 'W_v': W_v, 'mu_r': mu_r, 'mu_k': mu_k}
    _L3_ffn_all = _L3_ffn_setup()
    _L3_ffn_in = {k: v for k, v in _L3_ffn_all.items() if k in ('W_r', 'W_k', 'W_v', 'mu_r', 'mu_k')}
    del _L3_ffn_all
    return {'x': x, 'ctx_1024': ctx_1024, 'mask_BxS2_ff1': mask_BxS2_ff1, 'mask_BxS2_bk0': mask_BxS2_bk0, 'g_xattn': g_xattn, 'g_ffn': g_ffn, 'L0_xattn_Wq': _L0_xattn_in['Wq'], 'L0_xattn_Wk': _L0_xattn_in['Wk'], 'L0_xattn_Wv': _L0_xattn_in['Wv'], 'L0_xattn_Wo': _L0_xattn_in['Wo'], 'L0_ffn_W_qkv': _L0_ffn_in['W_qkv'], 'L0_ffn_b_qkv': _L0_ffn_in['b_qkv'], 'L0_ffn_W_gate': _L0_ffn_in['W_gate'], 'L0_ffn_b_gate': _L0_ffn_in['b_gate'], 'L0_ffn_W_experts': _L0_ffn_in['W_experts'], 'L0_ffn_b_experts': _L0_ffn_in['b_experts'], 'L1_xattn_Wq': _L1_xattn_in['Wq'], 'L1_xattn_bq': _L1_xattn_in['bq'], 'L1_xattn_Wk': _L1_xattn_in['Wk'], 'L1_xattn_bk': _L1_xattn_in['bk'], 'L1_xattn_Wv': _L1_xattn_in['Wv'], 'L1_xattn_bv': _L1_xattn_in['bv'], 'L1_xattn_Wo': _L1_xattn_in['Wo'], 'L1_xattn_bo': _L1_xattn_in['bo'], 'L1_ffn_sg': _L1_ffn_in['sg'], 'L1_ffn_su': _L1_ffn_in['su'], 'L1_ffn_sd': _L1_ffn_in['sd'], 'L1_ffn_rg': _L1_ffn_in['rg'], 'L1_ffn_ru': _L1_ffn_in['ru'], 'L1_ffn_rd': _L1_ffn_in['rd'], 'L1_ffn_wr': _L1_ffn_in['wr'], 'L1_ffn_rb': _L1_ffn_in['rb'], 'L2_xattn_rms_scale': _L2_xattn_in['rms_scale'], 'L2_xattn_q_w': _L2_xattn_in['q_w'], 'L2_xattn_kv_w': _L2_xattn_in['kv_w'], 'L2_xattn_out_w': _L2_xattn_in['out_w'], 'L2_ffn_Wr': _L2_ffn_in['Wr'], 'L2_ffn_br': _L2_ffn_in['br'], 'L2_ffn_W1': _L2_ffn_in['W1'], 'L2_ffn_W2': _L2_ffn_in['W2'], 'L3_xattn_Wq': _L3_xattn_in['Wq'], 'L3_xattn_Wk': _L3_xattn_in['Wk'], 'L3_xattn_Wv': _L3_xattn_in['Wv'], 'L3_xattn_Wo': _L3_xattn_in['Wo'], 'L3_ffn_W_r': _L3_ffn_in['W_r'], 'L3_ffn_W_k': _L3_ffn_in['W_k'], 'L3_ffn_W_v': _L3_ffn_in['W_v'], 'L3_ffn_mu_r': _L3_ffn_in['mu_r'], 'L3_ffn_mu_k': _L3_ffn_in['mu_k']}

def reference(x, ctx_1024, mask_BxS2_ff1, mask_BxS2_bk0, g_xattn, g_ffn, L0_xattn_Wq, L0_xattn_Wk, L0_xattn_Wv, L0_xattn_Wo, L0_ffn_W_qkv, L0_ffn_b_qkv, L0_ffn_W_gate, L0_ffn_b_gate, L0_ffn_W_experts, L0_ffn_b_experts, L1_xattn_Wq, L1_xattn_bq, L1_xattn_Wk, L1_xattn_bk, L1_xattn_Wv, L1_xattn_bv, L1_xattn_Wo, L1_xattn_bo, L1_ffn_sg, L1_ffn_su, L1_ffn_sd, L1_ffn_rg, L1_ffn_ru, L1_ffn_rd, L1_ffn_wr, L1_ffn_rb, L2_xattn_rms_scale, L2_xattn_q_w, L2_xattn_kv_w, L2_xattn_out_w, L2_ffn_Wr, L2_ffn_br, L2_ffn_W1, L2_ffn_W2, L3_xattn_Wq, L3_xattn_Wk, L3_xattn_Wv, L3_xattn_Wo, L3_ffn_W_r, L3_ffn_W_k, L3_ffn_W_v, L3_ffn_mu_r, L3_ffn_mu_k):
    import jax
    import jax.numpy as jnp

    def _L0_xattn_ref(query, context, Wq, Wk, Wv, Wo):
        import jax, jax.numpy as jnp
        import numpy as np
        D_MODEL = 128
        N_HEADS = 16
        N_KV_HEADS = 4
        HEAD_DIM = 64
        B, Tq, _ = query.shape
        Tkv = context.shape[1]
        q = (query @ Wq.T).reshape(B, Tq, N_HEADS, HEAD_DIM).transpose(0, 2, 1, 3)
        k = (context @ Wk.T).reshape(B, Tkv, N_KV_HEADS, HEAD_DIM).transpose(0, 2, 1, 3)
        v = (context @ Wv.T).reshape(B, Tkv, N_KV_HEADS, HEAD_DIM).transpose(0, 2, 1, 3)
        groups = N_HEADS // N_KV_HEADS
        k = jnp.repeat(k, groups, axis=1)
        v = jnp.repeat(v, groups, axis=1)
        scale = jnp.sqrt(jnp.float32(HEAD_DIM))
        scores = jnp.einsum('bhqd,bhkd->bhqk', q, k) / scale
        attn = jax.nn.softmax(scores, axis=-1)
        out = jnp.einsum('bhqk,bhkd->bhqd', attn, v)
        out = out.transpose(0, 2, 1, 3).reshape(B, Tq, N_HEADS * HEAD_DIM)
        return out @ Wo.T

    def _L0_ffn_ref(x, W_qkv, b_qkv, W_gate, b_gate, W_experts, b_experts):
        import jax, jax.numpy as jnp
        import numpy as np
        NUM_HEADS = 16
        TOP_K = 2
        B, S, D = x.shape
        H = NUM_HEADS
        hd = D // H
        E = W_gate.shape[-1]
        qkv = (x @ W_qkv + b_qkv).reshape(B, S, 3, H, hd)
        q, k, v = (qkv[:, :, 0], qkv[:, :, 1], qkv[:, :, 2])
        attn = jnp.einsum('bqhd,bkhd->bhqk', q, k) / jnp.sqrt(jnp.asarray(hd, x.dtype))
        attn = jax.nn.softmax(attn, axis=-1)
        attn_out = jnp.einsum('bhqk,bkhd->bqhd', attn, v).reshape(B, S, D)
        gate = jax.nn.softmax(x @ W_gate + b_gate, axis=-1)
        top_g, top_i = jax.lax.top_k(gate, TOP_K)
        combine = jnp.sum(jax.nn.one_hot(top_i, E, dtype=x.dtype) * top_g[..., None], axis=2)
        expert_out = jnp.einsum('bsd,edf->bsef', x, W_experts) + b_experts
        moe_out = jnp.einsum('bsef,bse->bsf', expert_out, combine)
        return attn_out + moe_out

    def _L1_xattn_ref(query, key, key_padding_mask, Wq, bq, Wk, bk, Wv, bv, Wo, bo):
        import jax, jax.numpy as jnp
        import numpy as np
        EMBED_DIM = 128
        NUM_HEADS = 16
        HEAD_DIM = EMBED_DIM // NUM_HEADS
        BSZ, TGT, SRC = (4, 256, 256)

        def _split_heads(x, bsz, seqlen):
            return x.reshape(bsz, seqlen, NUM_HEADS, HEAD_DIM).transpose(0, 2, 1, 3)
        bsz, src_len, embed_dim = key.shape
        tgt_len = query.shape[1]
        scaling = HEAD_DIM ** (-0.5)
        q = (query @ Wq.T + bq) * scaling
        k = key @ Wk.T + bk
        v = key @ Wv.T + bv
        qh = _split_heads(q, bsz, tgt_len)
        kh = _split_heads(k, bsz, src_len)
        vh = _split_heads(v, bsz, src_len)
        scores = jnp.einsum('bhtd,bhsd->bhts', qh, kh)
        inv = 1.0 - key_padding_mask.astype(scores.dtype)
        neg = jnp.finfo(scores.dtype).min
        add_mask = jnp.where(inv.astype(bool), neg, inv)
        scores = scores + add_mask[:, None, None, :]
        probs = jax.nn.softmax(scores, axis=-1)
        out = jnp.einsum('bhts,bhsd->bhtd', probs, vh)
        out = out.transpose(0, 2, 1, 3).reshape(bsz, tgt_len, embed_dim)
        return out @ Wo.T + bo

    def _L1_ffn_ref(x, sg, su, sd, rg, ru, rd, wr, rb):
        import jax, jax.numpy as jnp
        import numpy as np
        H, I, E_ROUTED, TOP_K = (128, 352, 7, 2)
        B, S = (4, 256)

        def _expert(h, g, u, d):
            return jnp.einsum('...i,hi->...h', jax.nn.silu(h @ g.T) * (h @ u.T), d)
        shared_out = _expert(x, sg, su, sd)
        logits = x @ wr.T + rb
        probs = jax.nn.softmax(logits, axis=-1)
        scores, idx = jax.lax.top_k(probs, TOP_K)
        scores = scores / scores.sum(axis=-1, keepdims=True)
        w = jnp.sum(scores[..., None] * jax.nn.one_hot(idx, E_ROUTED, dtype=x.dtype), axis=-2)
        out = shared_out
        for e in range(E_ROUTED):
            out = out + w[..., e:e + 1] * _expert(x, rg[e], ru[e], rd[e])
        return out

    def _L2_xattn_ref(x, mem_seq, mem_mask, rms_scale, q_w, kv_w, out_w):
        import jax, jax.numpy as jnp
        import numpy as np
        NUM_HEADS, NUM_KV, HEAD_DIM, WIDTH = (4, 1, 32, 128)
        MASK_FILL = -2.3819763e+38

        def _apply_rope(x, positions, max_wavelength=10000.0):
            d = x.shape[-1]
            freq_exp = 2.0 / d * jnp.arange(d // 2, dtype=jnp.float32)
            timescale = max_wavelength ** freq_exp
            radians = positions[..., None].astype(jnp.float32) / timescale
            radians = radians[..., None, :]
            sin, cos = (jnp.sin(radians), jnp.cos(radians))
            x1, x2 = jnp.split(x, 2, axis=-1)
            out = jnp.concatenate([x1 * cos - x2 * sin, x2 * cos + x1 * sin], axis=-1)
            return out.astype(x.dtype)

        def _rmsnorm(x, scale):
            var = jnp.mean(jnp.square(x.astype(jnp.float32)), axis=-1, keepdims=True)
            normed = x * jax.lax.rsqrt(var + 1e-06)
            return (normed * (1 + scale)).astype(x.dtype)
        B, S, _ = mem_seq.shape
        T = x.shape[1]
        G = NUM_HEADS // NUM_KV
        xn = _rmsnorm(x, rms_scale)
        mn = _rmsnorm(mem_seq, rms_scale)
        q = jnp.einsum('BTD,NDH->BTNH', xn, q_w)
        kv = jnp.einsum('BSD,cKDH->cBSKH', mn, kv_w)
        k, v = (kv[0], kv[1])
        q_pos = jnp.broadcast_to(jnp.arange(S, T + S), (B, T))
        k_pos = jnp.broadcast_to(jnp.arange(S), (B, S))
        q = _apply_rope(q, q_pos) * HEAD_DIM ** (-0.5)
        k = _apply_rope(k, k_pos)
        q = q.reshape(B, T, NUM_KV, G, HEAD_DIM)
        logits = jnp.einsum('BTKGH,BSKH->BKGTS', q, k, preferred_element_type=jnp.float32)
        masked = jnp.where(mem_mask[:, None, None, None, :], logits, MASK_FILL)
        probs = jax.nn.softmax(masked, axis=-1).astype(x.dtype)
        enc = jnp.einsum('BKGTS,BSKH->BTKGH', probs, v).reshape(B, T, NUM_HEADS, HEAD_DIM)
        return jnp.einsum('BTNH,NHD->BTD', enc, out_w)

    def _L2_ffn_ref(hidden_states, Wr, br, W1, W2):
        import jax, jax.numpy as jnp
        import numpy as np
        B, S, H, FFN, E = (2, 256, 128, 512, 8)
        b, s, h = hidden_states.shape
        x = hidden_states.reshape(-1, h)
        route = jax.nn.sigmoid(x @ Wr + br)
        max_prob = jnp.max(route, axis=1, keepdims=True)
        max_ind = jnp.argmax(route, axis=1)
        out = jnp.zeros_like(x)
        n_experts = Wr.shape[1]
        for e in range(n_experts):
            mask = (max_ind == e)[:, None].astype(x.dtype)
            y = jax.nn.gelu(x @ W1[e], approximate=False) @ W2[e]
            out = out + mask * y
        out = out * max_prob
        return out.reshape(b, s, h)

    def _L3_xattn_ref(query, key, value, Wq, Wk, Wv, Wo):
        import jax, jax.numpy as jnp
        import numpy as np
        B, S, D = (1, 512, 128)
        NUM_HEADS, HEAD_DIM = (16, 64)
        WINDOW = 128
        EMBED = NUM_HEADS * HEAD_DIM
        Bq, Sq, _ = query.shape
        q = (query @ Wq).reshape(Bq, Sq, NUM_HEADS, HEAD_DIM).transpose(0, 2, 1, 3)
        k = (key @ Wk).reshape(Bq, Sq, NUM_HEADS, HEAD_DIM).transpose(0, 2, 1, 3)
        v = (value @ Wv).reshape(Bq, Sq, NUM_HEADS, HEAD_DIM).transpose(0, 2, 1, 3)
        idx = jnp.arange(Sq)
        local_mask = jnp.abs(idx[:, None] - idx[None, :]) > WINDOW
        scores = jnp.einsum('bhqd,bhkd->bhqk', q, k) / jnp.sqrt(jnp.float32(HEAD_DIM))
        scores = jnp.where(local_mask, -jnp.inf, scores)
        attn = jax.nn.softmax(scores, axis=-1)
        out = jnp.einsum('bhqk,bhkd->bhqd', attn, v)
        out = out.transpose(0, 2, 1, 3).reshape(Bq, Sq, EMBED)
        return out @ Wo

    def _L3_ffn_ref(x, W_r, W_k, W_v, mu_r, mu_k):
        import jax, jax.numpy as jnp
        import numpy as np
        DIM = 128

        def _reference_tuple_inner(x, W_r, W_k, W_v, mu_r, mu_k):
            B, T, C = x.shape
            x_prev = jnp.concatenate([jnp.zeros((B, 1, C), x.dtype), x[:, :-1, :]], axis=1)
            xr = mu_r * x + (1.0 - mu_r) * x_prev
            xk = mu_k * x + (1.0 - mu_k) * x_prev
            r = jax.nn.sigmoid(jnp.einsum('btc,dc->btd', xr, W_r))
            k = jnp.einsum('btc,dc->btd', xk, W_k)
            k_act = jnp.square(jax.nn.relu(k))
            out = r * jnp.einsum('btc,dc->btd', k_act, W_v)
            new_state = x[:, -1, :]
            return (out, new_state)
        return _reference_tuple_inner(x, W_r, W_k, W_v, mu_r, mu_k)[0]
    x = x + jnp.tanh(g_xattn[0]) * _L0_xattn_ref(_layernorm(x, axis=-1), ctx_1024, L0_xattn_Wq, L0_xattn_Wk, L0_xattn_Wv, L0_xattn_Wo)
    x = x + jnp.tanh(g_ffn[0]) * _L0_ffn_ref(_layernorm(x, axis=-1), L0_ffn_W_qkv, L0_ffn_b_qkv, L0_ffn_W_gate, L0_ffn_b_gate, L0_ffn_W_experts, L0_ffn_b_experts)
    x = x + jnp.tanh(g_xattn[1]) * _L1_xattn_ref(_layernorm(x, axis=-1), ctx_1024, mask_BxS2_ff1, L1_xattn_Wq, L1_xattn_bq, L1_xattn_Wk, L1_xattn_bk, L1_xattn_Wv, L1_xattn_bv, L1_xattn_Wo, L1_xattn_bo)
    x = x + jnp.tanh(g_ffn[1]) * _L1_ffn_ref(_layernorm(x, axis=-1), L1_ffn_sg, L1_ffn_su, L1_ffn_sd, L1_ffn_rg, L1_ffn_ru, L1_ffn_rd, L1_ffn_wr, L1_ffn_rb)
    x = x + jnp.tanh(g_xattn[2]) * _L2_xattn_ref(_layernorm(x, axis=-1), ctx_1024, mask_BxS2_bk0, L2_xattn_rms_scale, L2_xattn_q_w, L2_xattn_kv_w, L2_xattn_out_w)
    x = x + jnp.tanh(g_ffn[2]) * _L2_ffn_ref(_layernorm(x, axis=-1), L2_ffn_Wr, L2_ffn_br, L2_ffn_W1, L2_ffn_W2)
    x = x + jnp.tanh(g_xattn[3]) * _L3_xattn_ref(_layernorm(x, axis=-1), ctx_1024, ctx_1024, L3_xattn_Wq, L3_xattn_Wk, L3_xattn_Wv, L3_xattn_Wo)
    x = x + jnp.tanh(g_ffn[3]) * _L3_ffn_ref(_layernorm(x, axis=-1), L3_ffn_W_r, L3_ffn_W_k, L3_ffn_W_v, L3_ffn_mu_r, L3_ffn_mu_k)
    return x

_drawn_inputs = setup_inputs


def setup_inputs(seed=0):
    import zlib

    import numpy as np

    out = dict(_drawn_inputs(seed))
    spreads = {'L0_ffn_b_qkv': (0.0, 0.1),
     'L0_ffn_b_gate': (0.0, 0.68),
     'L0_ffn_b_experts': (0.0, 0.8),
     'L1_xattn_bq': (0.0, 0.587),
     'L1_xattn_bk': (0.0, 2.0),
     'L1_xattn_bv': (0.0, 0.1),
     'L1_xattn_bo': (0.0, 0.1),
     'L1_ffn_rb': (0.0, 0.8),
     'L2_ffn_br': (0.0, 0.8)}
    factors = {'g_ffn': 8.0,
     'L0_ffn_W_gate': 2.678,
     'L1_ffn_sg': 8.0,
     'L1_ffn_su': 8.0,
     'L1_ffn_sd': 8.0,
     'L1_ffn_rg': 8.0,
     'L1_ffn_ru': 8.0,
     'L1_ffn_rd': 8.0,
     'L1_ffn_wr': 8.0,
     'L2_xattn_rms_scale': 27.124,
     'L2_ffn_Wr': 4.623,
     'L2_ffn_W1': 4.296,
     'L2_ffn_W2': 4.24,
     'L3_ffn_W_r': 4.598,
     'L3_ffn_mu_r': 8.0,
     'L3_ffn_mu_k': 3.228,
     'L3_xattn_Wq': 2.739,
     'L3_xattn_Wk': 2.72}
    for name, (base, spread) in spreads.items():
        noise = np.random.default_rng([zlib.crc32(name.encode()), seed]).standard_normal(out[name].shape)
        drawn = base * np.exp(spread * noise) if base else spread * noise
        out[name] = jnp.asarray(drawn.astype(out[name].dtype))
    for name, factor in factors.items():
        out[name] = (out[name] * factor).astype(out[name].dtype)
    return out
```

```python
from contextlib import ExitStack

import concourse.bass as bass
from concourse import mybir

ALU = mybir.AluOpType
ACT = mybir.ActivationFunctionType
F32 = mybir.dt.float32
U8 = mybir.dt.uint8
AX_X = mybir.AxisListType.X

P = 128
B, S, D = 128, 64, 128
NT = B * S // P
GT = 256
TPG = GT // P
BPG = GT // S
NG = B * S // GT
PAIRS = NG // 2
LN_EPS = 1e-5
RMS_EPS = 1e-6
F32_MIN = -3.4028234663852886e38
MASK_FILL = -2.3819763e38
I_FF, E_FF1 = 352, 7
FFN2, E_FF2 = 512, 8
E_FF0 = 8
ROPE_D = 32

CREDIT = 64

SMALL = [
    ("l0x_wq", 1024), ("l0x_wk", 256), ("l0x_wv", 256), ("l0x_wo", 1024),
    ("l0f_wq", 128), ("l0f_wk", 128), ("l0f_wv", 128), ("l0f_bq", 1), ("l0f_bk", 1), ("l0f_bv", 64),
    ("l0f_wg", 8), ("l0f_bg", 8), ("l0f_we", 1024), ("l0f_be", 128),
    ("l1x_wq", 128), ("l1x_wk", 128), ("l1x_wv", 128), ("l1x_bq", 1), ("l1x_bk", 1), ("l1x_bv", 64),
    ("l1x_wo", 128), ("l1x_bo", 128),
    ("l1f_wg", 7), ("l1f_bg", 7), ("l1f_shared", 2 * 352 + 3 * 128),
    ("l2x_scale", 1), ("l2x_wq", 256), ("l2x_wk", 256), ("l2x_wv", 32), ("l2x_wo", 128),
    ("l2f_wg", 8), ("l2f_bg", 8),
    ("l3x_wq", 1024), ("l3x_wk", 1024), ("l3x_wv", 1024), ("l3x_wo", 1024),
    ("l3f_wr", 128), ("l3f_wk", 128), ("l3f_wv", 128), ("l3f_mur", 1), ("l3f_muk", 1),
    ("gates", 8), ("ident", 128), ("earlier", 64), ("rope", 256),
]
SMALL_AT, _n = {}, 0
for _name, _w in SMALL:
    SMALL_AT[_name] = (_n, _n + _w)
    _n += _w
SMALL_W = _n
EXPERT1 = 2 * I_FF + 3 * D
EXPERT2 = FFN2 + 4 * D
HID1 = [(0, 128), (128, 128), (256, 96)]


class Layer:

    def __init__(self, n, name, front, order, uses, body_banks, heads=0, scale=1.0, cross=False,
                 experts=0, top=0):
        self.n, self.name, self.front, self.order, self.uses = n, name, front, order, uses
        self.body_banks = body_banks
        self.heads, self.scale, self.cross = heads, scale, cross
        self.experts, self.top = experts, top
        self.first_use = {}
        u = 0
        for item in order:
            if item in front:
                continue
            self.first_use[item] = u
            u += uses.get(item[0], 0)
        self.body_uses = u


def interleave(body, front):
    out, done = [], 0
    for i, item in enumerate(body):
        out.append(item)
        upto = len(front) * (i + 1) // len(body)
        out += front[done:upto]
        done = upto
    return out


def attention_layer(n, name, front, stages, uses, heads, scale, cross, experts=0, top=0):
    body = [("S", 0), ("S", 1), ("T", 0), ("T", 1)] + [(s, t) for s in stages for t in range(TPG)]
    return Layer(n, name, front, interleave(body, front), uses, (6, 7), heads, scale, cross, experts, top)


def make_layers():
    q4 = [("Q", j) for j in range(4)]
    k4 = [("K", j) for j in range(4)]
    v4 = [("V", j) for j in range(4)]
    l0x = attention_layer(0, "l0x", [("F", 0)] + q4 + [("K", 0), ("V", 0)], ["A", "W"],
                          {"T": 2, "A": 2, "W": 1}, 16, scale=64 ** -0.5, cross=True)
    l0f = attention_layer(1, "l0f", [("F", 0), ("QK", 0), ("V", 0), ("G", 0), ("C", 0)],
                          ["A", "E", "Z"], {"T": 2, "A": 1, "E": 2, "Z": 1}, 16,
                          scale=8 ** -0.5, cross=False, experts=E_FF0, top=2)
    l1x = attention_layer(2, "l1x", [("F", 0), ("QK", 0), ("V", 0)], ["A", "X", "W"],
                          {"T": 2, "A": 1, "X": 1, "W": 1}, 16, scale=8 ** -0.5, cross=True)
    ff1 = [("U", e, c) for e in range(8) for c in range(3)]
    order = []
    for e in range(8):
        order += [("U", e, 0)]
        if e:
            order.append(("D", e - 1))
        order += [("U", e, 1), ("U", e, 2)]
    order.append(("D", 7))
    l1f = Layer(3, "l1f", [("F", 0), ("G", 0)], interleave(order, [("F", 0), ("G", 0)]),
                {"U": 1, "D": 1}, (0, 1, 2, 3), experts=E_FF1, top=2, cross=False)
    l2x = attention_layer(4, "l2x", [("F", 0), ("Q", 0), ("K", 0), ("V", 0)], ["A", "X", "W"],
                          {"T": 1, "A": 1, "X": 1, "W": 1}, 4, scale=32 ** -0.5, cross=True)
    order = []
    for e in range(8):
        order += [("U", e, 0)]
        if e:
            order.append(("D", e - 1))
        order += [("U", e, 1)]
    order.append(("D", 7))
    l2f = Layer(5, "l2f", [("F", 0), ("G", 0)], interleave(order, [("F", 0), ("G", 0)]),
                {"U": 1, "D": 1}, (0, 1, 2, 3), experts=E_FF2, top=1, cross=False)
    l3x = attention_layer(6, "l3x", [("F", 0)] + q4 + k4 + v4, ["A", "W"],
                          {"T": 2, "A": 2, "W": 1}, 16, scale=64 ** -0.5, cross=True)
    l3f = Layer(7, "l3f", [("F", 0)], [("K", 0), ("F", 0), ("R", 0), ("V", 0)],
                {"K": 1, "R": 1, "V": 1}, (0, 1, 2), cross=False)
    return [l0x, l0f, l1x, l1f, l2x, l2f, l3x, l3f]


class Group:

    def __init__(self, layer, pair, par):
        self.layer, self.pair, self.par = layer, pair, par

    def next(self):
        return Group(self.layer, self.pair, 1) if self.par == 0 else Group(self.layer, self.pair + 1, 0)

    def back(self, n):
        k = self.par - n
        return Group(self.layer, self.pair + k // 2, k % 2)

    def tile(self, t):
        return self.pair * (2 * TPG) + (self.par * TPG + t)


class Step:

    def __init__(self, sem, layers, per):
        self.credit = max(CREDIT, 4 * max(per.values()))
        self.sem, self.per, self.base, n = sem, per, {}, self.credit
        for layer in layers:
            self.base[layer.n] = n
            n += per.get(layer.name, 0) * NG
        self.base[len(layers)] = n

    def after(self, g, k):
        per = self.per[g.layer.name]
        return g.pair * (2 * per) + (self.base[g.layer.n] + g.par * per + k + 1)


class DmaStep:

    def __init__(self, sems, layers, per):
        self.credit = max(CREDIT, 2 * max(per.values()))
        self.sems, self.per, self.base, n = sems, per, {}, self.credit
        for layer in layers:
            self.base[layer.n] = n
            n += per.get(layer.name, 0) * PAIRS

    def sem(self, g):
        return self.sems[g.par]

    def all(self, g):
        per = self.per[g.layer.name]
        return g.pair * per + (self.base[g.layer.n] + per)


class Ring:

    def __init__(self, slots, uses, base):
        self.slots, self.uses, self.base = slots, uses, base
        assert 2 * uses % len(slots) == 0
        self.total = NG * uses // len(slots)

    def bank(self, g, u):
        return self.slots[(g.par * self.uses + u) % len(self.slots)]

    def count(self, g, u):
        n = g.par * self.uses + u
        per_pair = 2 * self.uses // len(self.slots)
        return g.pair * per_pair + (self.base[self.slots[n % len(self.slots)]] + n // len(self.slots) + 1)


def build(nc, x_in, ctx_in, ctxT_in, mask1_in, mask2_in, small_in, w1_in, w2_in, out):
    layers = make_layers()
    L0X, L0F, L1X, L1F, L2X, L2F, L3X, L3F = layers

    base = {b: CREDIT for b in range(8)}
    bank_base = []
    for layer in layers:
        bank_base.append(dict(base))
        layer.front_ring = Ring((4, 5), len(layer.front), dict(base))
        layer.body_ring = Ring(layer.body_banks, layer.body_uses, dict(base))
        rings = [layer.front_ring, layer.body_ring]
        if layer.heads:
            layer.score_ring = Ring((0, 2), TPG, dict(base))
            rings.append(layer.score_ring)
        for ring in rings:
            for b in ring.slots:
                base[b] += ring.total
    bank_base.append(dict(base))

    ctx = ExitStack()
    with ctx:
        def sb(name, shape, dt=F32):
            return ctx.enter_context(nc.sbuf_tensor(name, shape, dt))

        def step(name, **per):
            return Step(ctx.enter_context(nc.semaphore(name)), layers, per)

        def dma_step(name, **per):
            return DmaStep([ctx.enter_context(nc.semaphore(f"{name}{i}")) for i in range(2)], layers, per)

        ps = ctx.enter_context(nc.psum_tensor("ps", [P, 8, 512], F32))
        x_sb = sb("x_sb", [P, NT, D])
        small = sb("small", [P, SMALL_W])
        tgate = sb("tgate", [P, 8])
        arena_a = sb("arena_a", [P, 8192])
        arena_b = sb("arena_b", [P, 8192])
        xn = sb("xn", [P, TPG, D])
        ctxn = sb("ctxn", [P, TPG, D])
        ctx_sb = sb("ctx_sb", [P, 2, TPG, D])
        xcT = sb("xcT", [P, 2, 2 * GT])
        qT = sb("qT", [P, 2, 8, GT])
        kT = sb("kT", [P, 2, GT])
        probs = sb("probs", [P, TPG, 16 * S])
        pT = sb("pT", [P, TPG, 8, P])
        oT = sb("oT", [P, TPG, 8, P])
        vsmall = sb("vsmall", [P, 2, BPG * 8 * 16])
        o_sb = sb("o_sb", [P, TPG, D])
        acc = sb("acc", [P, TPG, D])
        masked = sb("masked", [P, NT, S], U8)
        st = sb("st", [P, 4, 6])
        mv = sb("mv", [P, 4, 2])
        agg = sb("agg", [P, 5, 4])
        veps = sb("veps", [P, 4])
        rstd = sb("rstd", [P, 4])
        neghalf = sb("neghalf", [P, 4])
        mx = sb("mx", [P, TPG, 16])
        sm = sb("sm", [P, TPG, 16])
        rv = sb("rv", [P, TPG, 16])
        route = sb("route", [P, 8, TPG * 8])
        cmp_gt = sb("cmp_gt", [P, TPG, 8, 8])
        cmp_eq = sb("cmp_eq", [P, TPG, 8, 8])
        comb = sb("comb", [P, 2, TPG, 8])
        combT = sb("combT", [8, 2, GT])
        rms_gain = sb("rms_gain", [P, 1])
        onemu = sb("onemu", [P, 2])

        def w(name):
            a, b = SMALL_AT[name]
            return small[:, a:b]

        filled = [ctx.enter_context(nc.semaphore(f"filled{b}")) for b in range(8)]
        drained = [ctx.enter_context(nc.semaphore(f"drained{b}")) for b in range(8)]
        att = dict(l0x=2, l0f=2, l1x=2, l2x=2, l3x=2)
        all2 = dict(att, l1f=2, l2f=2, l3f=2)
        s_stats = step("s_stats", **dict(all2, l2x=4))
        s_aggr = step("s_aggr", **{k: 7 for k in all2})
        s_veps = step("s_veps", **dict({k: 1 for k in all2}, l2x=3))
        s_rstd = step("s_rstd", **{k: 1 for k in all2})
        s_xn = step("s_xn", **dict(all2, l2x=4))
        s_ctx = dma_step("s_ctx", l0x=16, l1x=16, l2x=16, l3x=16)
        s_kspread = dma_step("s_kspread", l0f=256, l1x=256)
        s_rope = step("s_rope", l2x=4)
        s_mx = step("s_mx", **att)
        s_masked = step("s_masked", l1x=2, l2x=2)
        s_sub = step("s_sub", l1x=2, l2x=2)
        s_exp = step("s_exp", **att)
        s_sum = step("s_sum", **att)
        s_rv = step("s_rv", **att)
        s_probs = step("s_probs", **att)
        s_route = step("s_route", l0f=9, l1f=12, l2f=6)
        s_rexp = step("s_rexp", l0f=1, l1f=1, l2f=1)
        s_acc = step("s_acc", l0f=12)
        s_tmp = step("s_tmp", l1x=2, l3f=2)
        s_act = step("s_act", l1f=24)
        s_mix = step("s_mix", l3f=6)
        s_relu = step("s_relu", l3f=1)
        s_upd = step("s_upd", l0f=2, l1x=2, l1f=1, l2f=1, l3f=1)
        s_rank = step("s_rank", l0f=1, l1f=1, l2f=1)
        s_small = ctx.enter_context(nc.semaphore("s_small"))
        s_x = ctx.enter_context(nc.semaphore("s_x"))
        s_m1 = ctx.enter_context(nc.semaphore("s_m1"))
        s_m2 = ctx.enter_context(nc.semaphore("s_m2"))
        s_w1 = ctx.enter_context(nc.semaphore("s_w1"))
        s_w2 = ctx.enter_context(nc.semaphore("s_w2"))
        s_const = ctx.enter_context(nc.semaphore("s_const"))
        s_zero = ctx.enter_context(nc.semaphore("s_zero"))
        s_tanh = ctx.enter_context(nc.semaphore("s_tanh"))
        s_mask = ctx.enter_context(nc.semaphore("s_mask"))
        s_onemu = ctx.enter_context(nc.semaphore("s_onemu"))
        s_scale = ctx.enter_context(nc.semaphore("s_scale"))
        s_out = ctx.enter_context(nc.semaphore("s_out"))
        steps = [s_stats, s_aggr, s_veps, s_rstd, s_xn, s_rope, s_mx, s_masked, s_sub,
                 s_exp, s_sum, s_rv, s_probs, s_route, s_rexp, s_acc, s_tmp, s_act, s_mix, s_relu, s_upd, s_rank]

        ident = w("ident")

        def k_pairs(layer, par):
            arena = arena_b[:, par * 4096:(par + 1) * 4096]
            return arena.rearrange("p (c b k) -> p c b k", b=BPG, k=P)

        def v_pairs(layer, par):
            arena = arena_a[:, par * 4096:(par + 1) * 4096]
            return arena.rearrange("p (b c k) -> p b c k", b=BPG, k=P)

        def k_spread(par):
            return arena_a[:, par * 4096:(par + 1) * 4096].rearrange("p (h t) -> p h t", h=16)

        def k_rope(par):
            return arena_b[:, par * 1024:(par + 1) * 1024].rearrange("p (b n) -> p b n", b=BPG)

        def v_small(par):
            return vsmall[:, par, :].rearrange("p (b c e) -> p b c e", b=BPG, e=16)

        def v_rope(par):
            return vsmall[:, par, 0:BPG * 64].rearrange("p (b e) -> p b e", b=BPG)

        def w1_expert(e):
            return w("l1f_shared") if e == 0 else w1_sb[:, (e - 1) * EXPERT1:e * EXPERT1]

        w1_sb = arena_b
        w2_sb = arena_a

        def mask_staged(i):
            return (pT, oT)[i][:, :, :, :].rearrange("p a c t -> p (a c t)").rearrange("p (n k) -> p n k", k=S)

        def silu_buf(k):
            return kT[:, k % 2, :]

        def bank(b, n=512):
            return ps[:, b, 0:n]

        def score_bank(b):
            return ps[:, b:b + 2, :].rearrange("p a n -> p (a n)")

        def traverse(eng, do, start=None):
            for layer in layers:
                if start:
                    start(layer)
                for item in layer.front:
                    do(layer, item, Group(layer, 0, 0))

                def group(g, last=False):
                    for item in layer.order:
                        if item in layer.front:
                            if not last:
                                do(layer, item, g.next())
                        else:
                            do(layer, item, g)

                with eng.Fori(0, PAIRS - 1) as pair:
                    group(Group(layer, pair, 0))
                    group(Group(layer, pair, 1))
                group(Group(layer, PAIRS - 1, 0))
                group(Group(layer, PAIRS - 1, 1), last=True)

        block = ctx.enter_context(nc.Block())

        @block.sync
        def _(sp):
            for s in filled + drained:
                sp.sem_inc(s, CREDIT)
            for s in steps:
                sp.sem_inc(s.sem, s.credit)
            for s in (s_ctx, s_kspread):
                for i in range(2):
                    sp.sem_inc(s.sems[i], s.credit)
            sp.dma_start(small[:, :], small_in).then_inc(s_small, 16)
            x_v = x_in.rearrange("b s d -> (b s) d").rearrange("(n p) d -> p n d", p=P)
            for c in range(4):
                n = NT // 4
                sp.dma_start(x_sb[:, c * n:(c + 1) * n, :], x_v[:, c * n:(c + 1) * n, :]).then_inc(s_x, 16)
            ctx_v = ctx_in.rearrange("b s d -> (b s) d").rearrange("(n p) d -> p n d", p=P)
            out_v = out.rearrange("b s d -> (b s) d").rearrange("(n p) d -> p n d", p=P)

            def load_mask(dst, src, sem, n0, n1):
                src_v = src.rearrange("(n b) k -> b n k", b=2)
                for b in range(2):
                    sp.dma_start(dst[b * S:(b + 1) * S, :, :],
                                 src_v[b, n0:n1, :].partition_broadcast(S)).then_inc(sem, 16)

            def start(layer):
                if layer is L0X:
                    load_mask(mask_staged(0), mask1_in, s_m1, 0, NT // 2)
                    load_mask(mask_staged(1), mask1_in, s_m1, NT // 2, NT)
                if layer is L0F:
                    sp.wait_ge(s_zero, 1)
                    for b in L0X.body_banks:
                        sp.wait_ge(drained[b], bank_base[1][b])
                    sp.dma_start(w1_sb[:, 0:E_FF1 * EXPERT1], w1_in).then_inc(s_w1, 16)
                if layer is L1F:
                    for b in L1X.body_banks:
                        sp.wait_ge(drained[b], bank_base[3][b])
                    sp.dma_start(w2_sb[:, :], w2_in).then_inc(s_w2, 16)
                    load_mask(masked, mask2_in, s_m2, 0, NT)

            def do(layer, item, g):
                if item == ("F", 0) and layer.cross:
                    if layer is L2X:
                        sp.wait_ge(s_xn.sem, s_xn.after(g.back(2), 3))
                        sp.dma_start(ctx_sb[:, g.par, :, :],
                                     ctx_v[:, bass.ds(g.tile(0), TPG), :]).then_inc(s_ctx.sem(g), 16)
                    else:
                        u = len(layer.front) - 1
                        back = g.back(2)
                        sp.wait_ge(drained[layer.front_ring.bank(back, u)], layer.front_ring.count(back, u))
                        sp.dma_start(xcT[:, g.par, GT:2 * GT],
                                     ctxT_in[:, bass.ds(g.tile(0) * P, GT)]).then_inc(s_ctx.sem(g), 16)
                if item == ("QK", 0):
                    sp.wait_ge(drained[layer.front_ring.bank(g, 1)], layer.front_ring.count(g, 1))
                    back = g.back(2)
                    sp.wait_ge(filled[layer.score_ring.bank(back, TPG - 1)],
                               layer.score_ring.count(back, TPG - 1))
                    for h in range(16):
                        sp.dma_start(k_spread(g.par)[8 * h:8 * h + 8, h, :],
                                     kT[8 * h:8 * h + 8, g.par, :]).then_inc(s_kspread.sem(g), 16)
                if layer is L3F and item == ("V", 0):
                    sp.wait_ge(s_upd.sem, s_upd.after(g, 0))
                    sp.dma_start(out_v[:, bass.ds(g.tile(0), TPG), :],
                                 x_sb[:, bass.ds(g.tile(0), TPG), :]).then_inc(s_out, 16)

            traverse(sp, do, start)
            sp.wait_ge(s_out, 16 * NG)

        @block.gpsimd
        def _(pool):
            pool.memset(neghalf[:, :], -0.5).then_inc(s_const, 1)
            pool.memset(arena_b[:, :], 0.0).then_inc(s_const, 1)
            pool.memset(arena_a[:, :], 0.0).then_inc(s_const, 1)
            pool.memset(vsmall[:, :, :], 0.0).then_inc(s_const, 1)
            pool.wait_ge(s_const, 4)

            def start(layer):
                if layer is L0F:
                    for b in L0X.body_banks:
                        pool.wait_ge(drained[b], bank_base[1][b])
                    pool.memset(arena_a[:, :], 0.0).then_inc(s_zero, 1)
                if layer is L2X:
                    for b in L1F.body_banks:
                        pool.wait_ge(drained[b], bank_base[4][b])
                    pool.memset(arena_b[:, :], 0.0).then_inc(s_zero, 1)
                    pool.memset(vsmall[:, :, :], 0.0).then_inc(s_zero, 1)
                if layer is L2F:
                    for b in L2X.body_banks:
                        pool.wait_ge(drained[b], bank_base[5][b])
                    pool.memset(arena_b[:, :], 0.0).then_inc(s_zero, 1)
                if layer is L3X:
                    for b in L2F.body_banks:
                        pool.wait_ge(drained[b], bank_base[6][b])
                    pool.memset(arena_a[:, :], 0.0).then_inc(s_zero, 1)

            def do(layer, item, g):
                if item == ("F", 0):
                    n = 4 if layer is L2X else 2
                    last = 2 if layer is L2X else 0
                    pool.wait_ge(s_veps.sem, s_veps.after(g, last))
                    pool.wait_ge(s_xn.sem, s_xn.after(g.back(1), n - 1))
                    pool.tensor_tensor(rstd[:, 0:n], veps[:, 0:n], neghalf[:, 0:n],
                                       ALU.pow).then_inc(s_rstd.sem, 1)
                if item[0] == "S":
                    t, nh = item[1], layer.heads
                    pool.wait_ge(s_rv.sem, s_rv.after(g, t))
                    pr = probs[:, t, 0:nh * S].rearrange("p (h k) -> p h k", k=S)
                    pool.tensor_tensor(pr, pr, rv[:, t, 0:nh].unsqueeze(2).to_broadcast([P, nh, S]),
                                       ALU.mult).then_inc(s_probs.sem, 1)

            traverse(pool, do, start)

        @block.tensor
        def _(pe):
            def take(ring, g, u):
                b = ring.bank(g, u)
                pe.wait_ge(drained[b], ring.count(g, u) - 1)
                return b

            def wait_drained(ring, g, u):
                pe.wait_ge(drained[ring.bank(g, u)], ring.count(g, u))

            def last_uses(layer, kinds):
                return [v for v, item in enumerate(layer.front) if item[0] in kinds][-2:]

            def mm(o, lhsT, rhs, start=True, stop=True):
                return nc.tensor.matmul(o, lhsT, rhs, start=start, stop=stop, skip_group_check=True)

            def start(layer):
                if layer is L0X:
                    pe.wait_ge(s_small, 16)
                    pe.wait_ge(s_const, 4)
                if layer is L1F:
                    pe.wait_ge(s_w1, 16)
                if layer is L2F:
                    pe.wait_ge(s_w2, 16)

            def front(layer, item, g):
                ring = layer.front_ring
                u = layer.front.index(item)
                kind, j = item
                xT = xcT[:, g.par, 0:GT]
                cT = xcT[:, g.par, GT:2 * GT]
                b = take(ring, g, u)
                o = bank(b)
                if kind == "F":
                    for t in range(TPG):
                        pe.wait_ge(s_xn.sem, s_xn.after(g, t))
                        last = nc.tensor.transpose(o[:, t * P:(t + 1) * P], xn[:, t, :], ident)
                    if layer is L2X:
                        for t in range(TPG):
                            pe.wait_ge(s_xn.sem, s_xn.after(g, 2 + t))
                            last = nc.tensor.transpose(o[:, GT + t * P:GT + (t + 1) * P], ctxn[:, t, :], ident)
                    last.then_inc(filled[b], 1)
                    return
                if u == 1:
                    wait_drained(ring, g, 0)
                if layer.cross and layer is not L2X and kind in ("QK", "K", "V"):
                    pe.wait_ge(s_ctx.sem(g), s_ctx.all(g))
                if kind == "Q" and layer is not L2X:
                    for i in range(2):
                        c = 2 * j + i
                        last = mm(o[:, i * GT:(i + 1) * GT], w(layer.name + "_wq")[:, c * P:(c + 1) * P], xT)
                elif kind == "K" and layer is not L2X:
                    for i in range(2):
                        c = 2 * j + i
                        last = mm(o[:, i * GT:(i + 1) * GT], w(layer.name + "_wk")[:, c * P:(c + 1) * P], cT)
                elif kind == "Q" or kind == "K":
                    ww = w("l2x_wq") if kind == "Q" else w("l2x_wk")
                    for i in range(2):
                        last = mm(o[:, i * GT:(i + 1) * GT], ww[:, i * P:(i + 1) * P], xT if kind == "Q" else cT)
                elif kind == "QK":
                    mm(o[:, 0:GT], w(layer.name + "_wq"), xT)
                    last = mm(o[:, GT:2 * GT], w(layer.name + "_wk"), cT if layer.cross else xT)
                elif kind == "V":
                    src = cT if layer.cross else xT
                    wv = w(layer.name + "_wv")
                    seqs = [j] if layer is L3X else range(BPG)
                    n = {"l3x": 512, "l0x": 128, "l0f": 64, "l1x": 64, "l2x": 32}[layer.name]
                    for i, q in enumerate(seqs):
                        for half in range(2):
                            ww = wv if layer is L2X else wv[:, half * n:(half + 1) * n]
                            last = mm(o[half * S:(half + 1) * S, i * n:(i + 1) * n],
                                      src[:, q * S:(q + 1) * S], ww)
                elif kind == "G":
                    ne = layer.experts
                    for t in range(TPG):
                        last = mm(o[:, t * ne:(t + 1) * ne], xT[:, t * P:(t + 1) * P], w(layer.name + "_wg"))
                elif kind == "C":
                    pe.wait_ge(s_route.sem, s_route.after(g, 8))
                    for t in range(TPG):
                        last = nc.tensor.transpose(o[0:8, t * P:(t + 1) * P], comb[:, g.par, t, :], ident)
                last.then_inc(filled[b], 1)

            def do(layer, item, g):
                if item in layer.front:
                    front(layer, item, g)
                    return
                ring, fr = layer.body_ring, layer.front_ring
                kind = item[0]
                u = layer.first_use[item]
                xT = xcT[:, g.par, 0:GT]
                if kind == "S":
                    t = item[1]
                    b = take(layer.score_ring, g, t)
                    o = score_bank(b)
                    if t == 0:
                        for v in last_uses(layer, ("Q", "K", "QK")):
                            wait_drained(fr, g, v)
                        if layer in (L0F, L1X):
                            pe.wait_ge(s_kspread.sem(g), s_kspread.all(g))
                    for hb in range(2):
                        if layer in (L0F, L1X):
                            for half in range(2):
                                last = mm(o[hb * S:(hb + 1) * S, half * 512:(half + 1) * 512],
                                          qT[:, g.par, 0, t * P + hb * S:t * P + (hb + 1) * S],
                                          k_spread(g.par)[:, 8 * half:8 * half + 8,
                                                          t * P + hb * S:t * P + (hb + 1) * S])
                        if layer is L2X:
                            last = mm(o[hb * S:(hb + 1) * S, 0:4 * S],
                                      qT[:, g.par, 0, t * P + hb * S:t * P + (hb + 1) * S],
                                      k_rope(g.par)[:, 2 * t + hb, :])
                    if layer in (L0X, L3X):
                        for c in range(8):
                            for hb in range(2):
                                last = mm(o[hb * S:(hb + 1) * S, c * P:(c + 1) * P],
                                          qT[:, g.par, c, t * P + hb * S:t * P + (hb + 1) * S],
                                          k_pairs(layer, g.par)[:, c // 4 if layer is L0X else c, 2 * t + hb, :])
                    last.then_inc(filled[b], 1)
                elif kind == "T":
                    t = item[1]
                    pe.wait_ge(s_probs.sem, s_probs.after(g, t))
                    nchunk = layer.heads * S // P
                    for j in range(layer.uses["T"]):
                        b = take(ring, g, u + j)
                        for i in range(min(4, nchunk)):
                            c = 4 * j + i
                            last = nc.tensor.transpose(bank(b)[:, i * P:(i + 1) * P],
                                                       probs[:, t, c * P:(c + 1) * P], ident)
                        last.then_inc(filled[b], 1)
                elif kind == "A":
                    t = item[1]
                    ut = layer.first_use[("T", t)]
                    if t == 0:
                        for v in last_uses(layer, ("V",)):
                            wait_drained(fr, g, v)
                    for j in range(layer.uses["A"]):
                        b = take(ring, g, u + j)
                        o = bank(b)
                        for v in range(layer.uses["T"]):
                            if v == j or layer.uses["A"] == 1:
                                wait_drained(ring, g, ut + v)
                        if layer is L0X:
                            for hb in range(2):
                                last = mm(o[:, hb * 256:(hb + 1) * 256], v_pairs(layer, g.par)[:, 2 * t + hb, j, :],
                                          pT[:, t, 4 * j:4 * j + 4, hb * S:(hb + 1) * S])
                        elif layer is L3X:
                            for i in range(4):
                                for hb in range(2):
                                    last = mm(o[:, i * P + hb * S:i * P + (hb + 1) * S],
                                              v_pairs(layer, g.par)[:, 2 * t + hb, 4 * j + i, :],
                                              pT[:, t, 4 * j + i, hb * S:(hb + 1) * S])
                        elif layer is L2X:
                            for c in range(2):
                                last = mm(o[:, c * P:(c + 1) * P], pT[:, t, c, :],
                                          v_rope(g.par)[:, 2 * t:2 * t + 2, :])
                        else:
                            for c in range(8):
                                last = mm(o[:, c * 32:(c + 1) * 32], pT[:, t, c, :],
                                          v_small(g.par)[:, 2 * t:2 * t + 2, c, :])
                        last.then_inc(filled[b], 1)
                elif kind == "X":
                    t = item[1]
                    wait_drained(ring, g, layer.first_use[("A", t)])
                    b = take(ring, g, u)
                    nc.tensor.transpose(bank(b)[:, 0:P], o_sb[:, t, :], ident).then_inc(filled[b], 1)
                elif kind == "W":
                    t = item[1]
                    chunks = 8 if layer in (L0X, L3X) else 1
                    if chunks == 8:
                        for v in range(layer.uses["A"]):
                            wait_drained(ring, g, layer.first_use[("A", t)] + v)
                    else:
                        wait_drained(ring, g, layer.first_use[("X", t)])
                    b = take(ring, g, u)
                    for c in range(chunks):
                        last = mm(bank(b)[:, 0:D], oT[:, t, c, :], w(layer.name + "_wo")[:, c * D:(c + 1) * D],
                                  start=c == 0, stop=c == chunks - 1)
                    last.then_inc(filled[b], 1)
                elif kind == "E":
                    t = item[1]
                    for j in range(2):
                        b = take(ring, g, u + j)
                        mm(bank(b), xT[:, t * P:(t + 1) * P],
                           w("l0f_we")[:, j * 512:(j + 1) * 512]).then_inc(filled[b], 1)
                elif kind == "Z":
                    t = item[1]
                    wait_drained(fr, g, layer.front.index(("C", 0)))
                    b = take(ring, g, u)
                    mm(bank(b)[:, 0:D], combT[0:8, g.par, t * P:(t + 1) * P],
                       w("l0f_be")[0:8, :]).then_inc(filled[b], 1)
                elif kind == "U" and layer is L1F:
                    e, c = item[1:]
                    r0, n = HID1[c]
                    if item == layer.order[0]:
                        wait_drained(fr, g, 0)
                    b = take(ring, g, u)
                    mm(bank(b)[0:n, 0:GT], w1_expert(e)[:, r0:r0 + n], xT)
                    mm(bank(b)[0:n, GT:2 * GT], w1_expert(e)[:, I_FF + r0:I_FF + r0 + n], xT)\
                        .then_inc(filled[b], 1)
                elif kind == "U":
                    e, c = item[1:]
                    if item == layer.order[0]:
                        wait_drained(fr, g, 0)
                    b = take(ring, g, u)
                    for i in range(2):
                        a = e * EXPERT2 + (2 * c + i) * P
                        last = mm(bank(b)[:, i * GT:(i + 1) * GT], w2_sb[:, a:a + P], xT)
                    last.then_inc(filled[b], 1)
                elif kind == "D":
                    e = item[1]
                    nch = 3 if layer is L1F else 4
                    for c in range(nch if layer is L1F else 2):
                        wait_drained(ring, g, layer.first_use[("U", e, c)])
                    b = take(ring, g, u)
                    for t in range(TPG):
                        for c in range(nch):
                            if layer is L1F:
                                n = HID1[c][1]
                                a = 2 * I_FF + c * D
                                rhs = w1_expert(e)[0:n, a:a + D]
                            else:
                                n = P
                                a = e * EXPERT2 + FFN2 + c * D
                                rhs = w2_sb[:, a:a + D]
                            last = mm(bank(b)[:, t * D:(t + 1) * D],
                                      qT[0:n, e % 2, c, t * P:(t + 1) * P], rhs, start=c == 0, stop=c == nch - 1)
                    last.then_inc(filled[b], 1)
                elif layer is L3F and kind == "K":
                    pe.wait_ge(s_mix.sem, s_mix.after(g, 5))
                    b = take(ring, g, u)
                    mm(bank(b)[:, 0:GT], w("l3f_wk"), qT[:, g.par, 1, :]).then_inc(filled[b], 1)
                elif layer is L3F and kind == "R":
                    b = take(ring, g, u)
                    for t in range(TPG):
                        last = mm(bank(b)[:, t * D:(t + 1) * D], qT[:, g.par, 0, t * P:(t + 1) * P], w("l3f_wr"))
                    last.then_inc(filled[b], 1)
                elif layer is L3F and kind == "V":
                    pe.wait_ge(s_relu.sem, s_relu.after(g, 0))
                    b = take(ring, g, u)
                    for t in range(TPG):
                        last = mm(bank(b)[:, t * D:(t + 1) * D], qT[:, g.par, 3, t * P:(t + 1) * P], w("l3f_wv"))
                    last.then_inc(filled[b], 1)

            traverse(pe, do, start)

        @block.scalar
        def _(act):
            def wait_filled(ring, g, u):
                b = ring.bank(g, u)
                act.wait_ge(filled[b], ring.count(g, u))
                return b

            def wait_drained(ring, g, u):
                act.wait_ge(drained[ring.bank(g, u)], ring.count(g, u))

            def start(layer):
                if layer is L0X:
                    act.wait_ge(s_small, 16)
                    act.wait_ge(s_const, 4)
                    nc.scalar.activation(tgate[:, :], w("gates"), ACT.Tanh).then_inc(s_tanh, 1)
                    act.wait_ge(s_mask, 2)
                if layer is L2X:
                    act.wait_ge(s_scale, 1)
                    act.wait_ge(s_zero, 3)
                if layer is L0F:
                    act.wait_ge(s_zero, 1)
                if layer is L3X:
                    act.wait_ge(s_zero, 5)

            def do(layer, item, g):
                ring, fr = layer.body_ring, layer.front_ring
                kind = item[0]
                front = item in layer.front
                if front:
                    u = layer.front.index(item)
                else:
                    u = layer.first_use[item]
                if kind == "F":
                    b = wait_filled(fr, g, u)
                    if layer is L2X:
                        nc.scalar.activation(xcT[:, g.par, :], bank(b), ACT.Identity,
                                             scale=rms_gain[:, 0:1]).then_inc(drained[b], 1)
                    else:
                        nc.scalar.activation(xcT[:, g.par, 0:GT], bank(b, GT), ACT.Copy).then_inc(drained[b], 1)
                elif kind == "Q" and layer is not L2X:
                    b = wait_filled(fr, g, u)
                    j = item[1]
                    nc.scalar.activation(qT[:, g.par, 2 * j:2 * j + 2, :].rearrange("p c t -> p (c t)"), bank(b),
                                         ACT.Copy).then_inc(drained[b], 1)
                elif kind == "QK":
                    b = wait_filled(fr, g, u)
                    act.wait_ge(s_kspread.sem(g.back(2)), s_kspread.all(g.back(2)))
                    nc.scalar.activation(qT[:, g.par, 0, :], bank(b, GT), ACT.Identity,
                                         bias=w(layer.name + "_bq"))
                    nc.scalar.activation(kT[:, g.par, :], bank(b)[:, GT:2 * GT], ACT.Identity,
                                         bias=w(layer.name + "_bk")).then_inc(drained[b], 1)
                elif kind == "V" and layer in (L0X, L3X):
                    b = wait_filled(fr, g, u)
                    j = item[1]
                    for half in range(2):
                        rows = slice(half * S, (half + 1) * S)
                        if layer is L3X:
                            o = v_pairs(layer, g.par)[rows, j, :, half * S:(half + 1) * S]
                            i = bank(b)[rows, :].rearrange("p (c k) -> p c k", k=S)
                        else:
                            o = v_pairs(layer, g.par)[rows, :, 0:2, half * S:(half + 1) * S]
                            i = bank(b)[rows, :].rearrange("p (q c k) -> p q c k", c=2, k=S)
                        last = nc.scalar.activation(o, i, ACT.Copy)
                    last.then_inc(drained[b], 1)
                elif kind == "V" and layer is L2X:
                    b = wait_filled(fr, g, u)
                    for half in range(2):
                        rows = slice(half * S, (half + 1) * S)
                        last = nc.scalar.activation(v_rope(g.par)[rows, :, half * 32:(half + 1) * 32],
                                                    bank(b)[rows, 0:BPG * 32].rearrange("p (q d) -> p q d", d=32),
                                                    ACT.Copy)
                    last.then_inc(drained[b], 1)
                elif kind == "C":
                    b = wait_filled(fr, g, u)
                    nc.scalar.activation(combT[:, g.par, :], bank(b, GT)[0:8, :], ACT.Copy).then_inc(drained[b], 1)
                elif kind == "G":
                    n = TPG * layer.experts
                    if layer is L2F:
                        wait_drained(fr, g, u)
                        nc.scalar.activation(route[:, 1, 0:n], route[:, 0, 0:n], ACT.Exp,
                                             scale=-1.0).then_inc(s_rexp.sem, 1)
                    else:
                        act.wait_ge(s_route.sem, s_route.after(g, 1))
                        nc.scalar.activation(route[:, 1, 0:n], route[:, 0, 0:n], ACT.Exp).then_inc(s_rexp.sem, 1)
                elif kind == "S":
                    t = item[1]
                    if layer in (L1X, L2X):
                        act.wait_ge(s_sub.sem, s_sub.after(g, t))
                    else:
                        wait_drained(layer.score_ring, g, t)
                    pr = probs[:, t, 0:layer.heads * S]
                    nc.scalar.activation(pr, pr, ACT.Exp, scale=layer.scale).then_inc(s_exp.sem, 1)
                elif kind == "T":
                    t = item[1]
                    for j in range(layer.uses["T"]):
                        b = wait_filled(ring, g, u + j)
                        n = min(4, layer.heads * S // P)
                        nc.scalar.activation(pT[:, t, 4 * j:4 * j + n, :].rearrange("p c t -> p (c t)"),
                                             bank(b, n * P), ACT.Copy).then_inc(drained[b], 1)
                elif kind == "A" and layer in (L0X, L3X):
                    t = item[1]
                    for j in range(2):
                        b = wait_filled(ring, g, u + j)
                        if layer is L0X:
                            o = oT[:, t, 4 * j:4 * j + 4, :].rearrange("p i (b q) -> p b i q", b=2)
                            i = bank(b).rearrange("p (b i q) -> p b i q", b=2, i=4)
                        else:
                            o = oT[:, t, 4 * j:4 * j + 4, :].rearrange("p c t -> p (c t)")
                            i = bank(b)
                        nc.scalar.activation(o, i, ACT.Copy).then_inc(drained[b], 1)
                elif kind == "X":
                    t = item[1]
                    b = wait_filled(ring, g, u)
                    nc.scalar.activation(oT[:, t, 0, :], bank(b, P), ACT.Copy).then_inc(drained[b], 1)
                elif kind == "U" and layer is L1F:
                    e, c = item[1:]
                    n = HID1[c][1]
                    b = wait_filled(ring, g, u)
                    k = 3 * e + c
                    before = up_stages[k - 2]
                    gb = g if k >= 2 else g.back(1)
                    wait_drained(ring, gb, layer.first_use[before])
                    nc.scalar.activation(silu_buf(k)[0:n, :], bank(b)[0:n, 0:GT], ACT.Silu).then_inc(s_act.sem, 1)
                elif kind == "U":
                    e, c = item[1:]
                    b = wait_filled(ring, g, u)
                    nc.scalar.activation(qT[:, e % 2, 2 * c:2 * c + 2, :].rearrange("p c t -> p (c t)"), bank(b),
                                         ACT.Gelu).then_inc(drained[b], 1)
                elif layer is L3F and kind == "R":
                    b = wait_filled(ring, g, u)
                    act.wait_ge(s_upd.sem, s_upd.after(g.back(1), 0))
                    nc.scalar.activation(acc[:, :, :].rearrange("p t d -> p (t d)"), bank(b, GT),
                                         ACT.Sigmoid).then_inc(drained[b], 1)

            up_stages = [i for i in L1F.order if i[0] == "U"]
            traverse(act, do, start)

        @block.vector
        def _(dve):
            def wait_filled(ring, g, u):
                b = ring.bank(g, u)
                dve.wait_ge(filled[b], ring.count(g, u))
                return b

            def xt(g, t):
                return x_sb[:, bass.ds(g.tile(t), 1), :].rearrange("p a d -> p (a d)")

            def start(layer):
                if layer is not L0X:
                    dve.wait_ge(s_upd.sem, s_upd.base[layer.n])
                    for b in layers[layer.n - 1].body_banks:
                        dve.wait_ge(drained[b], bank_base[layer.n][b])
                if layer is L0X:
                    dve.wait_ge(s_x, 64)
                    dve.wait_ge(s_small, 16)
                    dve.wait_ge(s_const, 4)
                    dve.wait_ge(s_tanh, 1)
                    dve.wait_ge(s_m1, 64)
                    for i in range(2):
                        dve.tensor_scalar(masked[:, i * NT // 2:(i + 1) * NT // 2, :], mask_staged(i), 1.0, None,
                                          ALU.not_equal).then_inc(s_mask, 1)
                    dve.wait_ge(s_mask, 2)
                    dve.tensor_scalar(rms_gain[:, :], w("l2x_scale"), 1.0, None, ALU.add).then_inc(s_scale, 1)
                if layer is L0F:
                    dve.wait_ge(s_zero, 1)
                if layer is L2X:
                    dve.wait_ge(s_m2, 32)
                    dve.wait_ge(s_zero, 3)
                    dve.tensor_scalar(masked[:, :, :], masked[:, :, :], 0.0, None, ALU.is_equal).then_inc(s_mask, 1)
                    dve.wait_ge(s_mask, 3)
                if layer is L3X:
                    dve.wait_ge(s_zero, 5)

            def norm(layer, g):
                rms = layer is L2X
                if rms:
                    dve.wait_ge(s_ctx.sem(g), s_ctx.all(g))
                for t in range(TPG):
                    dve.bn_stats(st[:, t, :], xt(g, t)).then_inc(s_stats.sem, 1)
                if rms:
                    for t in range(TPG):
                        dve.bn_stats(st[:, 2 + t, :], ctx_sb[:, g.par, t, :]).then_inc(s_stats.sem, 1)
                n = 4 if rms else 2
                me, mo, ve, vo = (st[:, 0:n, i] for i in (1, 4, 2, 5))
                total, diff, within = (agg[:, i, 0:n] for i in range(3))
                dve.wait_ge(s_stats.sem, s_stats.after(g, n - 1))
                dve.tensor_tensor(total, me, mo, ALU.add).then_inc(s_aggr.sem, 1)
                dve.tensor_tensor(diff, me, mo, ALU.subtract).then_inc(s_aggr.sem, 1)
                dve.tensor_tensor(within, ve, vo, ALU.add).then_inc(s_aggr.sem, 1)
                dve.wait_ge(s_aggr.sem, s_aggr.after(g, 1))
                dve.tensor_tensor(agg[:, 3, 0:n], diff, diff, ALU.mult).then_inc(s_aggr.sem, 1)
                dve.tensor_scalar(mv[:, 0:n, 0], total, 0.5, None, ALU.mult).then_inc(s_aggr.sem, 1)
                dve.wait_ge(s_aggr.sem, s_aggr.after(g, 3))
                dve.scalar_tensor_tensor(out=agg[:, 4, 0:n], in0=agg[:, 3, 0:n], scalar=D / 4, in1=within,
                                         op0=ALU.mult, op1=ALU.add).then_inc(s_aggr.sem, 1)
                dve.wait_ge(s_aggr.sem, s_aggr.after(g, 5))
                dve.tensor_scalar(mv[:, 0:n, 1], agg[:, 4, 0:n], 1.0 / D, None, ALU.mult).then_inc(s_aggr.sem, 1)
                dve.wait_ge(s_aggr.sem, s_aggr.after(g, 6))
                if rms:
                    dve.tensor_scalar(veps[:, 0:2], mv[:, 0:2, 1], 1.0 + RMS_EPS, RMS_EPS * LN_EPS,
                                      ALU.mult, ALU.add).then_inc(s_veps.sem, 1)
                    dve.tensor_tensor(veps[:, 2:4], mv[:, 2:4, 0], mv[:, 2:4, 0], ALU.mult).then_inc(s_veps.sem, 1)
                    dve.wait_ge(s_veps.sem, s_veps.after(g, 1))
                    dve.scalar_tensor_tensor(out=veps[:, 2:4], in0=mv[:, 2:4, 1], scalar=RMS_EPS,
                                             in1=veps[:, 2:4], op0=ALU.add, op1=ALU.add).then_inc(s_veps.sem, 1)
                else:
                    dve.tensor_scalar(veps[:, 0:2], mv[:, 0:2, 1], LN_EPS, None, ALU.add).then_inc(s_veps.sem, 1)
                dve.wait_ge(s_rstd.sem, s_rstd.after(g, 0))
                wait_drained(layer.front_ring, g.back(1), 0)
                for t in range(TPG):
                    dve.tensor_scalar(xn[:, t, :], xt(g, t), mv[:, t, 0:1], rstd[:, t:t + 1],
                                      ALU.subtract, ALU.mult).then_inc(s_xn.sem, 1)
                if rms:
                    for t in range(TPG):
                        dve.tensor_scalar(ctxn[:, t, :], ctx_sb[:, g.par, t, :], rstd[:, 2 + t:3 + t], None,
                                          ALU.mult).then_inc(s_xn.sem, 1)

            def wait_drained(ring, g, u):
                dve.wait_ge(drained[ring.bank(g, u)], ring.count(g, u))

            def routing(layer, g, b):
                ne = layer.experts
                n = TPG * ne
                r = lambda k: route[:, k, 0:n].rearrange("p (t e) -> p t e", e=ne)
                k = [0]

                def chain(ins):
                    ins.then_inc(s_route.sem, 1)
                    dve.wait_ge(s_route.sem, s_route.after(g, k[0]))
                    k[0] += 1

                bc = lambda ap: ap.unsqueeze(2).to_broadcast([P, TPG, ne])
                bg = w(layer.name + "_bg").unsqueeze(1).to_broadcast([P, TPG, ne])
                dve.tensor_tensor(r(0), bank(b, n).rearrange("p (t e) -> p t e", e=ne), bg,
                                  ALU.add).then_inc(drained[b], 1)
                dve.wait_ge(drained[b], layer.front_ring.count(g, layer.front.index(("G", 0))))
                if layer is L2F:
                    dve.wait_ge(s_rexp.sem, s_rexp.after(g, 0))
                    chain(dve.tensor_scalar(r(2), r(1), 1.0, None, ALU.add))
                    chain(dve.reciprocal(r(3), r(2)))
                else:
                    chain(dve.tensor_reduce(route[:, 4, 0:TPG], r(0), AX_X, ALU.max))
                    chain(dve.tensor_tensor(r(0), r(0), bc(route[:, 4, 0:TPG]), ALU.subtract))
                    dve.wait_ge(s_rexp.sem, s_rexp.after(g, 0))
                    chain(dve.tensor_reduce(route[:, 4, 0:TPG], r(1), AX_X, ALU.add))
                    chain(dve.reciprocal(route[:, 5, 0:TPG], route[:, 4, 0:TPG]))
                    chain(dve.tensor_tensor(r(3), r(1), bc(route[:, 5, 0:TPG]), ALU.mult))
                gt = cmp_gt[:, :, 0:ne, 0:ne]
                eq = cmp_eq[:, :, 0:ne, 0:ne]
                other = r(3).unsqueeze(2).to_broadcast([P, TPG, ne, ne])
                own = r(3).unsqueeze(3).to_broadcast([P, TPG, ne, ne])
                tri = w("earlier").rearrange("p (e f) -> p e f", f=8)[:, 0:ne, 0:ne]
                dve.tensor_tensor(gt, other, own, ALU.is_gt)
                chain(dve.tensor_tensor(eq, other, own, ALU.is_equal))
                chain(dve.tensor_tensor(eq, eq, tri.unsqueeze(1).to_broadcast([P, TPG, ne, ne]), ALU.mult))
                chain(dve.tensor_tensor(gt, gt, eq, ALU.add))
                dve.tensor_reduce(r(6), gt, AX_X, ALU.add).then_inc(s_rank.sem, 1)
                dve.wait_ge(s_rank.sem, s_rank.after(g, 0))
                last = dve.scalar_tensor_tensor(out=comb[:, g.par, :, 0:ne], in0=r(6), scalar=float(layer.top),
                                                in1=r(3), op0=ALU.is_lt, op1=ALU.mult)
                if layer is L1F:
                    chain(last)
                    cw = comb[:, g.par, :, 0:ne]
                    chain(dve.tensor_reduce(route[:, 4, 0:TPG], cw, AX_X, ALU.add))
                    chain(dve.reciprocal(route[:, 5, 0:TPG], route[:, 4, 0:TPG]))
                    chain(dve.tensor_tensor(cw, cw, bc(route[:, 5, 0:TPG]), ALU.mult))
                else:
                    chain(last)
                assert k[0] == s_route.per[layer.name], (layer.name, k[0])

            def softmax(layer, g, t):
                nh = layer.heads
                b = wait_filled(layer.score_ring, g, t)
                sc = score_bank(b)[:, 0:nh * S].rearrange("p (h k) -> p h k", k=S)
                pr = probs[:, t, 0:nh * S].rearrange("p (h k) -> p h k", k=S)
                m = mx[:, t, 0:nh]
                mb = m.unsqueeze(2).to_broadcast([P, nh, S])
                back, ut = g.back(1), layer.first_use[("T", t)]
                for v in range(layer.uses["T"]):
                    wait_drained(layer.body_ring, back, ut + v)
                if layer in (L1X, L2X):
                    fill = F32_MIN if layer is L1X else MASK_FILL
                    mk = masked[:, bass.ds(g.tile(t), 1), :].to_broadcast([P, nh, S])
                    dve.scalar_tensor_tensor(out=pr, in0=mk, scalar=fill, in1=sc,
                                             op0=ALU.mult, op1=ALU.add).then_inc(drained[b], 1)
                    wait_drained(layer.score_ring, g, t)
                    dve.tensor_reduce(m, pr, AX_X, ALU.max).then_inc(s_mx.sem, 1)
                    dve.wait_ge(s_mx.sem, s_mx.after(g, t))
                    dve.tensor_tensor(pr, pr, mb, ALU.subtract).then_inc(s_sub.sem, 1)
                else:
                    dve.tensor_reduce(m, sc, AX_X, ALU.max).then_inc(s_mx.sem, 1)
                    dve.wait_ge(s_mx.sem, s_mx.after(g, t))
                    dve.tensor_tensor(pr, sc, mb, ALU.subtract).then_inc(drained[b], 1)
                dve.wait_ge(s_exp.sem, s_exp.after(g, t))
                dve.tensor_reduce(sm[:, t, 0:nh], pr, AX_X, ALU.add).then_inc(s_sum.sem, 1)
                dve.wait_ge(s_sum.sem, s_sum.after(g, t))
                dve.reciprocal(rv[:, t, 0:nh], sm[:, t, 0:nh]).then_inc(s_rv.sem, 1)

            def residual(layer, g, t, src, extra=None):
                return dve.scalar_tensor_tensor(out=xt(g, t), in0=src, scalar=tgate[:, layer.n:layer.n + 1],
                                                in1=xt(g, t), op0=ALU.mult, op1=ALU.add)

            def do(layer, item, g):
                ring, fr = layer.body_ring, layer.front_ring
                kind = item[0]
                front = item in layer.front
                u = layer.front.index(item) if front else layer.first_use[item]
                if kind == "F":
                    norm(layer, g)
                    if layer is L3F:
                        mix(g)
                elif kind == "K" and front and layer is not L2X:
                    b = wait_filled(fr, g, u)
                    j = item[1]
                    for half in range(2):
                        rows = slice(half * S, (half + 1) * S)
                        last = dve.tensor_copy(k_pairs(layer, g.par)[rows, 2 * j:2 * j + 2, :, half * S:(half + 1) * S],
                                               bank(b)[rows, :].rearrange("p (c q k) -> p c q k", c=2, k=S))
                    last.then_inc(drained[b], 1)
                elif kind in ("Q", "K") and layer is L2X:
                    b = wait_filled(fr, g, u)
                    at = 0 if kind == "Q" else 2
                    tab = w("rope").rearrange("p (n s) -> p n s", s=S)
                    cos = tab[:, at, :].unsqueeze(1).to_broadcast([P, BPG, S])
                    sin = tab[:, at + 1, :].unsqueeze(1).to_broadcast([P, BPG, S])
                    v = lambda ap: ap.rearrange("p (b s) -> p b s", s=S)
                    n = 0 if kind == "Q" else 2
                    c1 = v(qT[:, g.par, n + 2, :])
                    c2 = v(qT[:, g.par, n + 3, :])
                    dve.tensor_tensor(c1, v(bank(b, GT)), cos, ALU.mult).then_inc(s_rope.sem, 1)
                    dve.tensor_tensor(c2, v(bank(b)[:, GT:2 * GT]), sin, ALU.mult).then_inc(s_rope.sem, 1)
                    dve.wait_ge(s_rope.sem, s_rope.after(g, n + 1))
                    if kind == "Q":
                        dve.tensor_tensor(v(qT[:, g.par, 0, :]), c1, c2, ALU.add).then_inc(drained[b], 1)
                    else:
                        for h in range(4):
                            r0 = 32 * h
                            last = dve.tensor_tensor(k_rope(g.par)[r0:r0 + 32, :, h * S:(h + 1) * S],
                                                     c1[r0:r0 + 32], c2[r0:r0 + 32], ALU.add)
                        last.then_inc(drained[b], 1)
                elif kind == "V" and front and layer in (L0F, L1X):
                    b = wait_filled(fr, g, u)
                    for half in range(2):
                        rows = slice(half * S, (half + 1) * S)
                        bv = w(layer.name + "_bv")[rows, :].rearrange("p (c d) -> p c d", d=8)
                        last = dve.tensor_tensor(v_small(g.par)[rows, :, :, half * 8:(half + 1) * 8],
                                                 bank(b)[rows, 0:BPG * 64].rearrange("p (q c d) -> p q c d", c=8, d=8),
                                                 bv.unsqueeze(1).to_broadcast([S, BPG, 8, 8]), ALU.add)
                    last.then_inc(drained[b], 1)
                elif kind == "G":
                    routing(layer, g, wait_filled(fr, g, u))
                elif kind == "S":
                    softmax(layer, g, item[1])
                elif kind == "A" and layer in (L0F, L1X, L2X):
                    t = item[1]
                    b = wait_filled(ring, g, u)
                    e = 16 if layer is not L2X else 64
                    c = 8 if layer is not L2X else 2
                    src = bank(b, c * 2 * e).rearrange("p (c b e) -> p c b e", b=2, e=e)
                    for half in range(2):
                        rows = slice(half * S, (half + 1) * S)
                        last = dve.tensor_copy(o_sb[rows, t, :].rearrange("p (c e) -> p c e", e=e), src[rows, :, half, :])
                    last.then_inc(drained[b], 1)
                elif kind == "E":
                    t = item[1]
                    wait_drained(ring, g, layer.first_use[("A", t)])
                    for j in range(2):
                        b = wait_filled(ring, g, u + j)
                        for i in range(4):
                            e = 4 * j + i
                            src = o_sb[:, t, :] if e == 0 else acc[:, t, :]
                            add = dve.scalar_tensor_tensor(out=acc[:, t, :], in0=bank(b)[:, i * D:(i + 1) * D],
                                                           scalar=comb[:, g.par, t, e:e + 1], in1=src,
                                                           op0=ALU.mult, op1=ALU.add)
                            if i < 3:
                                add.then_inc(s_acc.sem, 1)
                                dve.wait_ge(s_acc.sem, s_acc.after(g, 6 * t + 3 * j + i))
                            else:
                                add.then_inc(drained[b], 1)
                                wait_drained(ring, g, u + j)
                elif kind == "Z":
                    t = item[1]
                    b = wait_filled(ring, g, u)
                    dve.tensor_tensor(acc[:, t, :], bank(b, D), acc[:, t, :], ALU.add).then_inc(drained[b], 1)
                    wait_drained(ring, g, u)
                    residual(layer, g, t, acc[:, t, :]).then_inc(s_upd.sem, 1)
                elif kind == "W":
                    t = item[1]
                    b = wait_filled(ring, g, u)
                    if layer is L1X:
                        dve.tensor_tensor(acc[:, t, :], bank(b, D), w("l1x_bo"), ALU.add).then_inc(drained[b], 1)
                        wait_drained(ring, g, u)
                        residual(layer, g, t, acc[:, t, :]).then_inc(s_upd.sem, 1)
                    else:
                        residual(layer, g, t, bank(b, D)).then_inc(drained[b], 1)
                elif kind == "U" and layer is L1F:
                    e, c = item[1:]
                    n = HID1[c][1]
                    b = ring.bank(g, u)
                    k = 3 * e + c
                    dve.wait_ge(s_act.sem, s_act.after(g, k))
                    dve.tensor_tensor(qT[0:n, e % 2, c, :], silu_buf(k)[0:n, :], bank(b)[0:n, GT:2 * GT],
                                      ALU.mult).then_inc(drained[b], 1)
                elif kind == "D":
                    e = item[1]
                    b = wait_filled(ring, g, u)
                    if layer is L1F and e == 0:
                        dve.tensor_copy(acc[:, :, :].rearrange("p t d -> p (t d)"), bank(b, GT)).then_inc(drained[b], 1)
                    else:
                        r = e - 1 if layer is L1F else e
                        for t in range(TPG):
                            src = bank(b)[:, t * D:(t + 1) * D]
                            if e == 0:
                                last = dve.tensor_scalar(acc[:, t, :], src, comb[:, g.par, t, r:r + 1], None, ALU.mult)
                            else:
                                last = dve.scalar_tensor_tensor(out=acc[:, t, :], in0=src,
                                                                scalar=comb[:, g.par, t, r:r + 1], in1=acc[:, t, :],
                                                                op0=ALU.mult, op1=ALU.add)
                        last.then_inc(drained[b], 1)
                    wait_drained(ring, g, u)
                    if e == 7:
                        xg = x_sb[:, bass.ds(g.tile(0), TPG), :]
                        dve.scalar_tensor_tensor(out=xg, in0=acc[:, :, :], scalar=tgate[:, layer.n:layer.n + 1],
                                                 in1=xg, op0=ALU.mult, op1=ALU.add).then_inc(s_upd.sem, 1)
                elif layer is L3F and kind == "K":
                    b = wait_filled(ring, g, u)
                    dve.tensor_scalar(qT[:, g.par, 2, :], bank(b, GT), 0.0, None, ALU.max).then_inc(drained[b], 1)
                    wait_drained(ring, g, u)
                    dve.tensor_tensor(qT[:, g.par, 3, :], qT[:, g.par, 2, :], qT[:, g.par, 2, :],
                                      ALU.mult).then_inc(s_relu.sem, 1)
                elif layer is L3F and kind == "V":
                    b = wait_filled(ring, g, u)
                    wait_drained(ring, g, layer.first_use[("R", 0)])
                    a = acc[:, :, :]
                    dve.tensor_tensor(a, bank(b, GT).rearrange("p (t d) -> p t d", d=D), a, ALU.mult)\
                        .then_inc(drained[b], 1)
                    wait_drained(ring, g, u)
                    xg = x_sb[:, bass.ds(g.tile(0), TPG), :]
                    dve.scalar_tensor_tensor(out=xg, in0=a, scalar=tgate[:, layer.n:layer.n + 1],
                                             in1=xg, op0=ALU.mult, op1=ALU.add).then_inc(s_upd.sem, 1)

            def mix(g):
                wait_drained(L3F.front_ring, g, 0)
                wait_drained(L3F.body_ring, g.back(2), 2)
                v = lambda ap: ap.rearrange("p (b s) -> p b s", s=S)
                xT = v(xcT[:, g.par, 0:GT])
                for i, mu in enumerate(("l3f_mur", "l3f_muk")):
                    m = w(mu)
                    o = v(qT[:, g.par, i, :])
                    prev = v(qT[:, g.par, 4 + i, :])
                    dve.tensor_scalar(prev, xT, onemu[:, i:i + 1], None, ALU.mult).then_inc(s_mix.sem, 1)
                    dve.tensor_scalar(o[:, :, 0:1], xT[:, :, 0:1], m, None, ALU.mult).then_inc(s_mix.sem, 1)
                    dve.wait_ge(s_mix.sem, s_mix.after(g, 3 * i))
                    dve.scalar_tensor_tensor(out=o[:, :, 1:S], in0=xT[:, :, 1:S], scalar=m, in1=prev[:, :, 0:S - 1],
                                             op0=ALU.mult, op1=ALU.add).then_inc(s_mix.sem, 1)

            dve.wait_ge(s_small, 16)
            for i, mu in enumerate(("l3f_mur", "l3f_muk")):
                dve.tensor_scalar(onemu[:, i:i + 1], w(mu), -1.0, 1.0, ALU.mult, ALU.add).then_inc(s_onemu, 1)
            dve.wait_ge(s_onemu, 2)
            traverse(dve, do, start)


def _pack_small(np, a):
    def rows(v, n=P):
        return np.broadcast_to(v[None, :], (n, v.shape[0]))

    def col(v):
        return v[:, None]

    def value_cols(wt):
        d = wt.shape[1] // 16
        return wt.reshape(D, 8, 2, d).transpose(0, 2, 1, 3).reshape(D, -1)

    def value_bias(v):
        v = v.reshape(8, 2, 8)
        return np.concatenate([rows(v[:, 0].reshape(-1), S), rows(v[:, 1].reshape(-1), S)], 0)

    def swapped(wt):
        h = wt.shape[1] // ROPE_D
        return wt.reshape(D, h, 2, ROPE_D // 2)[:, :, ::-1].reshape(D, -1)

    def down(wt):
        n = -(-wt.shape[0] // P)
        full = np.zeros((n * P, D), np.float32)
        full[:wt.shape[0]] = wt
        return full.reshape(n, P, D).transpose(1, 0, 2).reshape(P, n * D)

    p = {}
    p["l0x_wq"] = a["L0_xattn_Wq"].reshape(2, 2, 4, 64, D).transpose(4, 0, 2, 1, 3).reshape(D, 1024)
    p["l0x_wk"] = a["L0_xattn_Wk"].T
    p["l0x_wv"] = a["L0_xattn_Wv"].T.reshape(D, 2, 2, 64).transpose(0, 2, 1, 3).reshape(D, 256)
    p["l0x_wo"] = a["L0_xattn_Wo"].reshape(D, 2, 2, 4, 64).transpose(2, 4, 1, 3, 0).reshape(P, 1024)
    qkv, bqkv = a["L0_ffn_W_qkv"], a["L0_ffn_b_qkv"]
    p["l0f_wq"], p["l0f_wk"], p["l0f_wv"] = qkv[:, :D], qkv[:, D:2 * D], value_cols(qkv[:, 2 * D:])
    p["l0f_bq"], p["l0f_bk"], p["l0f_bv"] = col(bqkv[:D]), col(bqkv[D:2 * D]), value_bias(bqkv[2 * D:])
    p["l0f_wg"], p["l0f_bg"] = a["L0_ffn_W_gate"], rows(a["L0_ffn_b_gate"])
    p["l0f_we"] = a["L0_ffn_W_experts"].transpose(1, 0, 2).reshape(D, 1024)
    be = np.zeros((P, D), np.float32)
    be[:E_FF0] = a["L0_ffn_b_experts"]
    p["l0f_be"] = be
    p["l1x_wq"], p["l1x_wk"], p["l1x_wv"] = a["L1_xattn_Wq"].T, a["L1_xattn_Wk"].T, value_cols(a["L1_xattn_Wv"].T)
    p["l1x_bq"], p["l1x_bk"], p["l1x_bv"] = col(a["L1_xattn_bq"]), col(a["L1_xattn_bk"]), value_bias(a["L1_xattn_bv"])
    p["l1x_wo"], p["l1x_bo"] = a["L1_xattn_Wo"].T, rows(a["L1_xattn_bo"])
    p["l1f_wg"], p["l1f_bg"] = a["L1_ffn_wr"].T, rows(a["L1_ffn_rb"])
    p["l1f_shared"] = np.concatenate([a["L1_ffn_sg"].T, a["L1_ffn_su"].T, down(a["L1_ffn_sd"].T)], 1)
    p["l2x_scale"] = col(a["L2_xattn_rms_scale"])
    q2 = a["L2_xattn_q_w"].transpose(1, 0, 2).reshape(D, D)
    k2 = np.concatenate([a["L2_xattn_kv_w"][0, 0]] * 4, 1)
    p["l2x_wq"] = np.concatenate([q2, swapped(q2)], 1)
    p["l2x_wk"] = np.concatenate([k2, swapped(k2)], 1)
    p["l2x_wv"] = a["L2_xattn_kv_w"][1, 0]
    p["l2x_wo"] = a["L2_xattn_out_w"].reshape(D, D)
    p["l2f_wg"], p["l2f_bg"] = a["L2_ffn_Wr"], rows(a["L2_ffn_br"])
    p["l3x_wq"], p["l3x_wk"], p["l3x_wv"] = a["L3_xattn_Wq"], a["L3_xattn_Wk"], value_cols(a["L3_xattn_Wv"])
    p["l3x_wo"] = a["L3_xattn_Wo"].reshape(8, P, D).transpose(1, 0, 2).reshape(P, 1024)
    p["l3f_wr"], p["l3f_wk"], p["l3f_wv"] = a["L3_ffn_W_r"].T, a["L3_ffn_W_k"].T, a["L3_ffn_W_v"].T
    p["l3f_mur"], p["l3f_muk"] = col(a["L3_ffn_mu_r"]), col(a["L3_ffn_mu_k"])
    p["gates"] = rows(np.stack([a["g_xattn"], a["g_ffn"]], 1).reshape(-1))
    p["ident"] = np.eye(P, dtype=np.float32)
    p["earlier"] = rows((np.arange(8)[:, None] > np.arange(8)[None, :]).astype(np.float32).reshape(-1))
    half = ROPE_D // 2
    d = np.arange(P) % ROPE_D
    timescale = np.float32(10000.0) ** (np.float32(2.0 / ROPE_D) * (d % half).astype(np.float32))
    sign = np.where(d < half, -1.0, 1.0).astype(np.float32)[:, None]
    tabs = []
    for pos in (np.arange(S, 2 * S), np.arange(S)):
        rad = pos.astype(np.float32)[None, :] / timescale[:, None]
        tabs += [np.cos(rad), np.sin(rad) * sign]
    p["rope"] = np.concatenate(tabs, 1).astype(np.float32)
    for name, width in SMALL:
        assert p[name].shape == (P, width), (name, p[name].shape)
    w1 = [np.concatenate([a["L1_ffn_rg"][e].T, a["L1_ffn_ru"][e].T, down(a["L1_ffn_rd"][e].T)], 1)
          for e in range(E_FF1)]
    w2 = [np.concatenate([a["L2_ffn_W1"][e], down(a["L2_ffn_W2"][e])], 1) for e in range(E_FF2)]
    return (np.concatenate([p[name] for name, _ in SMALL], 1), np.concatenate(w1, 1), np.concatenate(w2, 1))


def kernel(**inputs):
    import numpy as _np
    import concourse.bacc as _bacc
    from concourse import mybir as _mybir
    from concourse.bass_utils import run_bass_kernel_spmd as _run

    a = {k: _np.asarray(v) for k, v in inputs.items()}
    small, w1, w2 = _pack_small(_np, a)
    ctxT = a["ctx_1024"].reshape(B * S, D).T
    named = {
        "x": a["x"], "ctx": a["ctx_1024"], "ctxT": ctxT, "mask1": a["mask_BxS2_ff1"], "mask2": a["mask_BxS2_bk0"],
        "small": small, "w1": w1, "w2": w2,
    }
    nc = _bacc.Bacc("TRN2", target_bir_lowering=False, num_devices=1)
    arrays, args = {}, []
    for name, v in named.items():
        v = _np.ascontiguousarray(v)
        arrays[f"in_{name}"] = v
        args.append(nc.dram_tensor(f"in_{name}", v.shape, _mybir.dt.from_np(v.dtype), kind="ExternalInput").ap())
    args.append(nc.dram_tensor("out_0", (B, S, D), _mybir.dt.from_np(_np.dtype("float32")),
                               kind="ExternalOutput").ap())
    build(nc, *args)
    r = _run(nc, [arrays], core_ids=[0])
    return r.results[0]["out_0"]
```

```python
from contextlib import ExitStack

import concourse.bass as bass
from concourse import mybir

ALU = mybir.AluOpType
ACT = mybir.ActivationFunctionType
F32 = mybir.dt.float32
U8 = mybir.dt.uint8
AX_X = mybir.AxisListType.X

P = 128
B, S, D = 128, 64, 128
NT = B * S // P
GT = 256
TPG = GT // P
BPG = GT // S
NG = B * S // GT
PAIRS = NG // 2
LN_EPS = 1e-5
RMS_EPS = 1e-6
F32_MIN = -3.4028234663852886e38
E_F32 = 2.718281828459045
MASK_FILL = -2.3819763e38
I_FF, E_FF1 = 352, 7
FFN2, E_FF2 = 512, 8
E_FF0 = 8
ROPE_D = 32

CREDIT = 64

SMALL = [
    ("l0x_wq", 1024), ("l0x_wk", 256), ("l0x_wv", 256), ("l0x_wo", 1024),
    ("l0f_wq", 128), ("l0f_wk", 128), ("l0f_wv", 128), ("l0f_bq", 1), ("l0f_bk", 1), ("l0f_bv", 64),
    ("l0f_wg", 8), ("l0f_bg", 8), ("l0f_we", 1024), ("l0f_be", 128),
    ("l1x_wq", 128), ("l1x_wk", 128), ("l1x_wv", 128), ("l1x_bq", 1), ("l1x_bk", 1), ("l1x_bv", 64),
    ("l1x_wo", 128), ("l1x_bo", 128),
    ("l1f_wg", 7), ("l1f_bg", 7), ("l1f_shared", 2 * 352 + 3 * 128),
    ("l2x_scale", 1), ("l2x_wq", 256), ("l2x_wk", 256), ("l2x_wv", 32), ("l2x_wo", 128),
    ("l2f_wg", 8), ("l2f_bg", 8),
    ("l3f_wr", 128), ("l3f_wk", 128), ("l3f_wv", 128), ("l3f_mur", 1), ("l3f_muk", 1),
    ("gates", 8), ("ident", 128), ("earlier", 64), ("rope", 256),
]
SMALL_AT, _n = {}, 0
for _name, _w in SMALL:
    SMALL_AT[_name] = (_n, _n + _w)
    _n += _w
SMALL_W = _n
LATE = ["l3x_wq", "l3x_wk", "l3x_wv", "l3x_wo"]
for _i, _name in enumerate(LATE):
    SMALL_AT[_name] = (1024 * _i, 1024 * (_i + 1))
assert 1024 * len(LATE) <= SMALL_AT["l1x_wq"][0]
EXPERT1 = 2 * I_FF + 3 * D
EXPERT2 = FFN2 + 4 * D
HID1 = [(0, 128), (128, 128), (256, 96)]


class Layer:

    def __init__(self, n, name, order, uses, body_banks, heads=0, scale=1.0, cross=False,
                 experts=0, top=0):
        self.n, self.name, self.order, self.uses = n, name, order, uses
        self.body_banks = body_banks
        self.heads, self.scale, self.cross = heads, scale, cross
        self.experts, self.top = experts, top
        self.front = []
        self.body = []
        for item, lag in order:
            if item[0] in ("L", "M", "H", "S", "N"):
                continue
            (self.front if lag == 1 else self.body).extend([item] * uses.get(item[0], 1))

    def use(self, item):
        return (self.front if item in self.front else self.body).index(item)


def stages(text):
    out = []
    for word in text.split():
        name = word.rstrip("+-")
        lag = word.count("+") - word.count("-")
        kind = name.rstrip("0123456789.")
        numbers = [int(k) for k in name[len(kind):].split(".")] if name != kind else [0]
        out.append(((kind, *numbers), lag))
    return out


def make_layers():
    attention = {"T": 2, "A": 2}
    narrow = {"T": 2, "A": 1, "E": 2}
    l0x = Layer(0, "l0x", stages(
        "S0 T0- F+ T1- L++ S1 A0- Q0+ N0 A1- Q1+ M++ W0- Q2+ K0+ N1 W1- Q3+ V0+"),
        attention, (6, 7), 16, 64 ** -0.5, True)
    l0f = Layer(1, "l0f", stages(
        "F+ S0 T0- QK+ T1- G+ S1 A0- L++ A1- V+ N0 H+ E0+ M++ C+ N1 E1+ Z0+ Z1+"),
        narrow, (6, 7), 16, 8 ** -0.5, False, E_FF0, 2)
    l1x = Layer(2, "l1x", stages(
        "F+ S0 T0- QK+ T1- L++ S1 A0- N0 A1- V+ X0- M++ X1- N1 W0- W1-"),
        narrow, (6, 7), 16, 8 ** -0.5, True)
    order = []
    for e in range(8):
        order += [(("U", e, 0), 0), (("U", e, 1), 0)]
        if e:
            order.append((("D", e - 1), 0))
        order.append((("U", e, 2), 0))
        order += stages({0: "F+", 1: "L++", 2: "G+", 4: "M++", 5: "H+"}.get(e, ""))
    order.append((("D", 7), 0))
    l1f = Layer(3, "l1f", order, {}, (0, 1, 2, 3), experts=E_FF1, top=2)
    l2x = Layer(4, "l2x", stages(
        "F+ S0 T0- Q+ T1- L++ S1 A0- K+ N0 A1- V+ X0- M++ X1- N1 W0- W1-"),
        {"T": 1, "A": 1}, (6, 7), 4, 32 ** -0.5, True)
    order = []
    for e in range(8):
        order += [(("U", e, 0), 0), (("U", e, 1), 0)]
        if e:
            order.append((("D", e - 1), 0))
        order += stages({0: "F+", 1: "L++", 2: "G+", 4: "M++", 5: "H+"}.get(e, ""))
    order.append((("D", 7), 0))
    l2f = Layer(5, "l2f", order, {}, (0, 1, 2, 3), experts=E_FF2, top=1)
    l3x = Layer(6, "l3x", stages(
        "S0 T0- F+ T1- L++ S1 A0- Q0+ N0 A1- Q1+ M++ W0- Q2+ N1 W1- Q3+ K0+ K1+ K2+ K3+ V0+ V1+ V2+ V3+"),
        attention, (6, 7), 16, 64 ** -0.5, True)
    l3f = Layer(7, "l3f", stages("KF F+ L++ RF M++ VF"), {}, (0, 1, 2))
    return [l0x, l0f, l1x, l1f, l2x, l2f, l3x, l3f]


class Group:

    def __init__(self, layer, pair, par):
        self.layer, self.pair, self.par = layer, pair, par

    def ahead(self, n):
        k = self.par + n
        return Group(self.layer, self.pair + k // 2, k % 2)

    def back(self, n):
        return self.ahead(-n)

    def tile(self, t):
        return self.pair * (2 * TPG) + (self.par * TPG + t)


class Step:

    def __init__(self, sem, layers, per):
        self.credit = max(CREDIT, 4 * max(per.values()))
        self.sem, self.per, self.base, n = sem, per, {}, self.credit
        for layer in layers:
            self.base[layer.n] = n
            n += per.get(layer.name, 0) * NG
        self.base[len(layers)] = n

    def after(self, g, k):
        per = self.per[g.layer.name]
        return g.pair * (2 * per) + (self.base[g.layer.n] + g.par * per + k + 1)


class DmaStep:

    def __init__(self, sems, layers, per):
        self.credit = max(CREDIT, 2 * max(per.values()))
        self.sems, self.per, self.base, n = sems, per, {}, self.credit
        for layer in layers:
            self.base[layer.n] = n
            n += per.get(layer.name, 0) * PAIRS

    def sem(self, g):
        return self.sems[g.par]

    def all(self, g):
        per = self.per[g.layer.name]
        return g.pair * per + (self.base[g.layer.n] + per)


class Ring:

    def __init__(self, slots, uses, base):
        self.slots, self.uses, self.base = slots, uses, base
        assert 2 * uses % len(slots) == 0
        self.total = NG * uses // len(slots)

    def bank(self, g, u):
        return self.slots[(g.par * self.uses + u) % len(self.slots)]

    def count(self, g, u):
        n = g.par * self.uses + u
        per_pair = 2 * self.uses // len(self.slots)
        return g.pair * per_pair + (self.base[self.slots[n % len(self.slots)]] + n // len(self.slots) + 1)


def build(nc, x_in, ctx_in, ctxT_in, mask1_in, mask2_in, small_in, late_in, w1_in, w2_in, out):
    layers = make_layers()
    L0X, L0F, L1X, L1F, L2X, L2F, L3X, L3F = layers

    base = {b: CREDIT for b in range(8)}
    bank_base = []
    for layer in layers:
        bank_base.append(dict(base))
        layer.front_ring = Ring((4, 5), len(layer.front), dict(base))
        layer.body_ring = Ring(layer.body_banks, len(layer.body), dict(base))
        rings = [layer.front_ring, layer.body_ring]
        if layer.heads:
            layer.score_ring = Ring((0, 2), TPG, dict(base))
            rings.append(layer.score_ring)
        for ring in rings:
            for b in ring.slots:
                base[b] += ring.total
    bank_base.append(dict(base))

    ctx = ExitStack()
    with ctx:
        def sb(name, shape, dt=F32):
            return ctx.enter_context(nc.sbuf_tensor(name, shape, dt))

        def step(name, **per):
            return Step(ctx.enter_context(nc.semaphore(name)), layers, per)

        def dma_step(name, **per):
            return DmaStep([ctx.enter_context(nc.semaphore(f"{name}{i}")) for i in range(2)], layers, per)

        ps = ctx.enter_context(nc.psum_tensor("ps", [P, 8, 512], F32))
        x_sb = sb("x_sb", [P, NT, D])
        small = sb("small", [P, SMALL_W])
        tgate = sb("tgate", [P, 8])
        arena_a = sb("arena_a", [P, 8192])
        arena_b = sb("arena_b", [P, 8192])
        xn = sb("xn", [P, 2, TPG, D])
        ctxn = sb("ctxn", [P, 2, TPG, D])
        ctx_sb = sb("ctx_sb", [P, 2, TPG, D])
        xcT = sb("xcT", [P, 2, 2 * GT])
        qT = sb("qT", [P, 2, 8, GT])
        kT = sb("kT", [P, 2, GT])
        probs = sb("probs", [P, 2, TPG, 16 * S])
        pT = sb("pT", [P, TPG, 8, P])
        oT = sb("oT", [P, TPG, 8, P])
        vsmall = sb("vsmall", [P, 2, BPG * 8 * 16])
        o_sb = sb("o_sb", [P, TPG, D])
        acc = sb("acc", [P, 2, TPG, D])
        masked = sb("masked", [P, NT, S], U8)
        st = sb("st", [P, 4, 6])
        mv = sb("mv", [P, 4, 2])
        agg = sb("agg", [P, 5, 4])
        veps = sb("veps", [P, 4])
        rstd = sb("rstd", [P, 4])
        neghalf = sb("neghalf", [P, 4])
        e_base = sb("e_base", [P, TPG * 8])
        mx = sb("mx", [P, TPG, 16])
        sm = sb("sm", [P, TPG, 16])
        rv = sb("rv", [P, TPG, 16])
        route = sb("route", [P, 8, TPG * 8])
        cmp_gt = sb("cmp_gt", [P, TPG, 8, 8])
        cmp_eq = sb("cmp_eq", [P, TPG, 8, 8])
        comb = sb("comb", [P, 2, TPG, 8])
        combT = sb("combT", [8, 2, GT])
        rms_gain = sb("rms_gain", [P, 1])
        onemu = sb("onemu", [P, 2])

        def w(name):
            a, b = SMALL_AT[name]
            return small[:, a:b]

        filled = [ctx.enter_context(nc.semaphore(f"filled{b}")) for b in range(8)]
        drained = [ctx.enter_context(nc.semaphore(f"drained{b}")) for b in range(8)]
        att = dict(l0x=2, l0f=2, l1x=2, l2x=2, l3x=2)
        all2 = dict(att, l1f=2, l2f=2, l3f=2)
        s_stats = step("s_stats", **dict(all2, l2x=4))
        s_aggr = step("s_aggr", **{k: 7 for k in all2})
        s_veps = step("s_veps", **dict({k: 1 for k in all2}, l2x=3))
        s_rstd = step("s_rstd", **{k: 1 for k in all2})
        s_xn = step("s_xn", **dict(all2, l2x=4))
        s_ctx = dma_step("s_ctx", l0x=16, l1x=16, l2x=16, l3x=16)
        s_kspread = dma_step("s_kspread", l0f=256, l1x=256)
        s_rope = step("s_rope", l2x=4)
        s_mx = step("s_mx", **att)
        s_masked = step("s_masked", l1x=2, l2x=2)
        s_sub = step("s_sub", l1x=2, l2x=2)
        s_exp = step("s_exp", **att)
        s_sum = step("s_sum", **att)
        s_rv = step("s_rv", **att)
        s_probs = step("s_probs", **att)
        s_route = step("s_route", l0f=9, l1f=12, l2f=7)
        s_rexp = step("s_rexp", l0f=1, l1f=1, l2f=1)
        s_acc = step("s_acc", l0f=12)
        s_tmp = step("s_tmp", l1x=2, l3f=2)
        s_act = step("s_act", l1f=24)
        s_mix = step("s_mix", l3f=6)
        s_relu = step("s_relu", l3f=1)
        s_upd = step("s_upd", l0f=2, l1x=2, l1f=1, l2f=1, l3f=1)
        s_rank = step("s_rank", l0f=1, l1f=1, l2f=1)
        s_small = ctx.enter_context(nc.semaphore("s_small"))
        s_x = ctx.enter_context(nc.semaphore("s_x"))
        s_m1 = ctx.enter_context(nc.semaphore("s_m1"))
        s_m2 = ctx.enter_context(nc.semaphore("s_m2"))
        s_w1 = ctx.enter_context(nc.semaphore("s_w1"))
        s_late = ctx.enter_context(nc.semaphore("s_late"))
        s_w2 = ctx.enter_context(nc.semaphore("s_w2"))
        s_const = ctx.enter_context(nc.semaphore("s_const"))
        s_zero = ctx.enter_context(nc.semaphore("s_zero"))
        s_tanh = ctx.enter_context(nc.semaphore("s_tanh"))
        s_mask = ctx.enter_context(nc.semaphore("s_mask"))
        s_onemu = ctx.enter_context(nc.semaphore("s_onemu"))
        s_scale = ctx.enter_context(nc.semaphore("s_scale"))
        s_out = ctx.enter_context(nc.semaphore("s_out"))
        steps = [s_stats, s_aggr, s_veps, s_rstd, s_xn, s_rope, s_mx, s_masked, s_sub,
                 s_exp, s_sum, s_rv, s_probs, s_route, s_rexp, s_acc, s_tmp, s_act, s_mix, s_relu, s_upd, s_rank]

        ident = w("ident")

        def k_pairs(layer, par):
            arena = arena_b[:, par * 4096:(par + 1) * 4096]
            return arena.rearrange("p (c b k) -> p c b k", b=BPG, k=P)

        def v_pairs(layer, par):
            arena = arena_a[:, par * 4096:(par + 1) * 4096]
            return arena.rearrange("p (b c k) -> p b c k", b=BPG, k=P)

        def k_spread(par):
            return arena_a[:, par * 4096:(par + 1) * 4096].rearrange("p (h t) -> p h t", h=16)

        def k_rope(par):
            return arena_b[:, par * 1024:(par + 1) * 1024].rearrange("p (b n) -> p b n", b=BPG)

        def v_small(par):
            return vsmall[:, par, :].rearrange("p (b c e) -> p b c e", b=BPG, e=16)

        def v_rope(par):
            return vsmall[:, par, 0:BPG * 64].rearrange("p (b e) -> p b e", b=BPG)

        def w1_expert(e):
            return w("l1f_shared") if e == 0 else w1_sb[:, (e - 1) * EXPERT1:e * EXPERT1]

        w1_sb = arena_b
        w2_sb = arena_a

        def mask_staged(i):
            return (pT, oT)[i][:, :, :, :].rearrange("p a c t -> p (a c t)").rearrange("p (n k) -> p n k", k=S)

        def silu_buf(k):
            return kT[:, k % 2, :]

        def bank(b, n=512):
            return ps[:, b, 0:n]

        def score_bank(b):
            return ps[:, b:b + 2, :].rearrange("p a n -> p (a n)")

        def traverse(eng, do, start=None):
            for layer in layers:
                if start:
                    start(layer)

                def iteration(at, whole=False):
                    for item, lag in layer.order:
                        g = at.ahead(lag)
                        if whole or 0 <= g.pair < PAIRS:
                            do(layer, item, g)

                for i in (-2, -1, 0):
                    iteration(Group(layer, 0, 0).ahead(i))
                with eng.Fori(0, PAIRS - 2) as pair:
                    iteration(Group(layer, pair, 1), whole=True)
                    iteration(Group(layer, pair + 1, 0), whole=True)
                for i in range(NG - 3, NG + 1):
                    iteration(Group(layer, 0, 0).ahead(i))

        block = ctx.enter_context(nc.Block())

        @block.sync
        def _(sp):
            for s in filled + drained:
                sp.sem_inc(s, CREDIT)
            for s in steps:
                sp.sem_inc(s.sem, s.credit)
            for s in (s_ctx, s_kspread):
                for i in range(2):
                    sp.sem_inc(s.sems[i], s.credit)
            sp.dma_start(small[:, :], small_in).then_inc(s_small, 16)
            x_v = x_in.rearrange("b s d -> (b s) d").rearrange("(n p) d -> p n d", p=P)
            for c in range(4):
                n = NT // 4
                sp.dma_start(x_sb[:, c * n:(c + 1) * n, :], x_v[:, c * n:(c + 1) * n, :]).then_inc(s_x, 16)
            ctx_v = ctx_in.rearrange("b s d -> (b s) d").rearrange("(n p) d -> p n d", p=P)
            out_v = out.rearrange("b s d -> (b s) d").rearrange("(n p) d -> p n d", p=P)

            def load_mask(dst, src, sem, n0, n1):
                src_v = src.rearrange("(n b) k -> b n k", b=2)
                for b in range(2):
                    sp.dma_start(dst[b * S:(b + 1) * S, :, :],
                                 src_v[b, n0:n1, :].partition_broadcast(S)).then_inc(sem, 16)

            def start(layer):
                if layer is L0X:
                    load_mask(mask_staged(0), mask1_in, s_m1, 0, NT // 2)
                    load_mask(mask_staged(1), mask1_in, s_m1, NT // 2, NT)
                if layer is L0F:
                    sp.wait_ge(s_zero, 1)
                    for b in L0X.body_banks:
                        sp.wait_ge(drained[b], bank_base[1][b])
                    sp.dma_start(w1_sb[:, 0:E_FF1 * EXPERT1], w1_in).then_inc(s_w1, 16)
                if layer is L1X:
                    for b in L0F.body_banks:
                        sp.wait_ge(drained[b], bank_base[2][b])
                    sp.dma_start(small[:, 0:1024 * len(LATE)], late_in).then_inc(s_late, 16)
                if layer is L1F:
                    for b in L1X.body_banks:
                        sp.wait_ge(drained[b], bank_base[3][b])
                    sp.dma_start(w2_sb[:, :], w2_in).then_inc(s_w2, 16)
                    load_mask(masked, mask2_in, s_m2, 0, NT)

            def do(layer, item, g):
                if item == ("L", 0) and layer.cross:
                    if layer is L2X:
                        sp.wait_ge(s_xn.sem, s_xn.after(g.back(2), 3))
                        sp.dma_start(ctx_sb[:, g.par, :, :],
                                     ctx_v[:, bass.ds(g.tile(0), TPG), :]).then_inc(s_ctx.sem(g), 16)
                    else:
                        u = len(layer.front) - 1
                        back = g.back(2)
                        sp.wait_ge(drained[layer.front_ring.bank(back, u)], layer.front_ring.count(back, u))
                        sp.dma_start(xcT[:, g.par, GT:2 * GT],
                                     ctxT_in[:, bass.ds(g.tile(0) * P, GT)]).then_inc(s_ctx.sem(g), 16)
                if item == ("QK", 0):
                    sp.wait_ge(drained[layer.front_ring.bank(g, 1)], layer.front_ring.count(g, 1))
                    for h in range(16):
                        sp.dma_start(k_spread(g.par)[8 * h:8 * h + 8, h, :],
                                     kT[8 * h:8 * h + 8, g.par, :]).then_inc(s_kspread.sem(g), 16)
                if item == ("VF", 0):
                    sp.wait_ge(s_upd.sem, s_upd.after(g, 0))
                    sp.dma_start(out_v[:, bass.ds(g.tile(0), TPG), :],
                                 x_sb[:, bass.ds(g.tile(0), TPG), :]).then_inc(s_out, 16)

            traverse(sp, do, start)
            sp.wait_ge(s_out, 16 * NG)

        @block.gpsimd
        def _(pool):
            pool.memset(neghalf[:, :], -0.5).then_inc(s_const, 1)
            pool.memset(e_base[:, :], E_F32).then_inc(s_const, 1)
            pool.memset(arena_b[:, :], 0.0).then_inc(s_const, 1)
            pool.memset(arena_a[:, :], 0.0).then_inc(s_const, 1)
            pool.memset(vsmall[:, :, :], 0.0).then_inc(s_const, 1)
            pool.wait_ge(s_const, 5)

            def start(layer):
                if layer is L0F:
                    for b in L0X.body_banks:
                        pool.wait_ge(drained[b], bank_base[1][b])
                    pool.memset(arena_a[:, :], 0.0).then_inc(s_zero, 1)
                if layer is L2X:
                    for b in L1F.body_banks:
                        pool.wait_ge(drained[b], bank_base[4][b])
                    pool.memset(arena_b[:, :], 0.0).then_inc(s_zero, 1)
                    pool.memset(vsmall[:, :, :], 0.0).then_inc(s_zero, 1)
                if layer is L2F:
                    for b in L2X.body_banks:
                        pool.wait_ge(drained[b], bank_base[5][b])
                    pool.memset(arena_b[:, :], 0.0).then_inc(s_zero, 1)
                if layer is L3X:
                    for b in L2F.body_banks:
                        pool.wait_ge(drained[b], bank_base[6][b])
                    pool.memset(arena_a[:, :], 0.0).then_inc(s_zero, 1)

            def do(layer, item, g):
                if item == ("L", 0):
                    n = 4 if layer is L2X else 2
                    last = 2 if layer is L2X else 0
                    pool.wait_ge(s_veps.sem, s_veps.after(g, last))
                    pool.wait_ge(s_xn.sem, s_xn.after(g.back(1), n - 1))
                    pool.tensor_tensor(rstd[:, 0:n], veps[:, 0:n], neghalf[:, 0:n],
                                       ALU.pow).then_inc(s_rstd.sem, 1)
                if item == ("G", 0):
                    n = TPG * layer.experts
                    pool.wait_ge(s_route.sem, s_route.after(g, 0 if layer is L2F else 1))
                    pool.tensor_tensor(route[:, 1, 0:n], e_base[:, 0:n], route[:, 0, 0:n],
                                       ALU.pow).then_inc(s_rexp.sem, 1)
                if item[0] == "N":
                    t, nh = item[1], layer.heads
                    pool.wait_ge(s_rv.sem, s_rv.after(g, t))
                    pr = probs[:, g.par, t, 0:nh * S].rearrange("p (h k) -> p h k", k=S)
                    pool.tensor_tensor(pr, pr, rv[:, t, 0:nh].unsqueeze(2).to_broadcast([P, nh, S]),
                                       ALU.mult).then_inc(s_probs.sem, 1)

            traverse(pool, do, start)

        @block.tensor
        def _(pe):
            def take(ring, g, u):
                b = ring.bank(g, u)
                pe.wait_ge(drained[b], ring.count(g, u) - 1)
                return b

            def wait_drained(ring, g, u):
                pe.wait_ge(drained[ring.bank(g, u)], ring.count(g, u))

            def last_uses(layer, kinds):
                return [v for v, item in enumerate(layer.front) if item[0] in kinds][-2:]

            def mm(o, lhsT, rhs, start=True, stop=True):
                return nc.tensor.matmul(o, lhsT, rhs, start=start, stop=stop, skip_group_check=True)

            def start(layer):
                if layer is L0X:
                    pe.wait_ge(s_small, 16)
                    pe.wait_ge(s_const, 5)
                if layer is L1F:
                    pe.wait_ge(s_w1, 16)
                if layer is L2F:
                    pe.wait_ge(s_w2, 16)
                if layer is L3X:
                    pe.wait_ge(s_late, 16)

            def front(layer, item, g):
                ring = layer.front_ring
                u = layer.use(item)
                kind, j = item
                xT = xcT[:, g.par, 0:GT]
                cT = xcT[:, g.par, GT:2 * GT]
                if u == 1:
                    wait_drained(ring, g, 0)
                if kind == "E":
                    for i in range(2):
                        b = take(ring, g, u + i)
                        mm(bank(b), xT[:, j * P:(j + 1) * P],
                           w("l0f_we")[:, i * 512:(i + 1) * 512]).then_inc(filled[b], 1)
                    return
                b = take(ring, g, u)
                o = bank(b)
                if kind == "F":
                    for t in range(TPG):
                        pe.wait_ge(s_xn.sem, s_xn.after(g, t))
                        last = nc.tensor.transpose(o[:, t * P:(t + 1) * P], xn[:, g.par, t, :], ident)
                    if layer is L2X:
                        for t in range(TPG):
                            pe.wait_ge(s_xn.sem, s_xn.after(g, 2 + t))
                            last = nc.tensor.transpose(o[:, GT + t * P:GT + (t + 1) * P], ctxn[:, g.par, t, :], ident)
                    last.then_inc(filled[b], 1)
                    return
                if layer.cross and layer is not L2X and kind in ("QK", "K", "V"):
                    pe.wait_ge(s_ctx.sem(g), s_ctx.all(g))
                if kind == "Q" and layer is not L2X:
                    for i in range(2):
                        c = 2 * j + i
                        last = mm(o[:, i * GT:(i + 1) * GT], w(layer.name + "_wq")[:, c * P:(c + 1) * P], xT)
                elif kind == "K" and layer is not L2X:
                    for i in range(2):
                        c = 2 * j + i
                        last = mm(o[:, i * GT:(i + 1) * GT], w(layer.name + "_wk")[:, c * P:(c + 1) * P], cT)
                elif kind == "Q" or kind == "K":
                    ww = w("l2x_wq") if kind == "Q" else w("l2x_wk")
                    for i in range(2):
                        last = mm(o[:, i * GT:(i + 1) * GT], ww[:, i * P:(i + 1) * P], xT if kind == "Q" else cT)
                elif kind == "QK":
                    mm(o[:, 0:GT], w(layer.name + "_wq"), xT)
                    last = mm(o[:, GT:2 * GT], w(layer.name + "_wk"), cT if layer.cross else xT)
                elif kind == "V":
                    src = cT if layer.cross else xT
                    wv = w(layer.name + "_wv")
                    seqs = [j] if layer is L3X else range(BPG)
                    n = {"l3x": 512, "l0x": 128, "l0f": 64, "l1x": 64, "l2x": 32}[layer.name]
                    for i, q in enumerate(seqs):
                        for half in range(2):
                            ww = wv if layer is L2X else wv[:, half * n:(half + 1) * n]
                            last = mm(o[half * S:(half + 1) * S, i * n:(i + 1) * n],
                                      src[:, q * S:(q + 1) * S], ww)
                elif kind == "G":
                    ne = layer.experts
                    for t in range(TPG):
                        last = mm(o[:, t * ne:(t + 1) * ne], xT[:, t * P:(t + 1) * P], w(layer.name + "_wg"))
                elif kind == "C":
                    pe.wait_ge(s_route.sem, s_route.after(g, 8))
                    for t in range(TPG):
                        last = nc.tensor.transpose(o[0:8, t * P:(t + 1) * P], comb[:, g.par, t, :], ident)
                elif kind == "Z":
                    wait_drained(ring, g, layer.use(("C", 0)))
                    last = mm(o[:, 0:D], combT[0:8, g.par, j * P:(j + 1) * P], w("l0f_be")[0:8, :])
                last.then_inc(filled[b], 1)

            def do(layer, item, g):
                ring, fr = layer.body_ring, layer.front_ring
                kind = item[0]
                if kind in ("L", "M", "H", "N"):
                    return
                if item in layer.front:
                    front(layer, item, g)
                    return
                u = layer.use(item) if kind != "S" else None
                xT = xcT[:, g.par, 0:GT]
                if kind == "S":
                    t = item[1]
                    b = take(layer.score_ring, g, t)
                    o = score_bank(b)
                    if t == 0:
                        for v in last_uses(layer, ("Q", "K", "QK")):
                            wait_drained(fr, g, v)
                        if layer in (L0F, L1X):
                            pe.wait_ge(s_kspread.sem(g), s_kspread.all(g))
                    for hb in range(2):
                        if layer in (L0F, L1X):
                            for half in range(2):
                                last = mm(o[hb * S:(hb + 1) * S, half * 512:(half + 1) * 512],
                                          qT[:, g.par, 0, t * P + hb * S:t * P + (hb + 1) * S],
                                          k_spread(g.par)[:, 8 * half:8 * half + 8,
                                                          t * P + hb * S:t * P + (hb + 1) * S])
                        if layer is L2X:
                            last = mm(o[hb * S:(hb + 1) * S, 0:4 * S],
                                      qT[:, g.par, 0, t * P + hb * S:t * P + (hb + 1) * S],
                                      k_rope(g.par)[:, 2 * t + hb, :])
                    if layer in (L0X, L3X):
                        for c in range(8):
                            for hb in range(2):
                                last = mm(o[hb * S:(hb + 1) * S, c * P:(c + 1) * P],
                                          qT[:, g.par, c, t * P + hb * S:t * P + (hb + 1) * S],
                                          k_pairs(layer, g.par)[:, c // 4 if layer is L0X else c, 2 * t + hb, :])
                    last.then_inc(filled[b], 1)
                elif kind == "T":
                    t = item[1]
                    pe.wait_ge(s_probs.sem, s_probs.after(g, t))
                    nchunk = layer.heads * S // P
                    for j in range(layer.uses["T"]):
                        b = take(ring, g, u + j)
                        for i in range(min(4, nchunk)):
                            c = 4 * j + i
                            last = nc.tensor.transpose(bank(b)[:, i * P:(i + 1) * P],
                                                       probs[:, g.par, t, c * P:(c + 1) * P], ident)
                        last.then_inc(filled[b], 1)
                elif kind == "A":
                    t = item[1]
                    ut = layer.use(("T", t))
                    if t == 0:
                        for v in last_uses(layer, ("V",)):
                            wait_drained(fr, g, v)
                    for j in range(layer.uses["A"]):
                        b = take(ring, g, u + j)
                        o = bank(b)
                        for v in range(layer.uses["T"]):
                            if v == j or layer.uses["A"] == 1:
                                wait_drained(ring, g, ut + v)
                        if layer is L0X:
                            for hb in range(2):
                                last = mm(o[:, hb * 256:(hb + 1) * 256], v_pairs(layer, g.par)[:, 2 * t + hb, j, :],
                                          pT[:, t, 4 * j:4 * j + 4, hb * S:(hb + 1) * S])
                        elif layer is L3X:
                            for i in range(4):
                                for hb in range(2):
                                    last = mm(o[:, i * P + hb * S:i * P + (hb + 1) * S],
                                              v_pairs(layer, g.par)[:, 2 * t + hb, 4 * j + i, :],
                                              pT[:, t, 4 * j + i, hb * S:(hb + 1) * S])
                        elif layer is L2X:
                            for c in range(2):
                                last = mm(o[:, c * P:(c + 1) * P], pT[:, t, c, :],
                                          v_rope(g.par)[:, 2 * t:2 * t + 2, :])
                        else:
                            for c in range(8):
                                last = mm(o[:, c * 32:(c + 1) * 32], pT[:, t, c, :],
                                          v_small(g.par)[:, 2 * t:2 * t + 2, c, :])
                        last.then_inc(filled[b], 1)
                elif kind == "X":
                    t = item[1]
                    wait_drained(ring, g, layer.use(("A", t)))
                    b = take(ring, g, u)
                    nc.tensor.transpose(bank(b)[:, 0:P], o_sb[:, t, :], ident).then_inc(filled[b], 1)
                elif kind == "W":
                    t = item[1]
                    chunks = 8 if layer in (L0X, L3X) else 1
                    if chunks == 8:
                        for v in range(layer.uses["A"]):
                            wait_drained(ring, g, layer.use(("A", t)) + v)
                    else:
                        wait_drained(ring, g, layer.use(("X", t)))
                    b = take(ring, g, u)
                    for c in range(chunks):
                        last = mm(bank(b)[:, 0:D], oT[:, t, c, :], w(layer.name + "_wo")[:, c * D:(c + 1) * D],
                                  start=c == 0, stop=c == chunks - 1)
                    last.then_inc(filled[b], 1)
                elif kind == "U" and layer is L1F:
                    e, c = item[1:]
                    r0, n = HID1[c]
                    if item == ("U", 0, 0):
                        wait_drained(fr, g, 0)
                    b = take(ring, g, u)
                    mm(bank(b)[0:n, 0:GT], w1_expert(e)[:, r0:r0 + n], xT)
                    mm(bank(b)[0:n, GT:2 * GT], w1_expert(e)[:, I_FF + r0:I_FF + r0 + n], xT)\
                        .then_inc(filled[b], 1)
                elif kind == "U":
                    e, c = item[1:]
                    if item == ("U", 0, 0):
                        wait_drained(fr, g, 0)
                    b = take(ring, g, u)
                    for i in range(2):
                        a = e * EXPERT2 + (2 * c + i) * P
                        last = mm(bank(b)[:, i * GT:(i + 1) * GT], w2_sb[:, a:a + P], xT)
                    last.then_inc(filled[b], 1)
                elif kind == "D":
                    e = item[1]
                    nch = 3 if layer is L1F else 4
                    for c in range(nch if layer is L1F else 2):
                        wait_drained(ring, g, layer.use(("U", e, c)))
                    b = take(ring, g, u)
                    for t in range(TPG):
                        for c in range(nch):
                            if layer is L1F:
                                n = HID1[c][1]
                                a = 2 * I_FF + c * D
                                rhs = w1_expert(e)[0:n, a:a + D]
                            else:
                                n = P
                                a = e * EXPERT2 + FFN2 + c * D
                                rhs = w2_sb[:, a:a + D]
                            last = mm(bank(b)[:, t * D:(t + 1) * D],
                                      qT[0:n, e % 2, c, t * P:(t + 1) * P], rhs, start=c == 0, stop=c == nch - 1)
                    last.then_inc(filled[b], 1)
                elif kind == "KF":
                    pe.wait_ge(s_mix.sem, s_mix.after(g, 5))
                    b = take(ring, g, u)
                    mm(bank(b)[:, 0:GT], w("l3f_wk"), qT[:, g.par, 1, :]).then_inc(filled[b], 1)
                elif kind == "RF":
                    b = take(ring, g, u)
                    for t in range(TPG):
                        last = mm(bank(b)[:, t * D:(t + 1) * D], qT[:, g.par, 0, t * P:(t + 1) * P], w("l3f_wr"))
                    last.then_inc(filled[b], 1)
                elif kind == "VF":
                    pe.wait_ge(s_relu.sem, s_relu.after(g, 0))
                    b = take(ring, g, u)
                    for t in range(TPG):
                        last = mm(bank(b)[:, t * D:(t + 1) * D], qT[:, g.par, 3, t * P:(t + 1) * P], w("l3f_wv"))
                    last.then_inc(filled[b], 1)

            traverse(pe, do, start)

        @block.scalar
        def _(act):
            def wait_filled(ring, g, u):
                b = ring.bank(g, u)
                act.wait_ge(filled[b], ring.count(g, u))
                return b

            def wait_drained(ring, g, u):
                act.wait_ge(drained[ring.bank(g, u)], ring.count(g, u))

            def start(layer):
                if layer is L0X:
                    act.wait_ge(s_small, 16)
                    act.wait_ge(s_const, 5)
                    nc.scalar.activation(tgate[:, :], w("gates"), ACT.Tanh).then_inc(s_tanh, 1)
                    act.wait_ge(s_mask, 2)
                if layer is L2X:
                    act.wait_ge(s_scale, 1)
                    act.wait_ge(s_zero, 3)
                if layer is L0F:
                    act.wait_ge(s_zero, 1)
                if layer is L3X:
                    act.wait_ge(s_zero, 5)

            def do(layer, item, g):
                ring, fr = layer.body_ring, layer.front_ring
                kind = item[0]
                if kind in ("L", "M", "H", "N"):
                    return
                u = layer.use(item) if kind != "S" else None
                if kind == "F":
                    b = wait_filled(fr, g, u)
                    if layer is L2X:
                        nc.scalar.activation(xcT[:, g.par, :], bank(b), ACT.Identity,
                                             scale=rms_gain[:, 0:1]).then_inc(drained[b], 1)
                    else:
                        nc.scalar.activation(xcT[:, g.par, 0:GT], bank(b, GT), ACT.Copy).then_inc(drained[b], 1)
                elif kind == "Q" and layer is not L2X:
                    b = wait_filled(fr, g, u)
                    j = item[1]
                    nc.scalar.activation(qT[:, g.par, 2 * j:2 * j + 2, :].rearrange("p c t -> p (c t)"), bank(b),
                                         ACT.Copy).then_inc(drained[b], 1)
                elif kind == "QK":
                    b = wait_filled(fr, g, u)
                    act.wait_ge(s_kspread.sem(g.back(2)), s_kspread.all(g.back(2)))
                    nc.scalar.activation(qT[:, g.par, 0, :], bank(b, GT), ACT.Identity,
                                         bias=w(layer.name + "_bq"))
                    nc.scalar.activation(kT[:, g.par, :], bank(b)[:, GT:2 * GT], ACT.Identity,
                                         bias=w(layer.name + "_bk")).then_inc(drained[b], 1)
                elif kind == "V" and layer in (L0X, L3X):
                    b = wait_filled(fr, g, u)
                    j = item[1]
                    for half in range(2):
                        rows = slice(half * S, (half + 1) * S)
                        if layer is L3X:
                            o = v_pairs(layer, g.par)[rows, j, :, half * S:(half + 1) * S]
                            i = bank(b)[rows, :].rearrange("p (c k) -> p c k", k=S)
                        else:
                            o = v_pairs(layer, g.par)[rows, :, 0:2, half * S:(half + 1) * S]
                            i = bank(b)[rows, :].rearrange("p (q c k) -> p q c k", c=2, k=S)
                        last = nc.scalar.activation(o, i, ACT.Copy)
                    last.then_inc(drained[b], 1)
                elif kind == "V" and layer is L2X:
                    b = wait_filled(fr, g, u)
                    for half in range(2):
                        rows = slice(half * S, (half + 1) * S)
                        last = nc.scalar.activation(v_rope(g.par)[rows, :, half * 32:(half + 1) * 32],
                                                    bank(b)[rows, 0:BPG * 32].rearrange("p (q d) -> p q d", d=32),
                                                    ACT.Copy)
                    last.then_inc(drained[b], 1)
                elif kind == "C":
                    b = wait_filled(fr, g, u)
                    nc.scalar.activation(combT[:, g.par, :], bank(b, GT)[0:8, :], ACT.Copy).then_inc(drained[b], 1)
                elif kind == "S":
                    t = item[1]
                    if layer in (L1X, L2X):
                        act.wait_ge(s_sub.sem, s_sub.after(g, t))
                    else:
                        wait_drained(layer.score_ring, g, t)
                    pr = probs[:, g.par, t, 0:layer.heads * S]
                    nc.scalar.activation(pr, pr, ACT.Exp, scale=layer.scale).then_inc(s_exp.sem, 1)
                elif kind == "T":
                    t = item[1]
                    for j in range(layer.uses["T"]):
                        b = wait_filled(ring, g, u + j)
                        n = min(4, layer.heads * S // P)
                        nc.scalar.activation(pT[:, t, 4 * j:4 * j + n, :].rearrange("p c t -> p (c t)"),
                                             bank(b, n * P), ACT.Copy).then_inc(drained[b], 1)
                elif kind == "A" and layer in (L0X, L3X):
                    t = item[1]
                    for j in range(2):
                        b = wait_filled(ring, g, u + j)
                        if layer is L0X:
                            o = oT[:, t, 4 * j:4 * j + 4, :].rearrange("p i (b q) -> p b i q", b=2)
                            i = bank(b).rearrange("p (b i q) -> p b i q", b=2, i=4)
                        else:
                            o = oT[:, t, 4 * j:4 * j + 4, :].rearrange("p c t -> p (c t)")
                            i = bank(b)
                        nc.scalar.activation(o, i, ACT.Copy).then_inc(drained[b], 1)
                elif kind == "X":
                    t = item[1]
                    b = wait_filled(ring, g, u)
                    nc.scalar.activation(oT[:, t, 0, :], bank(b, P), ACT.Copy).then_inc(drained[b], 1)
                elif kind == "U" and layer is L1F:
                    e, c = item[1:]
                    n = HID1[c][1]
                    b = wait_filled(ring, g, u)
                    k = 3 * e + c
                    before = up_stages[k - 2]
                    gb = g if k >= 2 else g.back(1)
                    wait_drained(ring, gb, layer.use(before))
                    nc.scalar.activation(silu_buf(k)[0:n, :], bank(b)[0:n, 0:GT], ACT.Silu).then_inc(s_act.sem, 1)
                elif kind == "U":
                    e, c = item[1:]
                    b = wait_filled(ring, g, u)
                    nc.scalar.activation(qT[:, e % 2, 2 * c:2 * c + 2, :].rearrange("p c t -> p (c t)"), bank(b),
                                         ACT.Gelu).then_inc(drained[b], 1)
                elif kind == "RF":
                    b = wait_filled(ring, g, u)
                    act.wait_ge(s_upd.sem, s_upd.after(g.back(2), 0))
                    nc.scalar.activation(acc[:, g.par, :, :].rearrange("p t d -> p (t d)"), bank(b, GT),
                                         ACT.Sigmoid).then_inc(drained[b], 1)

            up_stages = [i for i, _ in L1F.order if i[0] == "U"]
            traverse(act, do, start)

        @block.vector
        def _(dve):
            def wait_filled(ring, g, u):
                b = ring.bank(g, u)
                dve.wait_ge(filled[b], ring.count(g, u))
                return b

            def xt(g, t):
                return x_sb[:, bass.ds(g.tile(t), 1), :].rearrange("p a d -> p (a d)")

            def start(layer):
                if layer is not L0X:
                    dve.wait_ge(s_upd.sem, s_upd.base[layer.n])
                    for b in layers[layer.n - 1].body_banks:
                        dve.wait_ge(drained[b], bank_base[layer.n][b])
                if layer is L0X:
                    dve.wait_ge(s_x, 64)
                    dve.wait_ge(s_small, 16)
                    dve.wait_ge(s_const, 5)
                    dve.wait_ge(s_tanh, 1)
                    dve.wait_ge(s_m1, 64)
                    for i in range(2):
                        dve.tensor_scalar(masked[:, i * NT // 2:(i + 1) * NT // 2, :], mask_staged(i), 1.0, None,
                                          ALU.not_equal).then_inc(s_mask, 1)
                    dve.wait_ge(s_mask, 2)
                    dve.tensor_scalar(rms_gain[:, :], w("l2x_scale"), 1.0, None, ALU.add).then_inc(s_scale, 1)
                if layer is L0F:
                    dve.wait_ge(s_zero, 1)
                if layer is L2X:
                    dve.wait_ge(s_m2, 32)
                    dve.wait_ge(s_zero, 3)
                    dve.tensor_scalar(masked[:, :, :], masked[:, :, :], 0.0, None, ALU.is_equal).then_inc(s_mask, 1)
                    dve.wait_ge(s_mask, 3)
                if layer is L3X:
                    dve.wait_ge(s_zero, 5)

            def statistics(layer, g):
                rms = layer is L2X
                dve.wait_ge(s_xn.sem, s_xn.after(g.back(1), 3 if rms else 1))
                if rms:
                    dve.wait_ge(s_ctx.sem(g), s_ctx.all(g))
                for t in range(TPG):
                    dve.bn_stats(st[:, t, :], xt(g, t)).then_inc(s_stats.sem, 1)
                if rms:
                    for t in range(TPG):
                        dve.bn_stats(st[:, 2 + t, :], ctx_sb[:, g.par, t, :]).then_inc(s_stats.sem, 1)
                n = 4 if rms else 2
                me, mo, ve, vo = (st[:, 0:n, i] for i in (1, 4, 2, 5))
                total, diff, within = (agg[:, i, 0:n] for i in range(3))
                dve.wait_ge(s_stats.sem, s_stats.after(g, n - 1))
                dve.tensor_tensor(total, me, mo, ALU.add).then_inc(s_aggr.sem, 1)
                dve.tensor_tensor(diff, me, mo, ALU.subtract).then_inc(s_aggr.sem, 1)
                dve.tensor_tensor(within, ve, vo, ALU.add).then_inc(s_aggr.sem, 1)
                dve.wait_ge(s_aggr.sem, s_aggr.after(g, 1))
                dve.tensor_tensor(agg[:, 3, 0:n], diff, diff, ALU.mult).then_inc(s_aggr.sem, 1)
                dve.tensor_scalar(mv[:, 0:n, 0], total, 0.5, None, ALU.mult).then_inc(s_aggr.sem, 1)
                dve.wait_ge(s_aggr.sem, s_aggr.after(g, 3))
                dve.scalar_tensor_tensor(out=agg[:, 4, 0:n], in0=agg[:, 3, 0:n], scalar=D / 4, in1=within,
                                         op0=ALU.mult, op1=ALU.add).then_inc(s_aggr.sem, 1)
                dve.wait_ge(s_aggr.sem, s_aggr.after(g, 5))
                dve.tensor_scalar(mv[:, 0:n, 1], agg[:, 4, 0:n], 1.0 / D, None, ALU.mult).then_inc(s_aggr.sem, 1)
                dve.wait_ge(s_aggr.sem, s_aggr.after(g, 6))
                if rms:
                    dve.tensor_scalar(veps[:, 0:2], mv[:, 0:2, 1], 1.0 + RMS_EPS, RMS_EPS * LN_EPS,
                                      ALU.mult, ALU.add).then_inc(s_veps.sem, 1)
                    dve.tensor_tensor(veps[:, 2:4], mv[:, 2:4, 0], mv[:, 2:4, 0], ALU.mult).then_inc(s_veps.sem, 1)
                    dve.wait_ge(s_veps.sem, s_veps.after(g, 1))
                    dve.scalar_tensor_tensor(out=veps[:, 2:4], in0=mv[:, 2:4, 1], scalar=RMS_EPS,
                                             in1=veps[:, 2:4], op0=ALU.add, op1=ALU.add).then_inc(s_veps.sem, 1)
                else:
                    dve.tensor_scalar(veps[:, 0:2], mv[:, 0:2, 1], LN_EPS, None, ALU.add).then_inc(s_veps.sem, 1)

            def normalise(layer, g):
                dve.wait_ge(s_rstd.sem, s_rstd.after(g, 0))
                wait_drained(layer.front_ring, g.back(2), 0)
                for t in range(TPG):
                    dve.tensor_scalar(xn[:, g.par, t, :], xt(g, t), mv[:, t, 0:1], rstd[:, t:t + 1],
                                      ALU.subtract, ALU.mult).then_inc(s_xn.sem, 1)
                if layer is L2X:
                    for t in range(TPG):
                        dve.tensor_scalar(ctxn[:, g.par, t, :], ctx_sb[:, g.par, t, :], rstd[:, 2 + t:3 + t], None,
                                          ALU.mult).then_inc(s_xn.sem, 1)

            def wait_drained(ring, g, u):
                dve.wait_ge(drained[ring.bank(g, u)], ring.count(g, u))

            def routing(layer, g, b):
                ne = layer.experts
                n = TPG * ne
                r = lambda k: route[:, k, 0:n].rearrange("p (t e) -> p t e", e=ne)
                k = [0]

                def chain(ins):
                    ins.then_inc(s_route.sem, 1)
                    dve.wait_ge(s_route.sem, s_route.after(g, k[0]))
                    k[0] += 1

                bc = lambda ap: ap.unsqueeze(2).to_broadcast([P, TPG, ne])
                bg = w(layer.name + "_bg").unsqueeze(1).to_broadcast([P, TPG, ne])
                if b is not None:
                    dve.tensor_tensor(r(0), bank(b, n).rearrange("p (t e) -> p t e", e=ne), bg,
                                      ALU.add).then_inc(drained[b], 1)
                    wait_drained(layer.front_ring, g, layer.use(("G", 0)))
                    if layer is L2F:
                        chain(dve.tensor_scalar(r(0), r(0), -1.0, None, ALU.mult))
                    else:
                        chain(dve.tensor_reduce(route[:, 4, 0:TPG], r(0), AX_X, ALU.max))
                        chain(dve.tensor_tensor(r(0), r(0), bc(route[:, 4, 0:TPG]), ALU.subtract))
                    return
                k[0] = 1 if layer is L2F else 2
                if layer is L2F:
                    dve.wait_ge(s_rexp.sem, s_rexp.after(g, 0))
                    chain(dve.tensor_scalar(r(2), r(1), 1.0, None, ALU.add))
                    chain(dve.reciprocal(r(3), r(2)))
                else:
                    dve.wait_ge(s_rexp.sem, s_rexp.after(g, 0))
                    chain(dve.tensor_reduce(route[:, 4, 0:TPG], r(1), AX_X, ALU.add))
                    chain(dve.reciprocal(route[:, 5, 0:TPG], route[:, 4, 0:TPG]))
                    chain(dve.tensor_tensor(r(3), r(1), bc(route[:, 5, 0:TPG]), ALU.mult))
                gt = cmp_gt[:, :, 0:ne, 0:ne]
                eq = cmp_eq[:, :, 0:ne, 0:ne]
                other = r(3).unsqueeze(2).to_broadcast([P, TPG, ne, ne])
                own = r(3).unsqueeze(3).to_broadcast([P, TPG, ne, ne])
                tri = w("earlier").rearrange("p (e f) -> p e f", f=8)[:, 0:ne, 0:ne]
                dve.tensor_tensor(gt, other, own, ALU.is_gt)
                chain(dve.tensor_tensor(eq, other, own, ALU.is_equal))
                chain(dve.tensor_tensor(eq, eq, tri.unsqueeze(1).to_broadcast([P, TPG, ne, ne]), ALU.mult))
                chain(dve.tensor_tensor(gt, gt, eq, ALU.add))
                dve.tensor_reduce(r(6), gt, AX_X, ALU.add).then_inc(s_rank.sem, 1)
                dve.wait_ge(s_rank.sem, s_rank.after(g, 0))
                last = dve.scalar_tensor_tensor(out=comb[:, g.par, :, 0:ne], in0=r(6), scalar=float(layer.top),
                                                in1=r(3), op0=ALU.is_lt, op1=ALU.mult)
                if layer is L1F:
                    chain(last)
                    cw = comb[:, g.par, :, 0:ne]
                    chain(dve.tensor_reduce(route[:, 4, 0:TPG], cw, AX_X, ALU.add))
                    chain(dve.reciprocal(route[:, 5, 0:TPG], route[:, 4, 0:TPG]))
                    chain(dve.tensor_tensor(cw, cw, bc(route[:, 5, 0:TPG]), ALU.mult))
                else:
                    chain(last)
                assert k[0] == s_route.per[layer.name], (layer.name, k[0])

            def softmax(layer, g, t):
                nh = layer.heads
                b = wait_filled(layer.score_ring, g, t)
                sc = score_bank(b)[:, 0:nh * S].rearrange("p (h k) -> p h k", k=S)
                pr = probs[:, g.par, t, 0:nh * S].rearrange("p (h k) -> p h k", k=S)
                m = mx[:, t, 0:nh]
                mb = m.unsqueeze(2).to_broadcast([P, nh, S])
                back, ut = g.back(2), layer.use(("T", t))
                for v in range(layer.uses["T"]):
                    wait_drained(layer.body_ring, back, ut + v)
                if layer in (L1X, L2X):
                    fill = F32_MIN if layer is L1X else MASK_FILL
                    mk = masked[:, bass.ds(g.tile(t), 1), :].to_broadcast([P, nh, S])
                    dve.scalar_tensor_tensor(out=pr, in0=mk, scalar=fill, in1=sc,
                                             op0=ALU.mult, op1=ALU.add).then_inc(drained[b], 1)
                    wait_drained(layer.score_ring, g, t)
                    dve.tensor_reduce(m, pr, AX_X, ALU.max).then_inc(s_mx.sem, 1)
                    dve.wait_ge(s_mx.sem, s_mx.after(g, t))
                    dve.tensor_tensor(pr, pr, mb, ALU.subtract).then_inc(s_sub.sem, 1)
                else:
                    dve.tensor_reduce(m, sc, AX_X, ALU.max).then_inc(s_mx.sem, 1)
                    dve.wait_ge(s_mx.sem, s_mx.after(g, t))
                    dve.tensor_tensor(pr, sc, mb, ALU.subtract).then_inc(drained[b], 1)

            def softmax_sum(layer, g, t):
                nh = layer.heads
                pr = probs[:, g.par, t, 0:nh * S].rearrange("p (h k) -> p h k", k=S)
                dve.wait_ge(s_exp.sem, s_exp.after(g, t))
                dve.tensor_reduce(sm[:, t, 0:nh], pr, AX_X, ALU.add).then_inc(s_sum.sem, 1)
                dve.wait_ge(s_sum.sem, s_sum.after(g, t))
                dve.reciprocal(rv[:, t, 0:nh], sm[:, t, 0:nh]).then_inc(s_rv.sem, 1)

            def residual(layer, g, t, src, extra=None):
                return dve.scalar_tensor_tensor(out=xt(g, t), in0=src, scalar=tgate[:, layer.n:layer.n + 1],
                                                in1=xt(g, t), op0=ALU.mult, op1=ALU.add)

            def do(layer, item, g):
                ring, fr = layer.body_ring, layer.front_ring
                kind = item[0]
                u = layer.use(item) if kind not in ("L", "M", "H", "S", "N") else None
                if kind == "L":
                    statistics(layer, g)
                elif kind == "M":
                    normalise(layer, g)
                elif kind == "F" and layer is L3F:
                    mix(g)
                elif kind == "N":
                    softmax_sum(layer, g, item[1])
                elif kind == "H":
                    routing(layer, g, None)
                elif kind == "K" and layer is not L2X:
                    b = wait_filled(fr, g, u)
                    j = item[1]
                    for half in range(2):
                        rows = slice(half * S, (half + 1) * S)
                        last = dve.tensor_copy(k_pairs(layer, g.par)[rows, 2 * j:2 * j + 2, :, half * S:(half + 1) * S],
                                               bank(b)[rows, :].rearrange("p (c q k) -> p c q k", c=2, k=S))
                    last.then_inc(drained[b], 1)
                elif kind in ("Q", "K") and layer is L2X:
                    b = wait_filled(fr, g, u)
                    at = 0 if kind == "Q" else 2
                    tab = w("rope").rearrange("p (n s) -> p n s", s=S)
                    cos = tab[:, at, :].unsqueeze(1).to_broadcast([P, BPG, S])
                    sin = tab[:, at + 1, :].unsqueeze(1).to_broadcast([P, BPG, S])
                    v = lambda ap: ap.rearrange("p (b s) -> p b s", s=S)
                    n = 0 if kind == "Q" else 2
                    c1 = v(qT[:, g.par, n + 2, :])
                    c2 = v(qT[:, g.par, n + 3, :])
                    dve.tensor_tensor(c1, v(bank(b, GT)), cos, ALU.mult).then_inc(s_rope.sem, 1)
                    dve.tensor_tensor(c2, v(bank(b)[:, GT:2 * GT]), sin, ALU.mult).then_inc(s_rope.sem, 1)
                    dve.wait_ge(s_rope.sem, s_rope.after(g, n + 1))
                    if kind == "Q":
                        dve.tensor_tensor(v(qT[:, g.par, 0, :]), c1, c2, ALU.add).then_inc(drained[b], 1)
                    else:
                        for h in range(4):
                            r0 = 32 * h
                            last = dve.tensor_tensor(k_rope(g.par)[r0:r0 + 32, :, h * S:(h + 1) * S],
                                                     c1[r0:r0 + 32], c2[r0:r0 + 32], ALU.add)
                        last.then_inc(drained[b], 1)
                elif kind == "V" and layer in (L0F, L1X):
                    b = wait_filled(fr, g, u)
                    for half in range(2):
                        rows = slice(half * S, (half + 1) * S)
                        bv = w(layer.name + "_bv")[rows, :].rearrange("p (c d) -> p c d", d=8)
                        last = dve.tensor_tensor(v_small(g.par)[rows, :, :, half * 8:(half + 1) * 8],
                                                 bank(b)[rows, 0:BPG * 64].rearrange("p (q c d) -> p q c d", c=8, d=8),
                                                 bv.unsqueeze(1).to_broadcast([S, BPG, 8, 8]), ALU.add)
                    last.then_inc(drained[b], 1)
                elif kind == "G":
                    routing(layer, g, wait_filled(fr, g, u))
                elif kind == "S":
                    softmax(layer, g, item[1])
                elif kind == "A" and layer in (L0F, L1X, L2X):
                    t = item[1]
                    b = wait_filled(ring, g, u)
                    e = 16 if layer is not L2X else 64
                    c = 8 if layer is not L2X else 2
                    src = bank(b, c * 2 * e).rearrange("p (c b e) -> p c b e", b=2, e=e)
                    if layer is L0F:
                        wait_drained(fr, g, layer.use(("Z", t)))
                    for half in range(2):
                        rows = slice(half * S, (half + 1) * S)
                        o = o_sb[rows, t, :].rearrange("p (c e) -> p c e", e=e)
                        if layer is L0F:
                            moe = acc[rows, g.par, t, :].rearrange("p (c e) -> p c e", e=e)
                            last = dve.tensor_tensor(o, src[rows, :, half, :], moe, ALU.add)
                        else:
                            last = dve.tensor_copy(o, src[rows, :, half, :])
                    last.then_inc(drained[b], 1)
                    if layer is L0F:
                        wait_drained(ring, g, u)
                        residual(layer, g, t, o_sb[:, t, :]).then_inc(s_upd.sem, 1)
                elif kind == "E":
                    t = item[1]
                    dve.wait_ge(s_upd.sem, s_upd.after(g.back(2), t))
                    a = acc[:, g.par, t, :]
                    for j in range(2):
                        b = wait_filled(fr, g, u + j)
                        for i in range(4):
                            e = 4 * j + i
                            src, cw = bank(b)[:, i * D:(i + 1) * D], comb[:, g.par, t, e:e + 1]
                            if e == 0:
                                add = dve.tensor_scalar(a, src, cw, None, ALU.mult)
                            else:
                                add = dve.scalar_tensor_tensor(out=a, in0=src, scalar=cw, in1=a,
                                                               op0=ALU.mult, op1=ALU.add)
                            if i < 3:
                                add.then_inc(s_acc.sem, 1)
                                dve.wait_ge(s_acc.sem, s_acc.after(g, 6 * t + 3 * j + i))
                            else:
                                add.then_inc(drained[b], 1)
                                wait_drained(fr, g, u + j)
                elif kind == "Z":
                    t = item[1]
                    b = wait_filled(fr, g, u)
                    a = acc[:, g.par, t, :]
                    dve.tensor_tensor(a, bank(b, D), a, ALU.add).then_inc(drained[b], 1)
                elif kind == "W":
                    t = item[1]
                    b = wait_filled(ring, g, u)
                    if layer is L1X:
                        dve.tensor_tensor(acc[:, g.par, t, :], bank(b, D), w("l1x_bo"), ALU.add).then_inc(drained[b], 1)
                        wait_drained(ring, g, u)
                        residual(layer, g, t, acc[:, g.par, t, :]).then_inc(s_upd.sem, 1)
                    else:
                        residual(layer, g, t, bank(b, D)).then_inc(drained[b], 1)
                elif kind == "U" and layer is L1F:
                    e, c = item[1:]
                    n = HID1[c][1]
                    b = ring.bank(g, u)
                    k = 3 * e + c
                    dve.wait_ge(s_act.sem, s_act.after(g, k))
                    dve.tensor_tensor(qT[0:n, e % 2, c, :], silu_buf(k)[0:n, :], bank(b)[0:n, GT:2 * GT],
                                      ALU.mult).then_inc(drained[b], 1)
                elif kind == "D":
                    e = item[1]
                    b = wait_filled(ring, g, u)
                    if layer is L1F and e == 0:
                        dve.tensor_copy(acc[:, g.par, :, :].rearrange("p t d -> p (t d)"), bank(b, GT)).then_inc(drained[b], 1)
                    else:
                        r = e - 1 if layer is L1F else e
                        for t in range(TPG):
                            src = bank(b)[:, t * D:(t + 1) * D]
                            if e == 0:
                                last = dve.tensor_scalar(acc[:, g.par, t, :], src, comb[:, g.par, t, r:r + 1], None, ALU.mult)
                            else:
                                last = dve.scalar_tensor_tensor(out=acc[:, g.par, t, :], in0=src,
                                                                scalar=comb[:, g.par, t, r:r + 1], in1=acc[:, g.par, t, :],
                                                                op0=ALU.mult, op1=ALU.add)
                        last.then_inc(drained[b], 1)
                    wait_drained(ring, g, u)
                    if e == 7:
                        xg = x_sb[:, bass.ds(g.tile(0), TPG), :]
                        dve.scalar_tensor_tensor(out=xg, in0=acc[:, g.par, :, :], scalar=tgate[:, layer.n:layer.n + 1],
                                                 in1=xg, op0=ALU.mult, op1=ALU.add).then_inc(s_upd.sem, 1)
                elif kind == "KF":
                    b = wait_filled(ring, g, u)
                    dve.tensor_scalar(qT[:, g.par, 2, :], bank(b, GT), 0.0, None, ALU.max).then_inc(drained[b], 1)
                    wait_drained(ring, g, u)
                    dve.tensor_tensor(qT[:, g.par, 3, :], qT[:, g.par, 2, :], qT[:, g.par, 2, :],
                                      ALU.mult).then_inc(s_relu.sem, 1)
                elif kind == "VF":
                    b = wait_filled(ring, g, u)
                    wait_drained(ring, g, layer.use(("RF", 0)))
                    a = acc[:, g.par, :, :]
                    dve.tensor_tensor(a, bank(b, GT).rearrange("p (t d) -> p t d", d=D), a, ALU.mult)\
                        .then_inc(drained[b], 1)
                    wait_drained(ring, g, u)
                    xg = x_sb[:, bass.ds(g.tile(0), TPG), :]
                    dve.scalar_tensor_tensor(out=xg, in0=a, scalar=tgate[:, layer.n:layer.n + 1],
                                             in1=xg, op0=ALU.mult, op1=ALU.add).then_inc(s_upd.sem, 1)

            def mix(g):
                wait_drained(L3F.front_ring, g, 0)
                wait_drained(L3F.body_ring, g.back(2), 2)
                v = lambda ap: ap.rearrange("p (b s) -> p b s", s=S)
                xT = v(xcT[:, g.par, 0:GT])
                for i, mu in enumerate(("l3f_mur", "l3f_muk")):
                    m = w(mu)
                    o = v(qT[:, g.par, i, :])
                    prev = v(qT[:, g.par, 4 + i, :])
                    dve.tensor_scalar(prev, xT, onemu[:, i:i + 1], None, ALU.mult).then_inc(s_mix.sem, 1)
                    dve.tensor_scalar(o[:, :, 0:1], xT[:, :, 0:1], m, None, ALU.mult).then_inc(s_mix.sem, 1)
                    dve.wait_ge(s_mix.sem, s_mix.after(g, 3 * i))
                    dve.scalar_tensor_tensor(out=o[:, :, 1:S], in0=xT[:, :, 1:S], scalar=m, in1=prev[:, :, 0:S - 1],
                                             op0=ALU.mult, op1=ALU.add).then_inc(s_mix.sem, 1)

            dve.wait_ge(s_small, 16)
            for i, mu in enumerate(("l3f_mur", "l3f_muk")):
                dve.tensor_scalar(onemu[:, i:i + 1], w(mu), -1.0, 1.0, ALU.mult, ALU.add).then_inc(s_onemu, 1)
            dve.wait_ge(s_onemu, 2)
            traverse(dve, do, start)


def _pack_small(np, a):
    def rows(v, n=P):
        return np.broadcast_to(v[None, :], (n, v.shape[0]))

    def col(v):
        return v[:, None]

    def value_cols(wt):
        d = wt.shape[1] // 16
        return wt.reshape(D, 8, 2, d).transpose(0, 2, 1, 3).reshape(D, -1)

    def value_bias(v):
        v = v.reshape(8, 2, 8)
        return np.concatenate([rows(v[:, 0].reshape(-1), S), rows(v[:, 1].reshape(-1), S)], 0)

    def swapped(wt):
        h = wt.shape[1] // ROPE_D
        return wt.reshape(D, h, 2, ROPE_D // 2)[:, :, ::-1].reshape(D, -1)

    def down(wt):
        n = -(-wt.shape[0] // P)
        full = np.zeros((n * P, D), np.float32)
        full[:wt.shape[0]] = wt
        return full.reshape(n, P, D).transpose(1, 0, 2).reshape(P, n * D)

    p = {}
    p["l0x_wq"] = a["L0_xattn_Wq"].reshape(2, 2, 4, 64, D).transpose(4, 0, 2, 1, 3).reshape(D, 1024)
    p["l0x_wk"] = a["L0_xattn_Wk"].T
    p["l0x_wv"] = a["L0_xattn_Wv"].T.reshape(D, 2, 2, 64).transpose(0, 2, 1, 3).reshape(D, 256)
    p["l0x_wo"] = a["L0_xattn_Wo"].reshape(D, 2, 2, 4, 64).transpose(2, 4, 1, 3, 0).reshape(P, 1024)
    qkv, bqkv = a["L0_ffn_W_qkv"], a["L0_ffn_b_qkv"]
    p["l0f_wq"], p["l0f_wk"], p["l0f_wv"] = qkv[:, :D], qkv[:, D:2 * D], value_cols(qkv[:, 2 * D:])
    p["l0f_bq"], p["l0f_bk"], p["l0f_bv"] = col(bqkv[:D]), col(bqkv[D:2 * D]), value_bias(bqkv[2 * D:])
    p["l0f_wg"], p["l0f_bg"] = a["L0_ffn_W_gate"], rows(a["L0_ffn_b_gate"])
    p["l0f_we"] = a["L0_ffn_W_experts"].transpose(1, 0, 2).reshape(D, 1024)
    be = np.zeros((P, D), np.float32)
    be[:E_FF0] = a["L0_ffn_b_experts"]
    p["l0f_be"] = be
    p["l1x_wq"], p["l1x_wk"], p["l1x_wv"] = a["L1_xattn_Wq"].T, a["L1_xattn_Wk"].T, value_cols(a["L1_xattn_Wv"].T)
    p["l1x_bq"], p["l1x_bk"], p["l1x_bv"] = col(a["L1_xattn_bq"]), col(a["L1_xattn_bk"]), value_bias(a["L1_xattn_bv"])
    p["l1x_wo"], p["l1x_bo"] = a["L1_xattn_Wo"].T, rows(a["L1_xattn_bo"])
    p["l1f_wg"], p["l1f_bg"] = a["L1_ffn_wr"].T, rows(a["L1_ffn_rb"])
    p["l1f_shared"] = np.concatenate([a["L1_ffn_sg"].T, a["L1_ffn_su"].T, down(a["L1_ffn_sd"].T)], 1)
    p["l2x_scale"] = col(a["L2_xattn_rms_scale"])
    q2 = a["L2_xattn_q_w"].transpose(1, 0, 2).reshape(D, D)
    k2 = np.concatenate([a["L2_xattn_kv_w"][0, 0]] * 4, 1)
    p["l2x_wq"] = np.concatenate([q2, swapped(q2)], 1)
    p["l2x_wk"] = np.concatenate([k2, swapped(k2)], 1)
    p["l2x_wv"] = a["L2_xattn_kv_w"][1, 0]
    p["l2x_wo"] = a["L2_xattn_out_w"].reshape(D, D)
    p["l2f_wg"], p["l2f_bg"] = a["L2_ffn_Wr"], rows(a["L2_ffn_br"])
    p["l3x_wq"], p["l3x_wk"], p["l3x_wv"] = a["L3_xattn_Wq"], a["L3_xattn_Wk"], value_cols(a["L3_xattn_Wv"])
    p["l3x_wo"] = a["L3_xattn_Wo"].reshape(8, P, D).transpose(1, 0, 2).reshape(P, 1024)
    p["l3f_wr"], p["l3f_wk"], p["l3f_wv"] = a["L3_ffn_W_r"].T, a["L3_ffn_W_k"].T, a["L3_ffn_W_v"].T
    p["l3f_mur"], p["l3f_muk"] = col(a["L3_ffn_mu_r"]), col(a["L3_ffn_mu_k"])
    p["gates"] = rows(np.stack([a["g_xattn"], a["g_ffn"]], 1).reshape(-1))
    p["ident"] = np.eye(P, dtype=np.float32)
    p["earlier"] = rows((np.arange(8)[:, None] > np.arange(8)[None, :]).astype(np.float32).reshape(-1))
    half = ROPE_D // 2
    d = np.arange(P) % ROPE_D
    timescale = np.float32(10000.0) ** (np.float32(2.0 / ROPE_D) * (d % half).astype(np.float32))
    sign = np.where(d < half, -1.0, 1.0).astype(np.float32)[:, None]
    tabs = []
    for pos in (np.arange(S, 2 * S), np.arange(S)):
        rad = pos.astype(np.float32)[None, :] / timescale[:, None]
        tabs += [np.cos(rad), np.sin(rad) * sign]
    p["rope"] = np.concatenate(tabs, 1).astype(np.float32)
    for name, width in SMALL:
        assert p[name].shape == (P, width), (name, p[name].shape)
    w1 = [np.concatenate([a["L1_ffn_rg"][e].T, a["L1_ffn_ru"][e].T, down(a["L1_ffn_rd"][e].T)], 1)
          for e in range(E_FF1)]
    w2 = [np.concatenate([a["L2_ffn_W1"][e], down(a["L2_ffn_W2"][e])], 1) for e in range(E_FF2)]
    return (np.concatenate([p[name] for name, _ in SMALL], 1), np.concatenate([p[name] for name in LATE], 1), np.concatenate(w1, 1), np.concatenate(w2, 1))


def kernel(**inputs):
    import numpy as _np
    import concourse.bacc as _bacc
    from concourse import mybir as _mybir
    from concourse.bass_utils import run_bass_kernel_spmd as _run

    a = {k: _np.asarray(v) for k, v in inputs.items()}
    small, late, w1, w2 = _pack_small(_np, a)
    ctxT = a["ctx_1024"].reshape(B * S, D).T
    named = {
        "x": a["x"], "ctx": a["ctx_1024"], "ctxT": ctxT, "mask1": a["mask_BxS2_ff1"], "mask2": a["mask_BxS2_bk0"],
        "small": small, "late": late, "w1": w1, "w2": w2,
    }
    nc = _bacc.Bacc("TRN2", target_bir_lowering=False, num_devices=1)
    arrays, args = {}, []
    for name, v in named.items():
        v = _np.ascontiguousarray(v)
        arrays[f"in_{name}"] = v
        args.append(nc.dram_tensor(f"in_{name}", v.shape, _mybir.dt.from_np(v.dtype), kind="ExternalInput").ap())
    args.append(nc.dram_tensor("out_0", (B, S, D), _mybir.dt.from_np(_np.dtype("float32")),
                               kind="ExternalOutput").ap())
    build(nc, *args)
    r = _run(nc, [arrays], core_ids=[0])
    return r.results[0]["out_0"]
```

```python
from contextlib import ExitStack

import concourse.bass as bass
from concourse import mybir

ALU = mybir.AluOpType
ACT = mybir.ActivationFunctionType
F32 = mybir.dt.float32
F32R = mybir.dt.float32r
U8 = mybir.dt.uint8
AX_X = mybir.AxisListType.X

P = 128
B, S, D = 128, 64, 128
NT = B * S // P
GT = 256
TPG = GT // P
BPG = GT // S
NG = B * S // GT
PAIRS = NG // 2
LN_EPS = 1e-5
RMS_EPS = 1e-6
F32_MIN = -3.4028234663852886e38
E_F32 = 2.718281828459045
MASK_FILL = -2.3819763e38
I_FF, E_FF1 = 352, 7
FFN2, E_FF2 = 512, 8
E_FF0 = 8
ROPE_D = 32

CREDIT = 64

SMALL = [
    ("gates", 8), ("ident", 128),
    ("l0x_wq", 1024), ("l0x_wk", 256), ("l0x_wv", 256), ("l0x_wo", 1024),
    ("l0f_wq", 128), ("l0f_wk", 128), ("l0f_wv", 128), ("l0f_bq", 1), ("l0f_bk", 1), ("l0f_bv", 64),
    ("l0f_wg", 8), ("l0f_bg", 8), ("l0f_we", 1024), ("l0f_be", 128),
    ("l1x_wq", 128), ("l1x_wk", 128), ("l1x_wv", 128), ("l1x_bq", 1), ("l1x_bk", 1), ("l1x_bv", 128),
    ("l1x_wo", 128), ("l1x_bo", 128),
    ("l1f_wg", 7), ("l1f_bg", 7), ("l1f_shared", 2 * 352 + 3 * 128),
    ("l2x_scale", 1), ("l2x_wq", 256), ("l2x_wk", 256), ("l2x_wv", 32), ("l2x_wo", 128),
    ("l2f_wg", 8), ("l2f_bg", 8),
    ("l3f_wr", 128), ("l3f_wk", 128), ("l3f_wv", 128), ("l3f_mur", 1), ("l3f_muk", 1),
    ("earlier", 64), ("rope", 256),
]
SMALL_AT, _n = {}, 0
for _name, _w in SMALL:
    SMALL_AT[_name] = (_n, _n + _w)
    _n += _w
SMALL_W = _n
LATE_AT = SMALL_AT["l0x_wq"][0]
FIRST_W = SMALL_AT["l0x_wo"][1]
LATE = ["l3x_wq", "l3x_wk", "l3x_wv", "l3x_wo"]
for _i, _name in enumerate(LATE):
    SMALL_AT[_name] = (LATE_AT + 1024 * _i, LATE_AT + 1024 * (_i + 1))
assert LATE_AT + 1024 * len(LATE) <= SMALL_AT["l1x_wq"][0]
EXPERT1 = 2 * I_FF + 3 * D
EXPERT2 = FFN2 + 4 * D
HID1 = [(0, 128), (128, 128), (256, 96)]


class Layer:

    def __init__(self, n, name, order, uses, body_banks, heads=0, scale=1.0, cross=False,
                 experts=0, top=0):
        self.n, self.name, self.order, self.uses = n, name, order, uses
        self.body_banks = body_banks
        self.heads, self.scale, self.cross = heads, scale, cross
        self.experts, self.top = experts, top
        self.front = []
        self.body = []
        for item, lag in order:
            if item[0] in ("L", "M", "H", "S", "P", "N"):
                continue
            (self.front if lag == 1 else self.body).extend([item] * uses.get(item[0], 1))

    def use(self, item):
        return (self.front if item in self.front else self.body).index(item)


def stages(text):
    out = []
    for word in text.split():
        name = word.rstrip("+-")
        lag = word.count("+") - word.count("-")
        kind = name.rstrip("0123456789.")
        numbers = [int(k) for k in name[len(kind):].split(".")] if name != kind else [0]
        out.append(((kind, *numbers), lag))
    return out


def make_layers():
    attention = {"T": 2, "A": 2}
    narrow = {"T": 2, "A": 1}
    l0x = Layer(0, "l0x", stages(
        "L++ T0- S0 T1- S1 P0 F+ A0- M++ Q0+ N0 K0+ A1- N1 Q1+ P1 Q2+ W0- Q3+ W1- V0+"),
        attention, (6, 7), 16, 64 ** -0.5, True)
    l0f = Layer(1, "l0f", stages(
        "T1- S0 F+ T0- QK+ L++ G+ S1 A0- P0 H+ P1 E0.0+ E0.1+ A1- C+ V0+ N0 N1 Z0+ E1.0+ E1.1+ M++ Z1+"),
        narrow, (6, 7), 16, 8 ** -0.5, False, E_FF0, 2)
    l1x = Layer(2, "l1x", stages(
        "F+ S0 QK+ S1 L++ T0- T1- N0 A0- A1- P0 P1 N1 M++ V+ X0- X1- W0- W1-"),
        narrow, (6, 7), 16, 8 ** -0.5, True)
    l1f = Layer(3, "l1f", stages(
        "U0.0 U0.1 U0.2 L++ U1.0 U1.1 F+ D0 U1.2 U2.0 U2.1 U2.2 D1 U3.0 U3.1 D2 U3.2 "
        "U4.0 U4.1 U4.2 M++ D3 G+ D4 U5.0 U5.1 U5.2 H+ U6.0 U6.1 U6.2 D5 U7.0 U7.1 U7.2 "
        "D6 D7"), {}, (0, 1, 2, 3), experts=E_FF1, top=2)
    l2x = Layer(4, "l2x", stages(
        "S0 L++ F+ S1 Q+ T0- T1- P0 A0- P1 A1- K+ N0 M++ X0- X1- N1 W0- V+ W1-"),
        {"T": 1, "A": 1}, (6, 7), 4, 32 ** -0.5, True)
    order = []
    for e in range(8):
        order += [(("U", e, 0), 0), (("U", e, 1), 0)]
        if e:
            order.append((("D", e - 1), 0))
        order += stages({0: "F+", 1: "L++", 2: "G+", 4: "M++", 5: "H+"}.get(e, ""))
    order.append((("D", 7), 0))
    l2f = Layer(5, "l2f", order, {}, (0, 1, 2, 3), experts=E_FF2, top=1)
    l3x = Layer(6, "l3x", stages(
        "T0- S0 T1- F+ P0 S1 Q2+ N0 Q0+ A0- K2+ P1 Q1+ A1- V2+ N1 K0+ W0- Q3+ K3+ L++ V0+ W1- M++ V3+ K1+ V1+"),
        attention, (6, 7), 16, 64 ** -0.5, True)
    l3f = Layer(7, "l3f", stages("KF L++ F+ M++ RF VF"), {}, (0, 1, 2))
    return [l0x, l0f, l1x, l1f, l2x, l2f, l3x, l3f]


class Group:

    def __init__(self, layer, pair, par):
        self.layer, self.pair, self.par = layer, pair, par

    def ahead(self, n):
        k = self.par + n
        return Group(self.layer, self.pair + k // 2, k % 2)

    def back(self, n):
        return self.ahead(-n)

    def tile(self, t):
        return self.pair * (2 * TPG) + (self.par * TPG + t)


class Step:

    def __init__(self, sem, layers, per):
        self.credit = max(CREDIT, 4 * max(per.values()))
        self.sem, self.per, self.base, n = sem, per, {}, self.credit
        for layer in layers:
            self.base[layer.n] = n
            n += per.get(layer.name, 0) * NG
        self.base[len(layers)] = n

    def after(self, g, k):
        per = self.per[g.layer.name]
        return g.pair * (2 * per) + (self.base[g.layer.n] + g.par * per + k + 1)


class DmaStep:

    def __init__(self, sems, layers, per):
        self.credit = max(CREDIT, 2 * max(per.values()))
        self.sems, self.per, self.base, n = sems, per, {}, self.credit
        for layer in layers:
            self.base[layer.n] = n
            n += per.get(layer.name, 0) * PAIRS

    def sem(self, g):
        return self.sems[g.par]

    def all(self, g):
        per = self.per[g.layer.name]
        return g.pair * per + (self.base[g.layer.n] + per)


class Ring:

    def __init__(self, slots, uses, base):
        self.slots, self.uses, self.base = slots, uses, base
        assert 2 * uses % len(slots) == 0
        self.total = NG * uses // len(slots)

    def bank(self, g, u):
        return self.slots[(g.par * self.uses + u) % len(self.slots)]

    def count(self, g, u):
        n = g.par * self.uses + u
        per_pair = 2 * self.uses // len(self.slots)
        return g.pair * per_pair + (self.base[self.slots[n % len(self.slots)]] + n // len(self.slots) + 1)


def build(nc, x_in, ctx_in, ctxT_in, mask1_in, mask2_in, small_in, late_in, w1_in, w2_in, out):
    layers = make_layers()
    L0X, L0F, L1X, L1F, L2X, L2F, L3X, L3F = layers

    base = {b: CREDIT for b in range(8)}
    bank_base = []
    for layer in layers:
        bank_base.append(dict(base))
        layer.front_ring = Ring((4, 5), len(layer.front), dict(base))
        layer.body_ring = Ring(layer.body_banks, len(layer.body), dict(base))
        rings = [layer.front_ring, layer.body_ring]
        if layer.heads:
            layer.score_ring = Ring((0, 2), TPG, dict(base))
            rings.append(layer.score_ring)
        for ring in rings:
            for b in ring.slots:
                base[b] += ring.total
    bank_base.append(dict(base))

    ctx = ExitStack()
    with ctx:
        def sb(name, shape, dt=F32):
            return ctx.enter_context(nc.sbuf_tensor(name, shape, dt))

        def step(name, **per):
            return Step(ctx.enter_context(nc.semaphore(name)), layers, per)

        def dma_step(name, **per):
            return DmaStep([ctx.enter_context(nc.semaphore(f"{name}{i}")) for i in range(2)], layers, per)

        ps = ctx.enter_context(nc.psum_tensor("ps", [P, 8, 512], F32))
        x_sb = sb("x_sb", [P, NT, D])
        small = sb("small", [P, SMALL_W])
        tgate = sb("tgate", [P, 8])
        arena_b = sb("arena_b", [P, 8192])
        xn = sb("xn", [P, 2, TPG, D])
        ctxn = sb("ctxn", [P, 2, TPG, D])
        ctx_sb = sb("ctx_sb", [P, 2, TPG, D])
        xcT = sb("xcT", [P, 2, 2 * GT])
        qT = sb("qT", [P, 2, 8, GT])
        xhi = sb("xhi", [P, 2, GT])
        xlo = sb("xlo", [P, 2, GT])
        kT = sb("kT", [P, 2, GT])
        vsmall = sb("vsmall", [P, 2, BPG * 8 * 16])
        o_sb = sb("o_sb", [P, TPG, D])
        acc = sb("acc", [P, 2, TPG, D])
        masked = sb("masked", [P, NT, S], U8)
        st = sb("st", [P, 4, 6])
        mv = sb("mv", [P, 4, 2])
        agg = sb("agg", [P, 5, 4])
        veps = sb("veps", [P, 4])
        rstd = sb("rstd", [P, 4])
        neghalf = sb("neghalf", [P, 4])
        e_base = sb("e_base", [P, TPG * 8])
        mx = sb("mx", [P, TPG, 16])
        negmax = sb("negmax", [P, TPG, 16])
        sm = sb("sm", [P, TPG, 16])
        rv = sb("rv", [P, TPG, 16])
        route = sb("route", [P, 8, TPG * 8])
        cmp_gt = sb("cmp_gt", [P, TPG, 8, 8])
        cmp_eq = sb("cmp_eq", [P, TPG, 8, 8])
        comb = sb("comb", [P, 2, TPG, 8])
        combT = sb("combT", [8, 2, GT])
        rms_gain = sb("rms_gain", [P, 1])
        onemu = sb("onemu", [P, 2])

        with ExitStack() as shared:
            def sb_shared(name, shape):
                return shared.enter_context(nc.sbuf_tensor(name, shape, F32))

            arena_a = sb_shared("arena_a", [P, 8192])
            probs = sb_shared("probs", [P, 2, TPG, 16 * S])
            pT = sb_shared("pT", [P, TPG, 8, P])
            oT = sb_shared("oT", [P, TPG, 8, P])
        parts_a = sb("parts_a", [P, 8192])
        parts_probs = sb("parts_probs", [P, 4096])
        parts_pT = sb("parts_pT", [P, 2048])
        parts_oT = sb("parts_oT", [P, 2048])

        def w(name):
            a, b = SMALL_AT[name]
            return small[:, a:b]

        filled = [ctx.enter_context(nc.semaphore(f"filled{b}")) for b in range(8)]
        drained = [ctx.enter_context(nc.semaphore(f"drained{b}")) for b in range(8)]
        att = dict(l0x=2, l0f=2, l1x=2, l2x=2, l3x=2)
        all2 = dict(att, l1f=2, l2f=2, l3f=2)
        s_stats = step("s_stats", **dict(all2, l2x=4))
        s_aggr = step("s_aggr", **{k: 7 for k in all2})
        s_veps = step("s_veps", **dict({k: 1 for k in all2}, l2x=3))
        s_rstd = step("s_rstd", **{k: 1 for k in all2})
        s_xn = step("s_xn", **dict(all2, l2x=4))
        s_ctx = dma_step("s_ctx", l0x=16, l1x=16, l2x=16, l3x=16)
        s_kspread = dma_step("s_kspread", l0f=256, l1x=256)
        s_rope = step("s_rope", l2x=4)
        s_mx = step("s_mx", **att)
        s_masked = step("s_masked", l1x=2, l2x=2)
        s_sub = step("s_sub", l0f=2, l1x=2, l2x=2)
        s_exp = step("s_exp", l0x=2, l1x=2, l2x=2, l3x=2)
        s_sum = step("s_sum", l0x=2, l1x=2, l2x=2, l3x=2)
        s_rv = step("s_rv", **att)
        s_probs = step("s_probs", **att)
        s_route = step("s_route", l0f=9, l1f=12, l2f=7)
        s_rexp = step("s_rexp", l0f=1, l1f=1, l2f=1)
        s_acc = step("s_acc", l0f=12)
        s_act = step("s_act", l1f=24)
        s_mix = step("s_mix", l3f=6)
        s_relu = step("s_relu", l3f=1)
        s_upd = step("s_upd", l0f=2, l1x=2, l1f=1, l2f=1, l3f=1)
        s_xlo = step("s_xlo", l1f=1, l2f=1)
        s_rank = step("s_rank", l0f=1, l1f=1, l2f=1)
        s_small = ctx.enter_context(nc.semaphore("s_small"))
        s_rest = ctx.enter_context(nc.semaphore("s_rest"))
        s_x0 = ctx.enter_context(nc.semaphore("s_x0"))
        s_x = ctx.enter_context(nc.semaphore("s_x"))
        s_m1 = ctx.enter_context(nc.semaphore("s_m1"))
        s_m2 = ctx.enter_context(nc.semaphore("s_m2"))
        s_w1 = ctx.enter_context(nc.semaphore("s_w1"))
        s_hi = ctx.enter_context(nc.semaphore("s_hi"))
        s_lo = ctx.enter_context(nc.semaphore("s_lo"))
        s_late = ctx.enter_context(nc.semaphore("s_late"))
        s_w2 = ctx.enter_context(nc.semaphore("s_w2"))
        s_const = ctx.enter_context(nc.semaphore("s_const"))
        s_zero = ctx.enter_context(nc.semaphore("s_zero"))
        s_tanh = ctx.enter_context(nc.semaphore("s_tanh"))
        s_mask = ctx.enter_context(nc.semaphore("s_mask"))
        s_onemu = ctx.enter_context(nc.semaphore("s_onemu"))
        s_scale = ctx.enter_context(nc.semaphore("s_scale"))
        s_out = ctx.enter_context(nc.semaphore("s_out"))
        steps = [s_stats, s_aggr, s_veps, s_rstd, s_xn, s_rope, s_mx, s_masked, s_sub,
                 s_exp, s_sum, s_rv, s_probs, s_route, s_rexp, s_acc, s_act, s_mix, s_relu, s_upd, s_rank, s_xlo]

        ident = w("ident")

        def k_pairs(layer, par):
            arena = arena_b[:, par * 4096:(par + 1) * 4096]
            return arena.rearrange("p (c b k) -> p c b k", b=BPG, k=P)

        def v_pairs(layer, par):
            arena = arena_a[:, par * 4096:(par + 1) * 4096]
            return arena.rearrange("p (b c k) -> p b c k", b=BPG, k=P)

        def k_spread(par):
            return arena_a[:, par * 4096:(par + 1) * 4096].rearrange("p (h t) -> p h t", h=16)

        def k_rope(par):
            return arena_b[:, par * 1024:(par + 1) * 1024].rearrange("p (b n) -> p b n", b=BPG)

        def v_small(par):
            return vsmall[:, par, :].rearrange("p (b c e) -> p b c e", b=BPG, e=16)

        def v_rope(par):
            return vsmall[:, par, 0:BPG * 64].rearrange("p (b e) -> p b e", b=BPG)

        def w1_expert(e):
            return w("l1f_shared") if e == 0 else w1_sb[:, (e - 1) * EXPERT1:e * EXPERT1]

        UP1, UP2 = 2 * I_FF, FFN2

        def as_r(ap):
            return ap.bitcast(F32R)

        def up_full(layer, e):
            return w1_expert(e)[:, 0:UP1] if layer is L1F else w2_sb[:, e * EXPERT2:e * EXPERT2 + UP2]

        def up_hi(layer, e):
            if layer is L1F:
                return parts_a[:, e * UP1:(e + 1) * UP1]
            return parts_probs[:, e * UP2:(e + 1) * UP2]

        def up_lo(layer, e):
            if layer is L1F:
                if e < 3:
                    return parts_a[:, (8 + e) * UP1:(9 + e) * UP1]
                return parts_probs[:, (e - 3) * UP1:(e - 2) * UP1]
            return (parts_pT, parts_oT)[e // 4][:, e % 4 * UP2:(e % 4 + 1) * UP2]

        w1_sb = arena_b
        w2_sb = arena_a

        def mask_staged():
            return arena_b[:, 0:NT * S].rearrange("p (n k) -> p n k", k=S)

        def silu_buf(k):
            return kT[:, k % 2, :]

        def bank(b, n=512):
            return ps[:, b, 0:n]

        def score_bank(b):
            return ps[:, b:b + 2, :].rearrange("p a n -> p (a n)")

        def first_of(g):
            return type(g.pair) is int and g.pair == 0 and g.par == 0

        def traverse(eng, do, start=None):
            for layer in layers:
                if start:
                    start(layer)

                def iteration(at, whole=False):
                    for item, lag in layer.order:
                        g = at.ahead(lag)
                        if whole or 0 <= g.pair < PAIRS:
                            do(layer, item, g)

                last = min(lag for _, lag in layer.order)
                first = 1 if last >= -1 else 3
                for i in range(-2, first):
                    iteration(Group(layer, 0, 0).ahead(i))
                count = (NG - 2 - first) // 2
                with eng.Fori(0, count) as pair:
                    at = Group(layer, pair, 0).ahead(first)
                    iteration(at, whole=True)
                    iteration(at.ahead(1), whole=True)
                for i in range(first + 2 * count, NG - last):
                    iteration(Group(layer, 0, 0).ahead(i))

        block = ctx.enter_context(nc.Block())

        @block.sync
        def _(sp):
            for s in filled + drained:
                sp.sem_inc(s, CREDIT)
            for s in steps:
                sp.sem_inc(s.sem, s.credit)
            for s in (s_ctx, s_kspread):
                for i in range(2):
                    sp.sem_inc(s.sems[i], s.credit)
            x_v = x_in.rearrange("b s d -> (b s) d").rearrange("(n p) d -> p n d", p=P)
            n = TPG * 2
            sp.dma_start(x_sb[:, 0:n, :], x_v[:, 0:n, :]).then_inc(s_x0, 16)
            sp.dma_start(small[:, 0:FIRST_W], small_in[:, 0:FIRST_W]).then_inc(s_small, 16)
            sp.dma_start(x_sb[:, n:NT, :], x_v[:, n:NT, :]).then_inc(s_x, 16)
            sp.dma_start(small[:, FIRST_W:SMALL_W], small_in[:, FIRST_W:SMALL_W]).then_inc(s_rest, 16)
            ctx_v = ctx_in.rearrange("b s d -> (b s) d").rearrange("(n p) d -> p n d", p=P)
            out_v = out.rearrange("b s d -> (b s) d").rearrange("(n p) d -> p n d", p=P)

            def load_mask(dst, src, sem, n0, n1):
                src_v = src.rearrange("(n b) k -> b n k", b=2)
                for b in range(2):
                    sp.dma_start(dst[b * S:(b + 1) * S, :, :],
                                 src_v[b, n0:n1, :].partition_broadcast(S)).then_inc(sem, 16)

            def start(layer):
                if layer is L0F:
                    sp.wait_ge(s_zero, 2)
                    for b in L0X.body_banks:
                        sp.wait_ge(drained[b], bank_base[1][b])
                    load_mask(mask_staged(), mask1_in, s_m1, 0, NT)
                if layer is L1F:
                    for b in L1X.body_banks:
                        sp.wait_ge(drained[b], bank_base[3][b])
                    load_mask(masked, mask2_in, s_m2, 0, NT)

            def do(layer, item, g):
                if item == ("L", 0) and layer.cross:
                    if layer is L2X:
                        sp.wait_ge(s_xn.sem, s_xn.after(g.back(2), 3))
                        sp.dma_start(ctx_sb[:, g.par, :, :],
                                     ctx_v[:, bass.ds(g.tile(0), TPG), :]).then_inc(s_ctx.sem(g), 16)
                    else:
                        u = len(layer.front) - 1
                        back = g.back(2)
                        sp.wait_ge(drained[layer.front_ring.bank(back, u)], layer.front_ring.count(back, u))
                        sp.dma_start(xcT[:, g.par, GT:2 * GT],
                                     ctxT_in[:, bass.ds(g.tile(0) * P, GT)]).then_inc(s_ctx.sem(g), 16)
                if item == ("QK", 0):
                    sp.wait_ge(drained[layer.front_ring.bank(g, 1)], layer.front_ring.count(g, 1))
                    for h in range(16):
                        sp.dma_start(k_spread(g.par)[8 * h:8 * h + 8, h, :],
                                     kT[8 * h:8 * h + 8, g.par, :]).then_inc(s_kspread.sem(g), 16)
                if item == ("VF", 0):
                    sp.wait_ge(s_upd.sem, s_upd.after(g, 0))
                    sp.dma_start(out_v[:, bass.ds(g.tile(0), TPG), :],
                                 x_sb[:, bass.ds(g.tile(0), TPG), :]).then_inc(s_out, 16)

            traverse(sp, do, start)
            sp.wait_ge(s_out, 16 * NG)

        @block.gpsimd
        def _(pool):
            pool.memset(neghalf[:, :], -0.5).then_inc(s_const, 1)
            pool.memset(e_base[:, :], E_F32).then_inc(s_const, 1)
            pool.memset(arena_b[:, :], 0.0).then_inc(s_const, 1)
            pool.memset(arena_a[:, :], 0.0).then_inc(s_const, 1)
            pool.memset(vsmall[:, :, :], 0.0).then_inc(s_const, 1)
            pool.wait_ge(s_const, 5)

            def start(layer):
                if layer is L0F:
                    for b in L0X.body_banks:
                        pool.wait_ge(drained[b], bank_base[1][b])
                    pool.memset(arena_a[:, 0:4096], 0.0).then_inc(s_zero, 1)
                if layer is L2X:
                    for b in L1F.body_banks:
                        pool.wait_ge(drained[b], bank_base[4][b])
                    pool.memset(arena_b[:, 0:2048], 0.0).then_inc(s_zero, 1)
                    pool.memset(vsmall[:, :, :], 0.0).then_inc(s_zero, 1)
                if layer is L2F:
                    for b in L2X.body_banks:
                        pool.wait_ge(drained[b], bank_base[5][b])
                    pool.memset(arena_b[:, :], 0.0).then_inc(s_zero, 1)
                if layer is L3X:
                    for b in L2F.body_banks:
                        pool.wait_ge(drained[b], bank_base[6][b])
                    pool.memset(arena_a[:, 0:4096], 0.0).then_inc(s_zero, 1)

            def do(layer, item, g):
                if item == ("L", 0):
                    n = 4 if layer is L2X else 2
                    last = 2 if layer is L2X else 0
                    pool.wait_ge(s_veps.sem, s_veps.after(g, last))
                    pool.wait_ge(s_xn.sem, s_xn.after(g.back(1), n - 1))
                    pool.tensor_tensor(rstd[:, 0:n], veps[:, 0:n], neghalf[:, 0:n],
                                       ALU.pow).then_inc(s_rstd.sem, 1)
                if item == ("G", 0):
                    n = TPG * layer.experts
                    pool.wait_ge(s_route.sem, s_route.after(g, 0 if layer is L2F else 1))
                    pool.tensor_tensor(route[:, 1, 0:n], e_base[:, 0:n], route[:, 0, 0:n],
                                       ALU.pow).then_inc(s_rexp.sem, 1)
                if item[0] == "N":
                    t, nh = item[1], layer.heads
                    pool.wait_ge(s_rv.sem, s_rv.after(g, t))
                    pr = probs[:, g.par, t, 0:nh * S].rearrange("p (h k) -> p h k", k=S)
                    pool.tensor_tensor(pr, pr, rv[:, t, 0:nh].unsqueeze(2).to_broadcast([P, nh, S]),
                                       ALU.mult).then_inc(s_probs.sem, 1)

            traverse(pool, do, start)

        @block.tensor
        def _(pe):
            def take(ring, g, u):
                b = ring.bank(g, u)
                pe.wait_ge(drained[b], ring.count(g, u) - 1)
                return b

            def wait_drained(ring, g, u):
                pe.wait_ge(drained[ring.bank(g, u)], ring.count(g, u))

            def last_uses(layer, kinds):
                return [v for v, item in enumerate(layer.front) if item[0] in kinds][-2:]

            def mm(o, lhsT, rhs, start=True, stop=True):
                return nc.tensor.matmul(o, lhsT, rhs, start=start, stop=stop, skip_group_check=True)

            def start(layer):
                if layer is L0X:
                    pe.wait_ge(s_small, 16)
                    pe.wait_ge(s_const, 5)
                if layer is L0F:
                    pe.wait_ge(s_rest, 16)
                if layer is L1F:
                    pe.wait_ge(s_w1, 16)
                if layer is L2F:
                    pe.wait_ge(s_w2, 16)
                if layer is L3X:
                    pe.wait_ge(s_late, 16)

            def front(layer, item, g):
                ring = layer.front_ring
                u = layer.use(item)
                kind, j = item[0:2]
                xT = xcT[:, g.par, 0:GT]
                cT = xcT[:, g.par, GT:2 * GT]
                if u == 1:
                    wait_drained(ring, g, 0)
                if kind == "E":
                    i = item[2]
                    b = take(ring, g, u)
                    mm(bank(b), xT[:, j * P:(j + 1) * P],
                       w("l0f_we")[:, i * 512:(i + 1) * 512]).then_inc(filled[b], 1)
                    return
                b = take(ring, g, u)
                o = bank(b)
                if kind == "F":
                    for t in range(TPG):
                        pe.wait_ge(s_xn.sem, s_xn.after(g, t))
                        last = nc.tensor.transpose(o[:, t * P:(t + 1) * P], xn[:, g.par, t, :], ident)
                    if layer is L2X:
                        for t in range(TPG):
                            pe.wait_ge(s_xn.sem, s_xn.after(g, 2 + t))
                            last = nc.tensor.transpose(o[:, GT + t * P:GT + (t + 1) * P], ctxn[:, g.par, t, :], ident)
                    last.then_inc(filled[b], 1)
                    return
                if layer.cross and layer is not L2X and kind in ("QK", "K", "V"):
                    pe.wait_ge(s_ctx.sem(g), s_ctx.all(g))
                if kind == "Q" and layer is not L2X:
                    for i in range(2):
                        c = 2 * j + i
                        last = mm(o[:, i * GT:(i + 1) * GT], w(layer.name + "_wq")[:, c * P:(c + 1) * P], xT)
                elif kind == "K" and layer is not L2X:
                    for i in range(2):
                        c = 2 * j + i
                        last = mm(o[:, i * GT:(i + 1) * GT], w(layer.name + "_wk")[:, c * P:(c + 1) * P], cT)
                elif kind == "Q" or kind == "K":
                    ww = w("l2x_wq") if kind == "Q" else w("l2x_wk")
                    for i in range(2):
                        last = mm(o[:, i * GT:(i + 1) * GT], ww[:, i * P:(i + 1) * P], xT if kind == "Q" else cT)
                elif kind == "QK":
                    mm(o[:, 0:GT], w(layer.name + "_wq"), xT)
                    last = mm(o[:, GT:2 * GT], w(layer.name + "_wk"), cT if layer.cross else xT)
                elif kind == "V":
                    src = cT if layer.cross else xT
                    wv = w(layer.name + "_wv")
                    seqs = [j] if layer is L3X else range(BPG)
                    n = {"l3x": 512, "l0x": 128, "l0f": 64, "l1x": 64, "l2x": 32}[layer.name]
                    for i, q in enumerate(seqs):
                        for half in range(2):
                            ww = wv if layer is L2X else wv[:, half * n:(half + 1) * n]
                            last = mm(o[half * S:(half + 1) * S, i * n:(i + 1) * n],
                                      src[:, q * S:(q + 1) * S], ww)
                elif kind == "G":
                    ne = layer.experts
                    for t in range(TPG):
                        last = mm(o[:, t * ne:(t + 1) * ne], xT[:, t * P:(t + 1) * P], w(layer.name + "_wg"))
                elif kind == "C":
                    pe.wait_ge(s_route.sem, s_route.after(g, 8))
                    for t in range(TPG):
                        last = nc.tensor.transpose(o[0:8, t * P:(t + 1) * P], comb[:, g.par, t, :], ident)
                elif kind == "Z":
                    wait_drained(ring, g, layer.use(("C", 0)))
                    last = mm(o[:, 0:D], combT[0:8, g.par, j * P:(j + 1) * P], w("l0f_be")[0:8, :])
                last.then_inc(filled[b], 1)

            def do(layer, item, g):
                ring, fr = layer.body_ring, layer.front_ring
                kind = item[0]
                if kind in ("L", "M", "H", "P", "N"):
                    return
                if item in layer.front:
                    front(layer, item, g)
                    return
                u = layer.use(item) if kind != "S" else None
                xT = xcT[:, g.par, 0:GT]
                if kind == "S":
                    t = item[1]
                    b = take(layer.score_ring, g, t)
                    o = score_bank(b)
                    if t == 0:
                        for v in last_uses(layer, ("Q", "K", "QK")):
                            wait_drained(fr, g, v)
                        if layer in (L0F, L1X):
                            pe.wait_ge(s_kspread.sem(g), s_kspread.all(g))
                    if layer in (L0F, L1X):
                        for half in range(2):
                            for hb in range(2):
                                last = mm(o[hb * S:(hb + 1) * S, half * 512:(half + 1) * 512],
                                          qT[:, g.par, 0, t * P + hb * S:t * P + (hb + 1) * S],
                                          k_spread(g.par)[:, 8 * half:8 * half + 8,
                                                          t * P + hb * S:t * P + (hb + 1) * S])
                    if layer is L2X:
                        for hb in range(2):
                            last = mm(o[hb * S:(hb + 1) * S, 0:4 * S],
                                      qT[:, g.par, 0, t * P + hb * S:t * P + (hb + 1) * S],
                                      k_rope(g.par)[:, 2 * t + hb, :])
                    if layer in (L0X, L3X):
                        for c in range(8):
                            for hb in range(2):
                                last = mm(o[hb * S:(hb + 1) * S, c * P:(c + 1) * P],
                                          qT[:, g.par, c, t * P + hb * S:t * P + (hb + 1) * S],
                                          k_pairs(layer, g.par)[:, c // 4 if layer is L0X else c, 2 * t + hb, :])
                    last.then_inc(filled[b], 1)
                elif kind == "T":
                    t = item[1]
                    pe.wait_ge(s_probs.sem, s_probs.after(g, t))
                    nchunk = layer.heads * S // P
                    for j in range(layer.uses["T"]):
                        b = take(ring, g, u + j)
                        for i in range(min(4, nchunk)):
                            c = 4 * j + i
                            last = nc.tensor.transpose(bank(b)[:, i * P:(i + 1) * P],
                                                       probs[:, g.par, t, c * P:(c + 1) * P], ident)
                        last.then_inc(filled[b], 1)
                elif kind == "A":
                    t = item[1]
                    ut = layer.use(("T", t))
                    if t == 0:
                        for v in last_uses(layer, ("V",)):
                            wait_drained(fr, g, v)
                    for j in range(layer.uses["A"]):
                        b = take(ring, g, u + j)
                        o = bank(b)
                        for v in range(layer.uses["T"]):
                            if v == j or layer.uses["A"] == 1:
                                wait_drained(ring, g, ut + v)
                        if layer is L0X:
                            for hb in range(2):
                                last = mm(o[:, hb * 256:(hb + 1) * 256], v_pairs(layer, g.par)[:, 2 * t + hb, j, :],
                                          pT[:, t, 4 * j:4 * j + 4, hb * S:(hb + 1) * S])
                        elif layer is L3X:
                            for i in range(4):
                                for hb in range(2):
                                    last = mm(o[:, i * P + hb * S:i * P + (hb + 1) * S],
                                              v_pairs(layer, g.par)[:, 2 * t + hb, 4 * j + i, :],
                                              pT[:, t, 4 * j + i, hb * S:(hb + 1) * S])
                        elif layer is L2X:
                            for c in range(2):
                                last = mm(o[:, c * P:(c + 1) * P], pT[:, t, c, :],
                                          v_rope(g.par)[:, 2 * t:2 * t + 2, :])
                        else:
                            for c in range(8):
                                last = mm(o[:, c * 32:(c + 1) * 32], pT[:, t, c, :],
                                          v_small(g.par)[:, 2 * t:2 * t + 2, c, :])
                        last.then_inc(filled[b], 1)
                elif kind == "X":
                    t = item[1]
                    wait_drained(ring, g, layer.use(("A", t)))
                    b = take(ring, g, u)
                    nc.tensor.transpose(bank(b)[:, 0:P], o_sb[:, t, :], ident).then_inc(filled[b], 1)
                elif kind == "W":
                    t = item[1]
                    chunks = 8 if layer in (L0X, L3X) else 1
                    if chunks == 8:
                        for v in range(layer.uses["A"]):
                            wait_drained(ring, g, layer.use(("A", t)) + v)
                    else:
                        wait_drained(ring, g, layer.use(("X", t)))
                    b = take(ring, g, u)
                    for c in range(chunks):
                        last = mm(bank(b)[:, 0:D], oT[:, t, c, :], w(layer.name + "_wo")[:, c * D:(c + 1) * D],
                                  start=c == 0, stop=c == chunks - 1)
                    last.then_inc(filled[b], 1)
                elif kind == "U":
                    e, c = item[1:]
                    if item == ("U", 0, 0):
                        pe.wait_ge(s_xlo.sem, s_xlo.after(g, 0))
                    if c == 0 and first_of(g):
                        pe.wait_ge(s_lo, 8 * (layer is L2F) + e + 1)
                    b = take(ring, g, u)
                    r0, n = HID1[c] if layer is L1F else (2 * c * P, P)
                    for i in range(2):
                        a = r0 + i * (I_FF if layer is L1F else P)
                        hi, lo = (as_r(v(layer, e)[:, a:a + n]) for v in (up_hi, up_lo))
                        o = bank(b)[0:n, i * GT:(i + 1) * GT]
                        mm(o, hi, as_r(xhi[:, g.par, :]), stop=False)
                        mm(o, hi, as_r(xlo[:, g.par, :]), start=False, stop=False)
                        last = mm(o, lo, as_r(xhi[:, g.par, :]), start=False)
                    last.then_inc(filled[b], 1)
                elif kind == "D":
                    e = item[1]
                    nch = 3 if layer is L1F else 4
                    for c in range(nch if layer is L1F else 2):
                        wait_drained(ring, g, layer.use(("U", e, c)))
                    b = take(ring, g, u)
                    for t in range(TPG):
                        for c in range(nch):
                            if layer is L1F:
                                n = HID1[c][1]
                                a = 2 * I_FF + c * D
                                rhs = w1_expert(e)[0:n, a:a + D]
                            else:
                                n = P
                                a = e * EXPERT2 + FFN2 + c * D
                                rhs = w2_sb[:, a:a + D]
                            last = mm(bank(b)[:, t * D:(t + 1) * D],
                                      qT[0:n, e % 2, c, t * P:(t + 1) * P], rhs, start=c == 0, stop=c == nch - 1)
                    last.then_inc(filled[b], 1)
                elif kind == "KF":
                    pe.wait_ge(s_mix.sem, s_mix.after(g, 5))
                    b = take(ring, g, u)
                    mm(bank(b)[:, 0:GT], w("l3f_wk"), qT[:, g.par, 1, :]).then_inc(filled[b], 1)
                elif kind == "RF":
                    b = take(ring, g, u)
                    for t in range(TPG):
                        last = mm(bank(b)[:, t * D:(t + 1) * D], qT[:, g.par, 0, t * P:(t + 1) * P], w("l3f_wr"))
                    last.then_inc(filled[b], 1)
                elif kind == "VF":
                    pe.wait_ge(s_relu.sem, s_relu.after(g, 0))
                    b = take(ring, g, u)
                    for t in range(TPG):
                        last = mm(bank(b)[:, t * D:(t + 1) * D], qT[:, g.par, 3, t * P:(t + 1) * P], w("l3f_wv"))
                    last.then_inc(filled[b], 1)

            traverse(pe, do, start)

        @block.scalar
        def _(act):
            def wait_filled(ring, g, u):
                b = ring.bank(g, u)
                act.wait_ge(filled[b], ring.count(g, u))
                return b

            def wait_drained(ring, g, u):
                act.wait_ge(drained[ring.bank(g, u)], ring.count(g, u))

            def start(layer):
                if layer is L0X:
                    act.wait_ge(s_small, 16)
                    act.wait_ge(s_const, 5)
                    nc.scalar.activation(tgate[:, :], w("gates"), ACT.Tanh).then_inc(s_tanh, 1)
                if layer is L1X:
                    act.wait_ge(s_mask, 1)
                    nc.scalar.dma_start(w1_sb[:, 0:E_FF1 * EXPERT1], w1_in).then_inc(s_w1, 16)
                    for b in L0F.body_banks:
                        act.wait_ge(drained[b], bank_base[2][b])
                    nc.scalar.dma_start(small[:, LATE_AT:LATE_AT + 1024 * len(LATE)], late_in).then_inc(s_late, 16)
                if layer is L2X:
                    for b in L1F.body_banks:
                        act.wait_ge(drained[b], bank_base[4][b])
                    nc.scalar.dma_start(w2_sb[:, :], w2_in).then_inc(s_w2, 16)
                    act.wait_ge(s_scale, 1)
                    act.wait_ge(s_zero, 4)
                if layer is L0F:
                    act.wait_ge(s_zero, 2)
                    act.wait_ge(s_rest, 16)
                if layer in (L1F, L2F):
                    for b in layers[layer.n - 1].body_banks:
                        act.wait_ge(drained[b], bank_base[layer.n][b])
                    if layer is L1F:
                        act.wait_ge(s_w1, 16)
                    else:
                        act.wait_ge(s_w2, 16)
                    for e in range(8):
                        nc.scalar.activation(as_r(up_hi(layer, e)), up_full(layer, e), ACT.Copy).then_inc(s_hi, 1)
                if layer is L3X:
                    act.wait_ge(s_zero, 7)

            def do(layer, item, g):
                ring, fr = layer.body_ring, layer.front_ring
                kind = item[0]
                if kind in ("L", "M", "H", "N", "S"):
                    return
                u = layer.use(item) if kind != "P" else None
                if kind == "F":
                    b = wait_filled(fr, g, u)
                    if layer is L2X:
                        nc.scalar.activation(xcT[:, g.par, :], bank(b), ACT.Identity,
                                             scale=rms_gain[:, 0:1]).then_inc(drained[b], 1)
                    elif layer in (L1F, L2F):
                        nc.scalar.activation(xcT[:, g.par, 0:GT], bank(b, GT), ACT.Copy)
                        nc.scalar.activation(as_r(xhi[:, g.par, :]), bank(b, GT), ACT.Copy).then_inc(drained[b], 1)
                    else:
                        nc.scalar.activation(xcT[:, g.par, 0:GT], bank(b, GT), ACT.Copy).then_inc(drained[b], 1)
                elif kind == "Q" and layer is not L2X:
                    b = wait_filled(fr, g, u)
                    j = item[1]
                    nc.scalar.activation(qT[:, g.par, 2 * j:2 * j + 2, :].rearrange("p c t -> p (c t)"), bank(b),
                                         ACT.Copy).then_inc(drained[b], 1)
                elif kind == "QK":
                    b = wait_filled(fr, g, u)
                    act.wait_ge(s_kspread.sem(g.back(2)), s_kspread.all(g.back(2)))
                    nc.scalar.activation(qT[:, g.par, 0, :], bank(b, GT), ACT.Identity,
                                         bias=w(layer.name + "_bq"))
                    nc.scalar.activation(kT[:, g.par, :], bank(b)[:, GT:2 * GT], ACT.Identity,
                                         bias=w(layer.name + "_bk")).then_inc(drained[b], 1)
                elif kind == "V" and layer in (L0X, L3X):
                    b = wait_filled(fr, g, u)
                    j = item[1]
                    for half in range(2):
                        rows = slice(half * S, (half + 1) * S)
                        if layer is L3X:
                            o = v_pairs(layer, g.par)[rows, j, :, half * S:(half + 1) * S]
                            i = bank(b)[rows, :].rearrange("p (c k) -> p c k", k=S)
                        else:
                            o = v_pairs(layer, g.par)[rows, :, 0:2, half * S:(half + 1) * S]
                            i = bank(b)[rows, :].rearrange("p (q c k) -> p q c k", c=2, k=S)
                        last = nc.scalar.activation(o, i, ACT.Copy)
                    last.then_inc(drained[b], 1)
                elif kind == "V" and layer is L1X:
                    b = wait_filled(fr, g, u)
                    for half in range(2):
                        rows = slice(half * S, (half + 1) * S)
                        last = nc.scalar.activation(v_small(g.par)[rows, :, :, half * 8:(half + 1) * 8],
                                                    bank(b)[rows, 0:BPG * 64].rearrange("p (q c d) -> p q c d", c=8, d=8),
                                                    ACT.Copy)
                    last.then_inc(drained[b], 1)
                elif kind == "V" and layer is L2X:
                    b = wait_filled(fr, g, u)
                    for half in range(2):
                        rows = slice(half * S, (half + 1) * S)
                        last = nc.scalar.activation(v_rope(g.par)[rows, :, half * 32:(half + 1) * 32],
                                                    bank(b)[rows, 0:BPG * 32].rearrange("p (q d) -> p q d", d=32),
                                                    ACT.Copy)
                    last.then_inc(drained[b], 1)
                elif kind == "C":
                    b = wait_filled(fr, g, u)
                    nc.scalar.activation(combT[:, g.par, :], bank(b, GT)[0:8, :], ACT.Copy).then_inc(drained[b], 1)
                elif kind == "P" and layer is L0F:
                    t = item[1]
                    act.wait_ge(s_sub.sem, s_sub.after(g, t))
                    act.wait_ge(s_rv.sem, s_rv.after(g.back(1), t))
                    b = layer.score_ring.bank(g, t)
                    for h in range(layer.heads):
                        last = nc.scalar.activation(probs[:, g.par, t, h * S:(h + 1) * S],
                                                    score_bank(b)[:, h * S:(h + 1) * S], ACT.Exp,
                                                    bias=negmax[:, t, h:h + 1], scale=layer.scale,
                                                    accum_out=sm[:, t, h:h + 1])
                    last.then_inc(drained[b], 1)
                elif kind == "P":
                    t = item[1]
                    if layer in (L1X, L2X):
                        act.wait_ge(s_sub.sem, s_sub.after(g, t))
                    else:
                        wait_drained(layer.score_ring, g, t)
                    pr = probs[:, g.par, t, 0:layer.heads * S]
                    nc.scalar.activation(pr, pr, ACT.Exp, scale=layer.scale).then_inc(s_exp.sem, 1)
                elif kind == "T":
                    t = item[1]
                    for j in range(layer.uses["T"]):
                        b = wait_filled(ring, g, u + j)
                        n = min(4, layer.heads * S // P)
                        nc.scalar.activation(pT[:, t, 4 * j:4 * j + n, :].rearrange("p c t -> p (c t)"),
                                             bank(b, n * P), ACT.Copy).then_inc(drained[b], 1)
                elif kind == "A" and layer in (L0X, L3X):
                    t = item[1]
                    for j in range(2):
                        b = wait_filled(ring, g, u + j)
                        if layer is L0X:
                            o = oT[:, t, 4 * j:4 * j + 4, :].rearrange("p i (b q) -> p b i q", b=2)
                            i = bank(b).rearrange("p (b i q) -> p b i q", b=2, i=4)
                        else:
                            o = oT[:, t, 4 * j:4 * j + 4, :].rearrange("p c t -> p (c t)")
                            i = bank(b)
                        nc.scalar.activation(o, i, ACT.Copy).then_inc(drained[b], 1)
                elif kind == "X":
                    t = item[1]
                    b = wait_filled(ring, g, u)
                    nc.scalar.activation(oT[:, t, 0, :], bank(b, P), ACT.Copy).then_inc(drained[b], 1)
                elif kind == "U" and layer is L1F:
                    e, c = item[1:]
                    n = HID1[c][1]
                    b = wait_filled(ring, g, u)
                    k = 3 * e + c
                    before = up_stages[k - 2]
                    gb = g if k >= 2 else g.back(1)
                    wait_drained(ring, gb, layer.use(before))
                    nc.scalar.activation(silu_buf(k)[0:n, :], bank(b)[0:n, 0:GT], ACT.Silu).then_inc(s_act.sem, 1)
                elif kind == "U":
                    e, c = item[1:]
                    b = wait_filled(ring, g, u)
                    nc.scalar.activation(qT[:, e % 2, 2 * c:2 * c + 2, :].rearrange("p c t -> p (c t)"), bank(b),
                                         ACT.Gelu).then_inc(drained[b], 1)
                elif kind == "RF":
                    b = wait_filled(ring, g, u)
                    act.wait_ge(s_upd.sem, s_upd.after(g.back(2), 0))
                    nc.scalar.activation(acc[:, g.par, :, :].rearrange("p t d -> p (t d)"), bank(b, GT),
                                         ACT.Sigmoid).then_inc(drained[b], 1)

            up_stages = [i for i, _ in L1F.order if i[0] == "U"]
            traverse(act, do, start)

        @block.vector
        def _(dve):
            def wait_filled(ring, g, u):
                b = ring.bank(g, u)
                dve.wait_ge(filled[b], ring.count(g, u))
                return b

            def xt(g, t):
                return x_sb[:, bass.ds(g.tile(t), 1), :].rearrange("p a d -> p (a d)")

            def start(layer):
                if layer is not L0X:
                    dve.wait_ge(s_upd.sem, s_upd.base[layer.n])
                    for b in layers[layer.n - 1].body_banks:
                        dve.wait_ge(drained[b], bank_base[layer.n][b])
                if layer is L0X:
                    dve.wait_ge(s_x0, 16)
                    dve.wait_ge(s_small, 16)
                    dve.wait_ge(s_const, 5)
                    dve.wait_ge(s_tanh, 1)
                if layer in (L0F, L3X):
                    dve.memset(arena_a[:, 4096:8192], 0.0).then_inc(s_zero, 1)
                if layer is L0F:
                    dve.wait_ge(s_zero, 2)
                    dve.wait_ge(s_rest, 16)
                    dve.tensor_scalar(rms_gain[:, :], w("l2x_scale"), 1.0, None, ALU.add).then_inc(s_scale, 1)
                    for i, mu in enumerate(("l3f_mur", "l3f_muk")):
                        dve.tensor_scalar(onemu[:, i:i + 1], w(mu), -1.0, 1.0, ALU.mult, ALU.add).then_inc(s_onemu, 1)
                    dve.wait_ge(s_onemu, 2)
                if layer is L1X:
                    dve.wait_ge(s_m1, 32)
                    dve.tensor_scalar(masked[:, :, :], mask_staged(), 1.0, None, ALU.not_equal).then_inc(s_mask, 1)
                    dve.wait_ge(s_mask, 1)
                if layer is L2X:
                    dve.wait_ge(s_m2, 32)
                    dve.wait_ge(s_zero, 4)
                    dve.tensor_scalar(masked[:, :, :], masked[:, :, :], 0.0, None, ALU.is_equal).then_inc(s_mask, 1)
                    dve.wait_ge(s_mask, 2)
                if layer is L3X:
                    dve.wait_ge(s_zero, 7)
                if layer in (L1F, L2F):
                    for e in range(8):
                        dve.wait_ge(s_hi, 8 * (layer is L2F) + e + 1)
                        dve.tensor_tensor(as_r(up_lo(layer, e)), up_full(layer, e), up_hi(layer, e),
                                          ALU.subtract).then_inc(s_lo, 1)

            def statistics(layer, g):
                rms = layer is L2X
                dve.wait_ge(s_xn.sem, s_xn.after(g.back(1), 3 if rms else 1))
                if rms:
                    dve.wait_ge(s_ctx.sem(g), s_ctx.all(g))
                for t in range(TPG):
                    dve.bn_stats(st[:, t, :], xt(g, t)).then_inc(s_stats.sem, 1)
                if rms:
                    for t in range(TPG):
                        dve.bn_stats(st[:, 2 + t, :], ctx_sb[:, g.par, t, :]).then_inc(s_stats.sem, 1)
                n = 4 if rms else 2
                me, mo, ve, vo = (st[:, 0:n, i] for i in (1, 4, 2, 5))
                total, diff, within = (agg[:, i, 0:n] for i in range(3))
                dve.wait_ge(s_stats.sem, s_stats.after(g, n - 1))
                dve.tensor_tensor(total, me, mo, ALU.add).then_inc(s_aggr.sem, 1)
                dve.tensor_tensor(diff, me, mo, ALU.subtract).then_inc(s_aggr.sem, 1)
                dve.tensor_tensor(within, ve, vo, ALU.add).then_inc(s_aggr.sem, 1)
                dve.wait_ge(s_aggr.sem, s_aggr.after(g, 1))
                dve.tensor_tensor(agg[:, 3, 0:n], diff, diff, ALU.mult).then_inc(s_aggr.sem, 1)
                dve.tensor_scalar(mv[:, 0:n, 0], total, 0.5, None, ALU.mult).then_inc(s_aggr.sem, 1)
                dve.wait_ge(s_aggr.sem, s_aggr.after(g, 3))
                dve.scalar_tensor_tensor(out=agg[:, 4, 0:n], in0=agg[:, 3, 0:n], scalar=D / 4, in1=within,
                                         op0=ALU.mult, op1=ALU.add).then_inc(s_aggr.sem, 1)
                dve.wait_ge(s_aggr.sem, s_aggr.after(g, 5))
                dve.tensor_scalar(mv[:, 0:n, 1], agg[:, 4, 0:n], 1.0 / D, None, ALU.mult).then_inc(s_aggr.sem, 1)
                dve.wait_ge(s_aggr.sem, s_aggr.after(g, 6))
                if rms:
                    dve.tensor_scalar(veps[:, 0:2], mv[:, 0:2, 1], 1.0 + RMS_EPS, RMS_EPS * LN_EPS,
                                      ALU.mult, ALU.add).then_inc(s_veps.sem, 1)
                    dve.tensor_tensor(veps[:, 2:4], mv[:, 2:4, 0], mv[:, 2:4, 0], ALU.mult).then_inc(s_veps.sem, 1)
                    dve.wait_ge(s_veps.sem, s_veps.after(g, 1))
                    dve.scalar_tensor_tensor(out=veps[:, 2:4], in0=mv[:, 2:4, 1], scalar=RMS_EPS,
                                             in1=veps[:, 2:4], op0=ALU.add, op1=ALU.add).then_inc(s_veps.sem, 1)
                else:
                    dve.tensor_scalar(veps[:, 0:2], mv[:, 0:2, 1], LN_EPS, None, ALU.add).then_inc(s_veps.sem, 1)

            def normalise(layer, g):
                dve.wait_ge(s_rstd.sem, s_rstd.after(g, 0))
                wait_drained(layer.front_ring, g.back(2), 0)
                for t in range(TPG):
                    dve.tensor_scalar(xn[:, g.par, t, :], xt(g, t), mv[:, t, 0:1], rstd[:, t:t + 1],
                                      ALU.subtract, ALU.mult).then_inc(s_xn.sem, 1)
                if layer is L2X:
                    for t in range(TPG):
                        dve.tensor_scalar(ctxn[:, g.par, t, :], ctx_sb[:, g.par, t, :], rstd[:, 2 + t:3 + t], None,
                                          ALU.mult).then_inc(s_xn.sem, 1)

            def wait_drained(ring, g, u):
                dve.wait_ge(drained[ring.bank(g, u)], ring.count(g, u))

            def routing(layer, g, b):
                ne = layer.experts
                n = TPG * ne
                r = lambda k: route[:, k, 0:n].rearrange("p (t e) -> p t e", e=ne)
                k = [0]

                def chain(ins):
                    ins.then_inc(s_route.sem, 1)
                    dve.wait_ge(s_route.sem, s_route.after(g, k[0]))
                    k[0] += 1

                bc = lambda ap: ap.unsqueeze(2).to_broadcast([P, TPG, ne])
                bg = w(layer.name + "_bg").unsqueeze(1).to_broadcast([P, TPG, ne])
                if b is not None:
                    dve.tensor_tensor(r(0), bank(b, n).rearrange("p (t e) -> p t e", e=ne), bg,
                                      ALU.add).then_inc(drained[b], 1)
                    wait_drained(layer.front_ring, g, layer.use(("G", 0)))
                    if layer is L2F:
                        chain(dve.tensor_scalar(r(0), r(0), -1.0, None, ALU.mult))
                    else:
                        chain(dve.tensor_reduce(route[:, 4, 0:TPG], r(0), AX_X, ALU.max))
                        chain(dve.tensor_tensor(r(0), r(0), bc(route[:, 4, 0:TPG]), ALU.subtract))
                    return
                k[0] = 1 if layer is L2F else 2
                if layer is L2F:
                    dve.wait_ge(s_rexp.sem, s_rexp.after(g, 0))
                    chain(dve.tensor_scalar(r(2), r(1), 1.0, None, ALU.add))
                    chain(dve.reciprocal(r(3), r(2)))
                else:
                    dve.wait_ge(s_rexp.sem, s_rexp.after(g, 0))
                    chain(dve.tensor_reduce(route[:, 4, 0:TPG], r(1), AX_X, ALU.add))
                    chain(dve.reciprocal(route[:, 5, 0:TPG], route[:, 4, 0:TPG]))
                    chain(dve.tensor_tensor(r(3), r(1), bc(route[:, 5, 0:TPG]), ALU.mult))
                gt = cmp_gt[:, :, 0:ne, 0:ne]
                eq = cmp_eq[:, :, 0:ne, 0:ne]
                other = r(3).unsqueeze(2).to_broadcast([P, TPG, ne, ne])
                own = r(3).unsqueeze(3).to_broadcast([P, TPG, ne, ne])
                tri = w("earlier").rearrange("p (e f) -> p e f", f=8)[:, 0:ne, 0:ne]
                dve.tensor_tensor(gt, other, own, ALU.is_gt)
                chain(dve.tensor_tensor(eq, other, own, ALU.is_equal))
                chain(dve.tensor_tensor(eq, eq, tri.unsqueeze(1).to_broadcast([P, TPG, ne, ne]), ALU.mult))
                chain(dve.tensor_tensor(gt, gt, eq, ALU.add))
                dve.tensor_reduce(r(6), gt, AX_X, ALU.add).then_inc(s_rank.sem, 1)
                dve.wait_ge(s_rank.sem, s_rank.after(g, 0))
                last = dve.scalar_tensor_tensor(out=comb[:, g.par, :, 0:ne], in0=r(6), scalar=float(layer.top),
                                                in1=r(3), op0=ALU.is_lt, op1=ALU.mult)
                if layer is L1F:
                    chain(last)
                    cw = comb[:, g.par, :, 0:ne]
                    chain(dve.tensor_reduce(route[:, 4, 0:TPG], cw, AX_X, ALU.add))
                    chain(dve.reciprocal(route[:, 5, 0:TPG], route[:, 4, 0:TPG]))
                    chain(dve.tensor_tensor(cw, cw, bc(route[:, 5, 0:TPG]), ALU.mult))
                else:
                    chain(last)
                assert k[0] == s_route.per[layer.name], (layer.name, k[0])

            def softmax(layer, g, t):
                nh = layer.heads
                b = wait_filled(layer.score_ring, g, t)
                sc = score_bank(b)[:, 0:nh * S].rearrange("p (h k) -> p h k", k=S)
                pr = probs[:, g.par, t, 0:nh * S].rearrange("p (h k) -> p h k", k=S)
                m = mx[:, t, 0:nh]
                mb = m.unsqueeze(2).to_broadcast([P, nh, S])
                back, ut = g.back(2), layer.use(("T", t))
                if layer is not L0F:
                    for v in range(layer.uses["T"]):
                        wait_drained(layer.body_ring, back, ut + v)
                if layer in (L1X, L2X):
                    fill = F32_MIN if layer is L1X else MASK_FILL
                    mk = masked[:, bass.ds(g.tile(t), 1), :].to_broadcast([P, nh, S])
                    dve.scalar_tensor_tensor(out=pr, in0=mk, scalar=fill, in1=sc,
                                             op0=ALU.mult, op1=ALU.add).then_inc(drained[b], 1)
                    wait_drained(layer.score_ring, g, t)
                    dve.tensor_reduce(m, pr, AX_X, ALU.max).then_inc(s_mx.sem, 1)
                    dve.wait_ge(s_mx.sem, s_mx.after(g, t))
                    dve.tensor_tensor(pr, pr, mb, ALU.subtract).then_inc(s_sub.sem, 1)
                elif layer is L0F:
                    wait_drained(layer.score_ring, g.back(1), t)
                    dve.tensor_reduce(m, sc, AX_X, ALU.max).then_inc(s_mx.sem, 1)
                    dve.wait_ge(s_mx.sem, s_mx.after(g, t))
                    dve.tensor_scalar(negmax[:, t, :], m, -layer.scale, None, ALU.mult).then_inc(s_sub.sem, 1)
                else:
                    dve.tensor_reduce(m, sc, AX_X, ALU.max).then_inc(s_mx.sem, 1)
                    dve.wait_ge(s_mx.sem, s_mx.after(g, t))
                    dve.tensor_tensor(pr, sc, mb, ALU.subtract).then_inc(drained[b], 1)

            def softmax_sum(layer, g, t):
                nh = layer.heads
                pr = probs[:, g.par, t, 0:nh * S].rearrange("p (h k) -> p h k", k=S)
                if layer is L0F:
                    wait_drained(layer.score_ring, g, t)
                    dve.reciprocal(rv[:, t, 0:nh], sm[:, t, 0:nh]).then_inc(s_rv.sem, 1)
                    return
                dve.wait_ge(s_exp.sem, s_exp.after(g, t))
                dve.tensor_reduce(sm[:, t, 0:nh], pr, AX_X, ALU.add).then_inc(s_sum.sem, 1)
                dve.wait_ge(s_sum.sem, s_sum.after(g, t))
                dve.reciprocal(rv[:, t, 0:nh], sm[:, t, 0:nh]).then_inc(s_rv.sem, 1)

            def residual(layer, g, t, src, extra=None):
                return dve.scalar_tensor_tensor(out=xt(g, t), in0=src, scalar=tgate[:, layer.n:layer.n + 1],
                                                in1=xt(g, t), op0=ALU.mult, op1=ALU.add)

            def do(layer, item, g):
                ring, fr = layer.body_ring, layer.front_ring
                kind = item[0]
                u = layer.use(item) if kind not in ("L", "M", "H", "S", "P", "N") else None
                if kind == "L":
                    if layer is L0X and type(g.pair) is int and (g.pair, g.par) == (1, 0):
                        dve.wait_ge(s_x, 16)
                    statistics(layer, g)
                elif kind == "M":
                    normalise(layer, g)
                elif kind == "F" and layer is L3F:
                    mix(g)
                elif kind == "F":
                    if layer in (L1F, L2F):
                        dve.wait_ge(drained[fr.bank(g, u)], fr.count(g, u))
                        dve.tensor_tensor(as_r(xlo[:, g.par, :]), xcT[:, g.par, 0:GT], xhi[:, g.par, :],
                                          ALU.subtract).then_inc(s_xlo.sem, 1)
                elif kind == "N":
                    softmax_sum(layer, g, item[1])
                elif kind == "H":
                    routing(layer, g, None)
                elif kind == "K" and layer is not L2X:
                    b = wait_filled(fr, g, u)
                    j = item[1]
                    for half in range(2):
                        rows = slice(half * S, (half + 1) * S)
                        last = dve.tensor_copy(k_pairs(layer, g.par)[rows, 2 * j:2 * j + 2, :, half * S:(half + 1) * S],
                                               bank(b)[rows, :].rearrange("p (c q k) -> p c q k", c=2, k=S))
                    last.then_inc(drained[b], 1)
                elif kind in ("Q", "K") and layer is L2X:
                    b = wait_filled(fr, g, u)
                    at = 0 if kind == "Q" else 2
                    tab = w("rope").rearrange("p (n s) -> p n s", s=S)
                    cos = tab[:, at, :].unsqueeze(1).to_broadcast([P, BPG, S])
                    sin = tab[:, at + 1, :].unsqueeze(1).to_broadcast([P, BPG, S])
                    v = lambda ap: ap.rearrange("p (b s) -> p b s", s=S)
                    n = 0 if kind == "Q" else 2
                    c1 = v(qT[:, g.par, n + 2, :])
                    c2 = v(qT[:, g.par, n + 3, :])
                    dve.tensor_tensor(c1, v(bank(b, GT)), cos, ALU.mult).then_inc(s_rope.sem, 1)
                    dve.tensor_tensor(c2, v(bank(b)[:, GT:2 * GT]), sin, ALU.mult).then_inc(s_rope.sem, 1)
                    dve.wait_ge(s_rope.sem, s_rope.after(g, n + 1))
                    if kind == "Q":
                        dve.tensor_tensor(v(qT[:, g.par, 0, :]), c1, c2, ALU.add).then_inc(drained[b], 1)
                    else:
                        for h in range(4):
                            r0 = 32 * h
                            last = dve.tensor_tensor(k_rope(g.par)[r0:r0 + 32, :, h * S:(h + 1) * S],
                                                     c1[r0:r0 + 32], c2[r0:r0 + 32], ALU.add)
                        last.then_inc(drained[b], 1)
                elif kind == "V" and layer is L0F:
                    b = wait_filled(fr, g, u)
                    for half in range(2):
                        rows = slice(half * S, (half + 1) * S)
                        bv = w(layer.name + "_bv")[rows, :].rearrange("p (c d) -> p c d", d=8)
                        last = dve.tensor_tensor(v_small(g.par)[rows, :, :, half * 8:(half + 1) * 8],
                                                 bank(b)[rows, 0:BPG * 64].rearrange("p (q c d) -> p q c d", c=8, d=8),
                                                 bv.unsqueeze(1).to_broadcast([S, BPG, 8, 8]), ALU.add)
                    last.then_inc(drained[b], 1)
                elif kind == "G":
                    routing(layer, g, wait_filled(fr, g, u))
                elif kind == "S":
                    softmax(layer, g, item[1])
                elif kind == "A" and layer in (L0F, L1X, L2X):
                    t = item[1]
                    b = wait_filled(ring, g, u)
                    e = 16 if layer is not L2X else 64
                    c = 8 if layer is not L2X else 2
                    src = bank(b, c * 2 * e).rearrange("p (c b e) -> p c b e", b=2, e=e)
                    if layer is L0F:
                        wait_drained(fr, g, layer.use(("Z", t)))
                    for half in range(2):
                        rows = slice(half * S, (half + 1) * S)
                        o = o_sb[rows, t, :].rearrange("p (c e) -> p c e", e=e)
                        if layer is L0F:
                            moe = acc[rows, g.par, t, :].rearrange("p (c e) -> p c e", e=e)
                            last = dve.tensor_tensor(o, src[rows, :, half, :], moe, ALU.add)
                        elif layer is L1X:
                            bv = w("l1x_bv")[rows, :].rearrange("p (c e) -> p c e", e=e)
                            last = dve.tensor_tensor(o, src[rows, :, half, :], bv, ALU.add)
                        else:
                            last = dve.tensor_copy(o, src[rows, :, half, :])
                    last.then_inc(drained[b], 1)
                    if layer is L0F:
                        wait_drained(ring, g, u)
                        residual(layer, g, t, o_sb[:, t, :]).then_inc(s_upd.sem, 1)
                elif kind == "E":
                    t, j = item[1:]
                    if j == 0:
                        dve.wait_ge(s_upd.sem, s_upd.after(g.back(2), t))
                    a = acc[:, g.par, t, :]
                    b = wait_filled(fr, g, u)
                    for i in range(4):
                        e = 4 * j + i
                        src, cw = bank(b)[:, i * D:(i + 1) * D], comb[:, g.par, t, e:e + 1]
                        if e == 0:
                            add = dve.tensor_scalar(a, src, cw, None, ALU.mult)
                        else:
                            add = dve.scalar_tensor_tensor(out=a, in0=src, scalar=cw, in1=a,
                                                           op0=ALU.mult, op1=ALU.add)
                        if i < 3:
                            add.then_inc(s_acc.sem, 1)
                            dve.wait_ge(s_acc.sem, s_acc.after(g, 6 * t + 3 * j + i))
                        else:
                            add.then_inc(drained[b], 1)
                            wait_drained(fr, g, u)
                elif kind == "Z":
                    t = item[1]
                    b = wait_filled(fr, g, u)
                    a = acc[:, g.par, t, :]
                    dve.tensor_tensor(a, bank(b, D), a, ALU.add).then_inc(drained[b], 1)
                elif kind == "W":
                    t = item[1]
                    b = wait_filled(ring, g, u)
                    if layer is L1X:
                        dve.tensor_tensor(acc[:, g.par, t, :], bank(b, D), w("l1x_bo"), ALU.add).then_inc(drained[b], 1)
                        wait_drained(ring, g, u)
                        residual(layer, g, t, acc[:, g.par, t, :]).then_inc(s_upd.sem, 1)
                    else:
                        residual(layer, g, t, bank(b, D)).then_inc(drained[b], 1)
                elif kind == "U" and layer is L1F:
                    e, c = item[1:]
                    n = HID1[c][1]
                    b = ring.bank(g, u)
                    k = 3 * e + c
                    dve.wait_ge(s_act.sem, s_act.after(g, k))
                    dve.tensor_tensor(qT[0:n, e % 2, c, :], silu_buf(k)[0:n, :], bank(b)[0:n, GT:2 * GT],
                                      ALU.mult).then_inc(drained[b], 1)
                elif kind == "D":
                    e = item[1]
                    b = wait_filled(ring, g, u)
                    if layer is L1F and e == 0:
                        dve.tensor_copy(acc[:, g.par, :, :].rearrange("p t d -> p (t d)"), bank(b, GT)).then_inc(drained[b], 1)
                    else:
                        r = e - 1 if layer is L1F else e
                        for t in range(TPG):
                            src = bank(b)[:, t * D:(t + 1) * D]
                            if e == 0:
                                last = dve.tensor_scalar(acc[:, g.par, t, :], src, comb[:, g.par, t, r:r + 1], None, ALU.mult)
                            else:
                                last = dve.scalar_tensor_tensor(out=acc[:, g.par, t, :], in0=src,
                                                                scalar=comb[:, g.par, t, r:r + 1], in1=acc[:, g.par, t, :],
                                                                op0=ALU.mult, op1=ALU.add)
                        last.then_inc(drained[b], 1)
                    wait_drained(ring, g, u)
                    if e == 7:
                        xg = x_sb[:, bass.ds(g.tile(0), TPG), :]
                        dve.scalar_tensor_tensor(out=xg, in0=acc[:, g.par, :, :], scalar=tgate[:, layer.n:layer.n + 1],
                                                 in1=xg, op0=ALU.mult, op1=ALU.add).then_inc(s_upd.sem, 1)
                elif kind == "KF":
                    b = wait_filled(ring, g, u)
                    dve.tensor_scalar(qT[:, g.par, 2, :], bank(b, GT), 0.0, None, ALU.max).then_inc(drained[b], 1)
                    wait_drained(ring, g, u)
                    dve.tensor_tensor(qT[:, g.par, 3, :], qT[:, g.par, 2, :], qT[:, g.par, 2, :],
                                      ALU.mult).then_inc(s_relu.sem, 1)
                elif kind == "VF":
                    b = wait_filled(ring, g, u)
                    wait_drained(ring, g, layer.use(("RF", 0)))
                    a = acc[:, g.par, :, :]
                    dve.tensor_tensor(a, bank(b, GT).rearrange("p (t d) -> p t d", d=D), a, ALU.mult)\
                        .then_inc(drained[b], 1)
                    wait_drained(ring, g, u)
                    xg = x_sb[:, bass.ds(g.tile(0), TPG), :]
                    dve.scalar_tensor_tensor(out=xg, in0=a, scalar=tgate[:, layer.n:layer.n + 1],
                                             in1=xg, op0=ALU.mult, op1=ALU.add).then_inc(s_upd.sem, 1)

            def mix(g):
                wait_drained(L3F.front_ring, g, 0)
                wait_drained(L3F.body_ring, g.back(2), 2)
                v = lambda ap: ap.rearrange("p (b s) -> p b s", s=S)
                xT = v(xcT[:, g.par, 0:GT])
                for i, mu in enumerate(("l3f_mur", "l3f_muk")):
                    m = w(mu)
                    o = v(qT[:, g.par, i, :])
                    prev = v(qT[:, g.par, 4 + i, :])
                    dve.tensor_scalar(prev, xT, onemu[:, i:i + 1], None, ALU.mult).then_inc(s_mix.sem, 1)
                    dve.tensor_scalar(o[:, :, 0:1], xT[:, :, 0:1], m, None, ALU.mult).then_inc(s_mix.sem, 1)
                    dve.wait_ge(s_mix.sem, s_mix.after(g, 3 * i))
                    dve.scalar_tensor_tensor(out=o[:, :, 1:S], in0=xT[:, :, 1:S], scalar=m, in1=prev[:, :, 0:S - 1],
                                             op0=ALU.mult, op1=ALU.add).then_inc(s_mix.sem, 1)

            traverse(dve, do, start)


def _pack_small(np, a):
    def rows(v, n=P):
        return np.broadcast_to(v[None, :], (n, v.shape[0]))

    def col(v):
        return v[:, None]

    def value_cols(wt):
        d = wt.shape[1] // 16
        return wt.reshape(D, 8, 2, d).transpose(0, 2, 1, 3).reshape(D, -1)

    def value_bias(v):
        v = v.reshape(8, 2, 8)
        return np.concatenate([rows(v[:, 0].reshape(-1), S), rows(v[:, 1].reshape(-1), S)], 0)

    def swapped(wt):
        h = wt.shape[1] // ROPE_D
        return wt.reshape(D, h, 2, ROPE_D // 2)[:, :, ::-1].reshape(D, -1)

    def down(wt):
        n = -(-wt.shape[0] // P)
        full = np.zeros((n * P, D), np.float32)
        full[:wt.shape[0]] = wt
        return full.reshape(n, P, D).transpose(1, 0, 2).reshape(P, n * D)

    p = {}
    p["l0x_wq"] = a["L0_xattn_Wq"].reshape(2, 2, 4, 64, D).transpose(4, 0, 2, 1, 3).reshape(D, 1024)
    p["l0x_wk"] = a["L0_xattn_Wk"].T
    p["l0x_wv"] = a["L0_xattn_Wv"].T.reshape(D, 2, 2, 64).transpose(0, 2, 1, 3).reshape(D, 256)
    p["l0x_wo"] = a["L0_xattn_Wo"].reshape(D, 2, 2, 4, 64).transpose(2, 4, 1, 3, 0).reshape(P, 1024)
    qkv, bqkv = a["L0_ffn_W_qkv"], a["L0_ffn_b_qkv"]
    p["l0f_wq"], p["l0f_wk"], p["l0f_wv"] = qkv[:, :D], qkv[:, D:2 * D], value_cols(qkv[:, 2 * D:])
    p["l0f_bq"], p["l0f_bk"], p["l0f_bv"] = col(bqkv[:D]), col(bqkv[D:2 * D]), value_bias(bqkv[2 * D:])
    p["l0f_wg"], p["l0f_bg"] = a["L0_ffn_W_gate"], rows(a["L0_ffn_b_gate"])
    p["l0f_we"] = a["L0_ffn_W_experts"].transpose(1, 0, 2).reshape(D, 1024)
    be = np.zeros((P, D), np.float32)
    be[:E_FF0] = a["L0_ffn_b_experts"]
    p["l0f_be"] = be
    p["l1x_wq"], p["l1x_wk"], p["l1x_wv"] = a["L1_xattn_Wq"].T, a["L1_xattn_Wk"].T, value_cols(a["L1_xattn_Wv"].T)
    p["l1x_bq"], p["l1x_bk"], p["l1x_bv"] = col(a["L1_xattn_bq"]), col(a["L1_xattn_bk"]), rows(a["L1_xattn_bv"])
    p["l1x_wo"], p["l1x_bo"] = a["L1_xattn_Wo"].T, rows(a["L1_xattn_bo"])
    p["l1f_wg"], p["l1f_bg"] = a["L1_ffn_wr"].T, rows(a["L1_ffn_rb"])
    p["l1f_shared"] = np.concatenate([a["L1_ffn_sg"].T, a["L1_ffn_su"].T, down(a["L1_ffn_sd"].T)], 1)
    p["l2x_scale"] = col(a["L2_xattn_rms_scale"])
    q2 = a["L2_xattn_q_w"].transpose(1, 0, 2).reshape(D, D)
    k2 = np.concatenate([a["L2_xattn_kv_w"][0, 0]] * 4, 1)
    p["l2x_wq"] = np.concatenate([q2, swapped(q2)], 1)
    p["l2x_wk"] = np.concatenate([k2, swapped(k2)], 1)
    p["l2x_wv"] = a["L2_xattn_kv_w"][1, 0]
    p["l2x_wo"] = a["L2_xattn_out_w"].reshape(D, D)
    p["l2f_wg"], p["l2f_bg"] = a["L2_ffn_Wr"], rows(a["L2_ffn_br"])
    p["l3x_wq"], p["l3x_wk"], p["l3x_wv"] = a["L3_xattn_Wq"], a["L3_xattn_Wk"], value_cols(a["L3_xattn_Wv"])
    p["l3x_wo"] = a["L3_xattn_Wo"].reshape(8, P, D).transpose(1, 0, 2).reshape(P, 1024)
    p["l3f_wr"], p["l3f_wk"], p["l3f_wv"] = a["L3_ffn_W_r"].T, a["L3_ffn_W_k"].T, a["L3_ffn_W_v"].T
    p["l3f_mur"], p["l3f_muk"] = col(a["L3_ffn_mu_r"]), col(a["L3_ffn_mu_k"])
    p["gates"] = rows(np.stack([a["g_xattn"], a["g_ffn"]], 1).reshape(-1))
    p["ident"] = np.eye(P, dtype=np.float32)
    p["earlier"] = rows((np.arange(8)[:, None] > np.arange(8)[None, :]).astype(np.float32).reshape(-1))
    half = ROPE_D // 2
    d = np.arange(P) % ROPE_D
    timescale = np.float32(10000.0) ** (np.float32(2.0 / ROPE_D) * (d % half).astype(np.float32))
    sign = np.where(d < half, -1.0, 1.0).astype(np.float32)[:, None]
    tabs = []
    for pos in (np.arange(S, 2 * S), np.arange(S)):
        rad = pos.astype(np.float32)[None, :] / timescale[:, None]
        tabs += [np.cos(rad), np.sin(rad) * sign]
    p["rope"] = np.concatenate(tabs, 1).astype(np.float32)
    for name, width in SMALL:
        assert p[name].shape == (P, width), (name, p[name].shape)
    w1 = [np.concatenate([a["L1_ffn_rg"][e].T, a["L1_ffn_ru"][e].T, down(a["L1_ffn_rd"][e].T)], 1)
          for e in range(E_FF1)]
    w2 = [np.concatenate([a["L2_ffn_W1"][e], down(a["L2_ffn_W2"][e])], 1) for e in range(E_FF2)]
    return (np.concatenate([p[name] for name, _ in SMALL], 1), np.concatenate([p[name] for name in LATE], 1), np.concatenate(w1, 1), np.concatenate(w2, 1))


def kernel(**inputs):
    import numpy as _np
    import concourse.bacc as _bacc
    from concourse import mybir as _mybir
    from concourse.bass_utils import run_bass_kernel_spmd as _run

    a = {k: _np.asarray(v) for k, v in inputs.items()}
    small, late, w1, w2 = _pack_small(_np, a)
    ctxT = a["ctx_1024"].reshape(B * S, D).T
    named = {
        "x": a["x"], "ctx": a["ctx_1024"], "ctxT": ctxT, "mask1": a["mask_BxS2_ff1"], "mask2": a["mask_BxS2_bk0"],
        "small": small, "late": late, "w1": w1, "w2": w2,
    }
    nc = _bacc.Bacc("TRN2", target_bir_lowering=False, num_devices=1)
    arrays, args = {}, []
    for name, v in named.items():
        v = _np.ascontiguousarray(v)
        arrays[f"in_{name}"] = v
        args.append(nc.dram_tensor(f"in_{name}", v.shape, _mybir.dt.from_np(v.dtype), kind="ExternalInput").ap())
    args.append(nc.dram_tensor("out_0", (B, S, D), _mybir.dt.from_np(_np.dtype("float32")),
                               kind="ExternalOutput").ap())
    build(nc, *args)
    r = _run(nc, [arrays], core_ids=[0])
    return r.results[0]["out_0"]
```
